# Optimizing a Trainium2 kernel written in Bass

```python
import numpy as np
import jax
import jax.numpy as jnp

def _softmax(x, axis=-1):
    return jax.nn.softmax(x, axis=axis)

def _gelu(x):
    return jax.nn.gelu(x, approximate=True)

def _silu(x):
    return jax.nn.silu(x)

def _sigmoid(x):
    return jax.nn.sigmoid(x)

def _layernorm(x, axis=-1, eps=1e-05):
    m = jnp.mean(x, axis=axis, keepdims=True)
    v = jnp.var(x, axis=axis, keepdims=True)
    return (x - m) / jnp.sqrt(v + eps)

def _scatter_add(tgt, idx, src, axis=0):
    return tgt.at[idx].add(src)

def _segment_sum(src, seg, n):
    return jax.ops.segment_sum(src, seg, n)
kernel_name = 'mk_xattn_ffn_d2_seqx_r8_34bc14'

def setup_inputs(seed: int=0):
    np.random.seed(seed)
    _w = jnp.asarray

    def _rec_inputs():
        import jax
        import jax.numpy as jnp
        _rk = jax.random.key(seed)
        x = -0.0002928 + 1 * jax.random.normal(jax.random.fold_in(_rk, 1), (1, 1024, 128), jnp.float32)
        _lenS = 1024 - jax.random.randint(jax.random.fold_in(_rk, 7), (1,), 0, max(1, 1024 // 4) + 1, jnp.int32)
        _lenS2 = 6404 - jax.random.randint(jax.random.fold_in(_rk, 8), (1,), 0, max(1, 6404 // 4) + 1, jnp.int32)
        _ctx_1024P = jax.random.normal(jax.random.fold_in(_rk, 11), (1, 16, 128), jnp.float32)
        _ctx_1024c = jax.random.dirichlet(jax.random.fold_in(_rk, 511), 0.3 * jnp.ones((16,), jnp.float32), (1, 6404))
        _ctx_1024t = jnp.einsum('bsk,bkd->bsd', _ctx_1024c, _ctx_1024P)
        _ctx_1024t = _ctx_1024t * jax.lax.rsqrt(jnp.mean(jnp.square(_ctx_1024t)) + 1e-12) * 0.953939
        ctx_1024 = -1.39393e-06 + 0.999914 * (_ctx_1024t + 0.3 * jax.random.normal(jax.random.fold_in(_rk, 611), (1, 6404, 128), jnp.float32))
        _validS = jnp.arange(1024)[None, :] < _lenS[:, None]
        _validS2 = jnp.arange(6404)[None, :] < _lenS2[:, None]
        _causal = jnp.tril(jnp.ones((1024, 1024), dtype=bool))
        mask_BxS2_ik0 = jnp.where(jnp.broadcast_to(_validS2[:, :], (1, 6404)), 0, 1).astype(jnp.int32)
        return (x, ctx_1024, mask_BxS2_ik0)
    x, ctx_1024, mask_BxS2_ik0 = _rec_inputs()

    def _L0_xattn_setup():
        import jax, jax.numpy as jnp
        import numpy as np
        B, SQ, SKV, D, H = (2, 256, 256, 128, 16)
        W = D // H

        def _heads(x):
            b, s, _ = x.shape
            return x.reshape(b, s, H, W).transpose(0, 2, 1, 3)
        key = jax.random.key(seed)
        ks = jax.random.split(key, 10)
        s = 1.0 / np.sqrt(D)
        return {'x_q': jax.random.normal(ks[0], (B, SQ, D), jnp.float32), 'x_k': jax.random.normal(ks[1], (B, SKV, D), jnp.float32), 'x_v': jax.random.normal(ks[2], (B, SKV, D), jnp.float32), 'mask': jax.random.randint(ks[3], (B, SKV), 0, 2, jnp.int32), 'Wq': jax.random.normal(ks[4], (D, D), jnp.float32) * s, 'bq': jnp.zeros((D,), jnp.float32), 'Wk': jax.random.normal(ks[5], (D, D), jnp.float32) * s, 'bk': jnp.zeros((D,), jnp.float32), 'Wv': jax.random.normal(ks[6], (D, D), jnp.float32) * s, 'bv': jnp.zeros((D,), jnp.float32)}
    _L0_xattn_all = _L0_xattn_setup()
    _L0_xattn_in = {k: v for k, v in _L0_xattn_all.items() if k in ('Wq', 'bq', 'Wk', 'bk', 'Wv', 'bv')}
    del _L0_xattn_all

    def _L0_ffn_setup():
        import jax, jax.numpy as jnp
        import numpy as np
        H = 128
        I = 128
        E = 16
        K = 4
        LIMIT = 7.0
        ALPHA = 1.702
        EPS = 1e-05
        key = jax.random.key(seed)
        ks = jax.random.split(key, 8)
        x = jax.random.normal(ks[0], (2, 64, H), dtype=jnp.float32)
        norm_scale = jnp.ones((H,), dtype=jnp.float32)
        wg = jax.random.normal(ks[1], (H, E), dtype=jnp.float32) * 0.02
        bg = jax.random.normal(ks[2], (E,), dtype=jnp.float32) * 0.02
        w1 = jax.random.normal(ks[3], (E, H, 2 * I), dtype=jnp.float32) * 0.02
        b1 = jax.random.normal(ks[4], (E, 2 * I), dtype=jnp.float32) * 0.02
        w2 = jax.random.normal(ks[5], (E, I, H), dtype=jnp.float32) * 0.02
        b2 = jax.random.normal(ks[6], (E, H), dtype=jnp.float32) * 0.02
        return {'x': x, 'norm_scale': norm_scale, 'wg': wg, 'bg': bg, 'w1': w1, 'b1': b1, 'w2': w2, 'b2': b2}
    _L0_ffn_all = _L0_ffn_setup()
    _L0_ffn_in = {k: v for k, v in _L0_ffn_all.items() if k in ('norm_scale', 'wg', 'bg', 'w1', 'b1', 'w2', 'b2')}
    del _L0_ffn_all

    def _L1_xattn_setup():
        import jax, jax.numpy as jnp
        import numpy as np
        DIM = 128
        H = 16
        D = 64
        INNER = H * D
        EPS = 1e-05

        def layernorm(x, w, b):
            mu = jnp.mean(x, axis=-1, keepdims=True)
            var = jnp.var(x, axis=-1, keepdims=True)
            return (x - mu) * jax.lax.rsqrt(var + EPS) * w + b
        key = jax.random.key(seed)
        ks = jax.random.split(key, 8)
        B, N, S = (4, 32, 1024)
        s = 1.0 / np.sqrt(DIM)
        return {'latents': jax.random.normal(ks[0], (B, N, DIM), jnp.float32), 'context': jax.random.normal(ks[1], (B, S, DIM), jnp.float32), 'ln_l_w': jnp.ones((DIM,), jnp.float32), 'ln_l_b': jnp.zeros((DIM,), jnp.float32), 'ln_c_w': jnp.ones((DIM,), jnp.float32), 'ln_c_b': jnp.zeros((DIM,), jnp.float32), 'Wq': jax.random.normal(ks[2], (DIM, INNER), jnp.float32) * s, 'Wkv': jax.random.normal(ks[3], (DIM, 2 * INNER), jnp.float32) * s, 'Wo': jax.random.normal(ks[4], (INNER, DIM), jnp.float32) * (1.0 / np.sqrt(INNER)), 'bo': jnp.zeros((DIM,), jnp.float32)}
    _L1_xattn_all = _L1_xattn_setup()
    _L1_xattn_in = {k: v for k, v in _L1_xattn_all.items() if k in ('ln_l_w', 'ln_l_b', 'ln_c_w', 'ln_c_b', 'Wq', 'Wkv', 'Wo', 'bo')}
    del _L1_xattn_all

    def _L1_ffn_setup():
        import jax, jax.numpy as jnp
        import numpy as np
        B, T, D, E, K = (4, 256, 128, 8, 2)
        key = jax.random.key(seed)
        k1, k2, k3 = jax.random.split(key, 3)
        x = jax.random.normal(k1, (B, T, D), dtype=jnp.float32)
        Wg = jax.random.normal(k2, (D, E), dtype=jnp.float32) * (1.0 / np.sqrt(D))
        lim = float(np.sqrt(6.0 / (D + D)))
        We = jax.random.uniform(k3, (E, D, D), dtype=jnp.float32, minval=-lim, maxval=lim)
        return {'x': x, 'Wg': Wg, 'We': We}
    _L1_ffn_all = _L1_ffn_setup()
    _L1_ffn_in = {k: v for k, v in _L1_ffn_all.items() if k in ('Wg', 'We')}
    del _L1_ffn_all
    return {'x': x, 'ctx_1024': ctx_1024, 'mask_BxS2_ik0': mask_BxS2_ik0, 'L0_xattn_Wq': _L0_xattn_in['Wq'], 'L0_xattn_bq': _L0_xattn_in['bq'], 'L0_xattn_Wk': _L0_xattn_in['Wk'], 'L0_xattn_bk': _L0_xattn_in['bk'], 'L0_xattn_Wv': _L0_xattn_in['Wv'], 'L0_xattn_bv': _L0_xattn_in['bv'], 'L0_ffn_norm_scale': _L0_ffn_in['norm_scale'], 'L0_ffn_wg': _L0_ffn_in['wg'], 'L0_ffn_bg': _L0_ffn_in['bg'], 'L0_ffn_w1': _L0_ffn_in['w1'], 'L0_ffn_b1': _L0_ffn_in['b1'], 'L0_ffn_w2': _L0_ffn_in['w2'], 'L0_ffn_b2': _L0_ffn_in['b2'], 'L1_xattn_ln_l_w': _L1_xattn_in['ln_l_w'], 'L1_xattn_ln_l_b': _L1_xattn_in['ln_l_b'], 'L1_xattn_ln_c_w': _L1_xattn_in['ln_c_w'], 'L1_xattn_ln_c_b': _L1_xattn_in['ln_c_b'], 'L1_xattn_Wq': _L1_xattn_in['Wq'], 'L1_xattn_Wkv': _L1_xattn_in['Wkv'], 'L1_xattn_Wo': _L1_xattn_in['Wo'], 'L1_xattn_bo': _L1_xattn_in['bo'], 'L1_ffn_Wg': _L1_ffn_in['Wg'], 'L1_ffn_We': _L1_ffn_in['We']}

def reference(x, ctx_1024, mask_BxS2_ik0, L0_xattn_Wq, L0_xattn_bq, L0_xattn_Wk, L0_xattn_bk, L0_xattn_Wv, L0_xattn_bv, L0_ffn_norm_scale, L0_ffn_wg, L0_ffn_bg, L0_ffn_w1, L0_ffn_b1, L0_ffn_w2, L0_ffn_b2, L1_xattn_ln_l_w, L1_xattn_ln_l_b, L1_xattn_ln_c_w, L1_xattn_ln_c_b, L1_xattn_Wq, L1_xattn_Wkv, L1_xattn_Wo, L1_xattn_bo, L1_ffn_Wg, L1_ffn_We):
    import jax
    import jax.numpy as jnp

    def _L0_xattn_ref(x_q, x_k, x_v, mask, Wq, bq, Wk, bk, Wv, bv):
        import jax, jax.numpy as jnp
        import numpy as np
        B, SQ, SKV, D, H = (2, 256, 256, 128, 16)
        W = D // H

        def _heads(x):
            b, s, _ = x.shape
            return x.reshape(b, s, H, W).transpose(0, 2, 1, 3)
        q = _heads(x_q @ Wq.T + bq)
        k = _heads(x_k @ Wk.T + bk)
        v = _heads(x_v @ Wv.T + bv)
        scores = jnp.einsum('bhqw,bhkw->bhqk', q, k) / np.sqrt(W).astype(np.float32)
        m = mask[:, None, None, :].astype(scores.dtype)
        scores = scores - 10000.0 * (1.0 - m)
        p = jax.nn.softmax(scores, axis=-1)
        h = jnp.einsum('bhqk,bhkw->bhqw', p, v)
        return h.transpose(0, 2, 1, 3).reshape(x_q.shape[0], x_q.shape[1], D)

    def _L0_ffn_ref(x, norm_scale, wg, bg, w1, b1, w2, b2):
        import jax, jax.numpy as jnp
        import numpy as np
        H = 128
        I = 128
        E = 16
        K = 4
        LIMIT = 7.0
        ALPHA = 1.702
        EPS = 1e-05
        shape = x.shape
        xf = x.reshape(-1, shape[-1])
        xn = xf * jax.lax.rsqrt(jnp.mean(xf * xf, axis=-1, keepdims=True) + EPS) * norm_scale
        logits = xn @ wg + bg
        vals, idx = jax.lax.top_k(logits, K)
        gates = jax.nn.softmax(vals, axis=-1)
        gate_full = jnp.einsum('tke,tk->te', jax.nn.one_hot(idx, E, dtype=gates.dtype), gates)
        h = jnp.einsum('th,ehd->etd', xn, w1) + b1[:, None, :]
        a = jnp.minimum(h[..., ::2], LIMIT)
        b = jnp.clip(h[..., 1::2], -LIMIT, LIMIT)
        s = a * jax.nn.sigmoid(ALPHA * a) * (b + 1.0)
        y = jnp.einsum('eti,eih->eth', s, w2) + b2[:, None, :]
        t = jnp.einsum('eth,te->th', y, gate_full)
        return x + t.reshape(shape)

    def _L1_xattn_ref(latents, context, ln_l_w, ln_l_b, ln_c_w, ln_c_b, Wq, Wkv, Wo, bo):
        import jax, jax.numpy as jnp
        import numpy as np
        DIM = 128
        H = 16
        D = 64
        INNER = H * D
        EPS = 1e-05

        def layernorm(x, w, b):
            mu = jnp.mean(x, axis=-1, keepdims=True)
            var = jnp.var(x, axis=-1, keepdims=True)
            return (x - mu) * jax.lax.rsqrt(var + EPS) * w + b
        b, n, _ = latents.shape
        s = context.shape[1]
        lat = layernorm(latents, ln_l_w, ln_l_b)
        ctx = layernorm(context, ln_c_w, ln_c_b)
        q = (lat @ Wq).reshape(b, n, H, D).transpose(0, 2, 1, 3)
        kv = ctx @ Wkv
        k, v = jnp.split(kv, 2, axis=-1)
        k = k.reshape(b, s, H, D).transpose(0, 2, 1, 3)
        v = v.reshape(b, s, H, D).transpose(0, 2, 1, 3)
        scale = D ** (-0.5)
        attn = jnp.einsum('bhnd,bhsd->bhns', q, k) * scale
        attn = jnp.clip(attn, -11.0, 11.0)
        attn = jax.nn.softmax(attn, axis=-1)
        out = jnp.einsum('bhns,bhsd->bhnd', attn, v)
        out = out.transpose(0, 2, 1, 3).reshape(b, n, INNER)
        return out @ Wo + bo

    def _L1_ffn_ref(x, Wg, We):
        import jax, jax.numpy as jnp
        import numpy as np
        B, T, D, E, K = (4, 256, 128, 8, 2)
        logits = jnp.einsum('btd,de->bte', x, Wg)
        gate = jax.nn.softmax(logits, axis=-1)
        top_val, top_idx = jax.lax.top_k(gate, K)
        top_w = top_val / (jnp.sum(top_val, axis=-1, keepdims=True) + 1e-09)
        x_experts = jnp.einsum('btd,edm->btem', x, We)
        x_sel = jnp.take_along_axis(x_experts, top_idx[..., None], axis=2)
        out = jnp.sum(x_sel * top_w[..., None], axis=2)
        return out
    x = x + _L0_xattn_ref(_layernorm(x, axis=-1), ctx_1024, ctx_1024, mask_BxS2_ik0, L0_xattn_Wq, L0_xattn_bq, L0_xattn_Wk, L0_xattn_bk, L0_xattn_Wv, L0_xattn_bv)
    x = x + _L0_ffn_ref(_layernorm(x, axis=-1), L0_ffn_norm_scale, L0_ffn_wg, L0_ffn_bg, L0_ffn_w1, L0_ffn_b1, L0_ffn_w2, L0_ffn_b2)
    x = x + _L1_xattn_ref(_layernorm(x, axis=-1), ctx_1024, L1_xattn_ln_l_w, L1_xattn_ln_l_b, L1_xattn_ln_c_w, L1_xattn_ln_c_b, L1_xattn_Wq, L1_xattn_Wkv, L1_xattn_Wo, L1_xattn_bo)
    x = x + _L1_ffn_ref(_layernorm(x, axis=-1), L1_ffn_Wg, L1_ffn_We)
    return x

_drawn_inputs = setup_inputs


def setup_inputs(seed=0):
    import zlib

    import numpy as np

    out = dict(_drawn_inputs(seed))
    spreads = {'L0_xattn_bq': (0.0, 0.1),
     'L0_xattn_bk': (0.0, 0.8),
     'L0_xattn_bv': (0.0, 0.1),
     'L0_ffn_norm_scale': (1.0, 0.6),
     'L1_xattn_ln_l_w': (1.0, 0.2),
     'L1_xattn_ln_l_b': (0.0, 0.356),
     'L1_xattn_ln_c_w': (1.0, 0.2),
     'L1_xattn_ln_c_b': (0.0, 0.1),
     'L1_xattn_bo': (0.0, 0.1)}
    factors = {'L0_ffn_wg': 2.998,
     'L0_ffn_bg': 8.0,
     'L0_ffn_w1': 3.585,
     'L0_ffn_b1': 8.0,
     'L0_ffn_w2': 3.147,
     'L0_ffn_b2': 3.925}
    for name, (base, spread) in spreads.items():
        noise = np.random.default_rng([zlib.crc32(name.encode()), seed]).standard_normal(out[name].shape)
        drawn = base * np.exp(spread * noise) if base else spread * noise
        out[name] = jnp.asarray(drawn.astype(out[name].dtype))
    for name, factor in factors.items():
        out[name] = (out[name] * factor).astype(out[name].dtype)
    return out
```

```python
import math
from contextlib import ExitStack

import concourse.bass as bass
from concourse import mybir

F32 = mybir.dt.float32
F16 = mybir.dt.float16
I32 = mybir.dt.int32
ALU = mybir.AluOpType
ACT = mybir.ActivationFunctionType
AX = mybir.AxisListType

P = 128
SQ = 1024
QT = SQ // P
SK = 6404
KT = -(-SK // P)
KC = -(-SK // 512)
KT4 = 4 * KC
KPAD = KT4 * P
LAST = SK - (KT - 1) * P
D = 128
H = 16
W0 = 8
QUADS = H // 4
D1 = 64
VW = D1 + 1
E0 = 16
TOP0 = 4
E1 = 8
TOP1 = 2
EPS = 1e-5
LIMIT = 7.0
ALPHA = 1.702
MASKED = -10000.0
NO_KEY = -30000.0
CLIP = 11.0

SA = 16.0
SW = 256.0
SCORE = SA * SA
MASK_ROW = 24
MAX_ROW = 25

EXP_HI = math.exp(CLIP)
EXP_LO = math.exp(-CLIP)

C_ID = 0
C_ROWSEL = C_ID + P
C_NLOW_K = C_ROWSEL + 4
C_NLOW_Q = C_NLOW_K + 1
C_ADD_K = C_NLOW_Q + 1
C_ADD_Q = C_ADD_K + 1
C_MASKROW = C_ADD_Q + 1
C_TRI = C_MASKROW
C_LN = C_TRI + E0 * E0
C_N = C_LN + 4
EW = 3 * P + 2
ARENA = 39424
W1_AT = 18560
STEPS = KT // 2 + 1




def build(nc, x, ctx, ctx_t, mask, consts, mask_sel, w0, b0, bv0, norm_scale, wg0, bg0, ew0, b2,
          ln1, w1, wo, bo, wg1, we1, out):
    with ExitStack() as stack:
        def sb(name, shape, dt):
            return stack.enter_context(nc.sbuf_tensor(name, shape, dt))

        def psum(name, shape, dt):
            return stack.enter_context(nc.psum_tensor(name, shape, dt))

        def sem(name):
            return stack.enter_context(nc.semaphore(name))

        cst = sb("cst", [P, C_N], F32)
        cn_hi = sb("cn_hi", [P, KPAD], F16)
        cn_lo = sb("cn_lo", [P, KPAD], F16)
        probs = sb("probs", [P, 2, SQ], F32)
        xres = sb("xres", [P, QT, D], F32)
        xhat = sb("xhat", [P, QT, D], F32)
        small = sb("small", [P, 1792], F32)
        arena = sb("arena", [P, ARENA], F32)

        class Region:

            def __init__(self, of, at=0):
                self.of, self.at = of, at

            def take(self, n, dt=F32):
                words = n if dt in (F32, I32) else -(-n // 2)
                v = self.of[:, self.at:self.at + words]
                self.at += words
                return v if dt == F32 else v.bitcast(dt)

        r = Region(arena)
        cT_hi = r.take(KPAD, F16)
        cT_lo = r.take(KPAD, F16)
        v0_at = r.at
        v0 = r.take(KT4 * H * (W0 + 1)).rearrange("p (t h w) -> p t h w", h=H, w=W0 + 1)
        w0_hi = r.take(2 * 512 + D, F16)
        w0_lo = r.take(2 * 512 + D, F16)
        xT_hi = r.take(SQ, F16)
        xT_lo = r.take(SQ, F16)
        msel = r.take(KC * P, F16)[0:KC, :]
        mask_rows = r.take(512, F16)[0:KC, :]
        qz_at = r.at
        qz = r.take(H * SQ, F16).rearrange("p (h n) -> p h n", h=H)
        ks_at = r.at
        ks = r.take(QUADS * KPAD, F16).rearrange("p (g n) -> p g n", g=QUADS)
        assert r.at <= ARENA
        r = Region(arena, ks_at)
        c_raw = r.take(KT4 * D).rearrange("p (t d) -> p t d", d=D)
        cT = r.take(KPAD)
        r = Region(arena, qz_at)
        xb = r.take(2 * 512).rearrange("p (b n) -> p b n", b=2)
        yf = r.take(2 * 512).rearrange("p (b n) -> p b n", b=2)
        cbn = r.take(KT4 * 6).rearrange("p (t s) -> p t s", s=6)
        r = Region(arena, v0_at)
        mask_i = r.take(512, I32)[0:KC, :]
        msel_f = r.take(KC * P)[0:KC, :]
        w0f = probs[:, :, :].rearrange("p b n -> p (b n)")[:, 0:2 * 512 + D]
        kf = probs[:, :, :].rearrange("p b (c n) -> p (b c) n", n=512)
        qtmp = xhat[:, 0:4, :].rearrange("p t d -> p (t d)").bitcast(F16)
        mp = probs[:, :, :].rearrange("p b n -> p (b n)")[:, 0:KC * H * QT].rearrange(
            "p (c h q) -> p c h q", h=H, q=QT)
        maxsel = xhat[:, :, :].rearrange("p (b t) d -> p b t d", b=2)
        h0 = xhat
        r = Region(arena)
        fT = r.take(SQ)
        ewb = r.take(2 * EW).rearrange("p (b n) -> p b n", b=2)
        fab = r.take(4 * SQ)
        fa, fb, fsig, fs = (fab[:, i * SQ:(i + 1) * SQ] for i in range(4))
        xn = r.take(QT * D).rearrange("p (t d) -> p t d", d=D)
        gT = r.take(SQ)[0:E0, :]
        b2s = r.take(D)[0:E0, :]
        nscale = r.take(D)
        wg0s = r.take(E0)
        bg0s = r.take(E0)
        bos = r.take(D)
        assert r.at <= W1_AT
        r = Region(arena, W1_AT)
        w1_hi = r.take(2 * H * P + H * D1, F16)
        w1_lo = r.take(2 * H * P + H * D1, F16)
        w1f_at = r.at
        w1f = r.take(2 * H * P + H * D1)
        r = Region(arena, w1f_at)
        wos = r.take(8 * D).rearrange("p (c n) -> p c n", c=8)
        we1s = r.take(E1 * D)
        xT1 = r.take(SQ)
        bo1 = r.take(D)
        wg1s = r.take(E1)
        r = Region(arena, w1f_at + 2 * H * P + H * D1)
        lat_hi = r.take(SQ, F16)
        lat_lo = r.take(SQ, F16)
        q1_hi = r.take(2 * SQ, F16).rearrange("p (b n) -> p b n", b=2)
        q1_lo = r.take(2 * SQ, F16).rearrange("p (b n) -> p b n", b=2)
        v1b = r.take(KT * VW).rearrange("p (t w) -> p t w", w=VW)
        assert r.at <= ARENA, r.at
        r = Region(arena)
        k1 = r.take(2 * KT * P, F16).rearrange("p (b n) -> p b n", b=2)
        v1a = r.take(KT * VW).rearrange("p (t w) -> p t w", w=VW)
        o1 = r.take(QT * H * D1).rearrange("p (t n) -> p t n", t=QT)
        assert r.at <= W1_AT, r.at
        v1 = [v1a, v1b]
        oT = arena[:, 0:8 * SQ].rearrange("p (c n) -> p c n", c=8)
        wk1_hi, wk1_lo = (w[:, 0:H * P].rearrange("p (h n) -> p h n", h=H) for w in (w1_hi, w1_lo))
        wq1_hi, wq1_lo = (w[:, H * P:2 * H * P].rearrange("p (h n) -> p h n", h=H) for w in (w1_hi, w1_lo))
        wv1_hi, wv1_lo = (w[:, 2 * H * P:].rearrange("p (h n) -> p h n", h=H) for w in (w1_hi, w1_lo))

        r = Region(small)
        b0s = r.take(2 * QUADS)
        qkcol = r.take(2 * QUADS)
        bst = r.take(QT * 6).rearrange("p (t s) -> p t s", s=6)
        xmean = r.take(QT)
        xvar = r.take(QT)
        xstd = r.take(QT)
        xrstd = r.take(QT)
        stat = r.take(KT4)
        cmean = r.take(KT4)
        cvar = r.take(KT4)
        cstd = r.take(KT4)
        crstd = r.take(KT4)
        mx = r.take(H * QT)
        rec = r.take(QT)
        gate = r.take(QT * E0).rearrange("p (t e) -> p t e", e=E0)
        lg = r.take(QT * E0).rearrange("p (t e) -> p t e", e=E0)
        rank = r.take(QT * E0).rearrange("p (t e) -> p t e", e=E0)
        gmax = r.take(QT)
        gsum = r.take(QT)
        grec = r.take(QT)
        bvs = r.take(D)
        ln1s = r.take(4)
        ln1c = r.take(4)
        gate1 = r.take(QT * E1).rearrange("p (t e) -> p t e", e=E1)
        lg1 = r.take(QT * E1).rearrange("p (t e) -> p t e", e=E1)
        rank1 = r.take(QT * E1).rearrange("p (t e) -> p t e", e=E1)
        assert r.at <= 1792, r.at

        ident = cst[:, C_ID:C_ID + P]

        def rowsel(j):
            return cst[:, C_ROWSEL + j:C_ROWSEL + j + 1]

        S = psum("S", [P, 2, SQ], F32)
        A = psum("A", [P, 4, 512], F32)
        S4 = S[:, :, :].rearrange("p b (c n) -> p (b c) n", n=512)
        T4 = A[:, :, :]

        ld_cst = sem("ld_cst")
        ld_x = sem("ld_x")
        ld_ctx = sem("ld_ctx")
        ld_ctx_t = sem("ld_ctx_t")
        ld_mask = sem("ld_mask")
        ld_w0 = sem("ld_w0")
        ld_b0 = sem("ld_b0")
        ld_ffn0 = sem("ld_ffn0")
        ld_ew = [sem("ld_ew0"), sem("ld_ew1")]
        ld_w1 = sem("ld_w1")
        ld_end = sem("ld_end")
        stored = sem("stored")
        raw_zeroed = sem("raw_zeroed")
        dve_step = sem("dve_step")
        pool_step = sem("pool_step")
        w0_split = sem("w0_split")
        var_ready = sem("var_ready")
        std_ready = sem("std_ready")
        hat_ready = sem("hat_ready")
        hatT_ready = sem("hatT_ready")
        hatT_copied = sem("hatT_copied")
        latf_ready = sem("latf_ready")
        cT_hi_ready = sem("cT_hi_ready")
        xb_ready = sem("xb_ready")
        tr_done = sem("tr_done")
        yf_ready = sem("yf_ready")
        cn_hi_ready = sem("cn_hi_ready")
        cn_done = sem("cn_done")
        k0_psum = sem("k0_psum")
        k0_f = sem("k0_f")
        k0_hi = sem("k0_hi")
        k0_done = sem("k0_done")
        v0_psum = sem("v0_psum")
        v0_done = sem("v0_done")
        v0_ones = sem("v0_ones")
        q0_psum = sem("q0_psum")
        q0_f = sem("q0_f")
        q0_done = sem("q0_done")
        mx_psum = sem("mx_psum")
        mx_read = sem("mx_read")
        maxsel_ready = sem("maxsel_ready")
        maxT_ready = sem("maxT_ready")
        maxT_read = sem("maxT_read")
        scores_ready = [sem("scores_ready0"), sem("scores_ready1")]
        exp_done = [sem("exp_done0"), sem("exp_done1")]
        clipped = sem("clipped")
        pv_done = [sem("pv_done0"), sem("pv_done1")]
        acc_zero = [sem("acc_zero0"), sem("acc_zero1")]
        acc_read = [sem("acc_read0"), sem("acc_read1")]
        w1_split = sem("w1_split")
        v1_const = sem("v1_const")
        q1_psum = sem("q1_psum")
        q1_hi_done = sem("q1_hi_done")
        q1_done = sem("q1_done")
        k1_psum = sem("k1_psum")
        k1_hi_done = sem("k1_hi_done")
        k1_done = sem("k1_done")
        v1_psum = sem("v1_psum")
        v1_done = sem("v1_done")
        logits_ready = sem("logits_ready")
        gmax_done = sem("gmax_done")
        gexp_done = sem("gexp_done")
        gates_ready = sem("gates_ready")
        gateT_ready = sem("gateT_ready")
        gateT_copied = sem("gateT_copied")
        b2_ready = sem("b2_ready")
        ffn_base = sem("ffn_base")
        h_ready = sem("h_ready")
        a_ready = sem("a_ready")
        h_read = sem("h_read")
        sig_ready = sem("sig_ready")
        glu_done = sem("glu_done")
        s_ready = sem("s_ready")
        y_ready = sem("y_ready")
        y_added = sem("y_added")
        x2_ready = sem("x2_ready")
        oT_ready = sem("oT_ready")
        oT_copied = sem("oT_copied")
        proj_ready = sem("proj_ready")
        ex1_ready = sem("ex1_ready")
        ex1_added = sem("ex1_added")
        out_ready = sem("out_ready")
        attn0_done = sem("attn0_done")

        PIECE = KPAD // 4
        block = stack.enter_context(nc.Block())

        @block.sync
        def _(sp):
            sp.dma_start(cst[:, :], consts).then_inc(ld_cst, 16)
            sp.dma_start(xres[:, :, :], x.rearrange("(t p) d -> p t d", p=P)).then_inc(ld_x, 16)
            full = (KT - 1) * P
            sp.dma_start(c_raw[:, 0:KT - 1, :], ctx[0:full, :].rearrange("(t p) d -> p t d", p=P)).then_inc(ld_ctx, 16)
            sp.wait_ge(raw_zeroed, 1)
            sp.dma_start(c_raw[0:LAST, KT - 1, :], ctx[full:SK, :]).then_inc(ld_ctx, 16)
            sp.wait_ge(attn0_done, 1)
            for dst, src in ((b2s, b2), (nscale, norm_scale), (wg0s, wg0), (bg0s, bg0)):
                sp.dma_start(dst, src).then_inc(ld_ffn0, 16)
            sp.dma_start(w1f, w1).then_inc(ld_w1, 16)
            sp.dma_start(ln1s, ln1).then_inc(ld_w1, 16)
            for b in range(2):
                sp.dma_start(ewb[:, b, :], ew0[b, :, :]).then_inc(ld_ew[b], 16)
            with sp.Fori(0, E0 // 2 - 1) as i:
                for b in range(2):
                    sp.wait_ge(y_ready, 2 * i + b + 1)
                    sp.dma_start(ewb[:, b, :], ew0[2 * i + 2 + b, :, :]).then_inc(ld_ew[b], 16)
            sp.wait_ge(w1_split, 1)
            for dst, src in ((wos, wo), (we1s, we1), (bo1, bo), (wg1s, wg1)):
                sp.dma_start(dst, src).then_inc(ld_end, 16)
            sp.wait_ge(out_ready, 1)
            sp.dma_start(out.rearrange("(t p) d -> p t d", p=P), xres[:, :, :]).then_inc(stored, 16)
            sp.wait_ge(stored, 16)

        @block.gpsimd
        def _(pool):
            steps = [0]

            def step(ins):
                steps[0] += 1
                ins.then_inc(pool_step, 1)
                pool.wait_ge(pool_step, steps[0])

            nc.gpsimd.memset(c_raw[:, KT - 1:KT4, :], 0.0).then_inc(raw_zeroed, 1)
            pool.wait_ge(w0_split, 2)
            nc.gpsimd.memset(v0[:, :, :, W0:W0 + 1], 1.0).then_inc(v0_ones, 1)
            pool.wait_ge(ld_w1, 32)
            step(nc.gpsimd.tensor_scalar(w1f, w1f, SW, None, ALU.mult))
            step(nc.gpsimd.tensor_copy(w1_hi, w1f))
            nc.gpsimd.tensor_tensor(w1_lo, w1f, w1_hi, ALU.subtract).then_inc(w1_split, 1)

        def act_sqrt(act, n, std, var):
            act.wait_ge(var_ready, n)
            nc.scalar.activation(std, var, ACT.Sqrt).then_inc(std_ready, 1)

        @block.scalar
        def _(act):
            for dst, src, s in ((w0f, w0, ld_w0), (b0s, b0, ld_b0), (bvs, bv0, ld_b0),
                                (mask_i, mask, ld_mask), (msel_f, mask_sel, ld_mask), (cT, ctx_t, ld_ctx_t)):
                act.dma_start(dst, src).then_inc(s, 16)
            act_sqrt(act, 1, xstd, xvar)
            act.wait_ge(hatT_ready, 1)
            nc.scalar.activation(xT_hi, S[:, 0, :], ACT.Copy, scale=SA).then_inc(hatT_copied, 1)
            act.wait_ge(ld_ctx_t, 16)
            for i in range(4):
                nc.scalar.activation(cT_hi[:, i * PIECE:(i + 1) * PIECE], cT[:, i * PIECE:(i + 1) * PIECE],
                                     ACT.Copy, scale=SA).then_inc(cT_hi_ready, 1)
            act_sqrt(act, 2, cstd, cvar)
            act.sem_inc(yf_ready, 2)

            def scaled(c, b):
                act.wait_ge(tr_done, c + 3)
                act.wait_ge(cn_done, c + 1)
                nc.scalar.activation(yf[:, b, :], S4[:, b, :], ACT.Identity, bias=ln1c[:, 3:4],
                                     scale=ln1c[:, 2:3]).then_inc(yf_ready, 1)

            with act.Fori(0, KC // 2) as i:
                for b in range(2):
                    scaled(2 * i + b, b)
            scaled(KC - 1, 0)
            act.sem_inc(k0_f, 4)
            act.sem_inc(v0_done, 4)
            with act.Fori(0, KC) as c:
                for g in range(QUADS):
                    act.wait_ge(k0_psum, 4 * c + g + 1)
                    act.wait_ge(k0_done, 4 * c + g + 1)
                    nc.scalar.activation(kf[:, g, :], S4[:, g, :], ACT.Identity, bias=qkcol[:, QUADS + g:QUADS + g + 1],
                                         scale=1.0 / SW).then_inc(k0_f, 1)
                for u in range(4):
                    act.wait_ge(v0_psum, 4 * c + u + 1)
                    nc.scalar.activation(v0[:, 4 * c + u, :, 0:W0],
                                         T4[:, u, 0:D].rearrange("p (h w) -> p h w", w=W0),
                                         ACT.Copy, scale=1.0 / (SA * SW)).then_inc(v0_done, 1)
            for g in range(QUADS):
                act.wait_ge(q0_psum, g + 1)
                if g >= 2:
                    act.wait_ge(q0_done, g - 1)
                else:
                    act.wait_ge(k0_done, 4 * KC + 4)
                nc.scalar.activation(probs[:, g % 2, :], S[:, g % 2, :], ACT.Identity, bias=qkcol[:, g:g + 1],
                                     scale=SA / (SA * SW * math.sqrt(W0))).then_inc(q0_f, 1)
            nc.scalar.preload_act_table(ACT.Exp)
            act.sem_inc(exp_done[0], 2)

            def exp0(g, b):
                act.wait_ge(scores_ready[0], g + 1)
                act.wait_ge(pv_done[0], g + 1)
                nc.scalar.activation(probs[:, b, :], S[:, b, :], ACT.Exp, scale=1.0 / SCORE).then_inc(exp_done[0], 1)

            act.wait_ge(mx_read, 4 * KC * H)
            act.wait_ge(maxT_read, 8)
            with act.Fori(0, QUADS) as quad:
                for j in range(4):
                    g0 = (quad * 4 + j) * KT
                    with act.Fori(0, KT // 2) as i:
                        for b in range(2):
                            exp0(g0 + 2 * i + b, (j * KT + b) % 2)
                    exp0(g0 + KT - 1, (j * KT + KT - 1) % 2)
            act_sqrt(act, 3, xstd, xvar)
            act_sqrt(act, 4, xstd, xvar)
            act.wait_ge(hatT_ready, 2)
            nc.scalar.copy(fT, S[:, 0, :]).then_inc(hatT_copied, 1)
            act.wait_ge(gmax_done, 1)
            nc.scalar.activation(gate[:, :, :], lg[:, :, :], ACT.Exp).then_inc(gexp_done, 1)
            act.wait_ge(gateT_ready, 1)
            nc.scalar.copy(gT, S[0:E0, 0, :]).then_inc(gateT_copied, 1)
            nc.scalar.preload_act_table(ACT.Sigmoid)
            act.sem_inc(sig_ready, 1)
            with act.Fori(0, E0) as e:
                act.wait_ge(a_ready, e + 1)
                act.wait_ge(s_ready, e + 1)
                nc.scalar.activation(fsig, fa, ACT.Sigmoid, scale=ALPHA).then_inc(sig_ready, 1)
            act_sqrt(act, 5, xstd, xvar)
            act_sqrt(act, 6, xstd, xvar)
            act.wait_ge(hatT_ready, 3)
            nc.scalar.activation(probs[:, 0, :], S[:, 0, :], ACT.Identity, bias=ln1c[:, 1:2],
                                 scale=ln1c[:, 0:1]).then_inc(latf_ready, 1)
            nc.scalar.preload_act_table(ACT.Exp)

            def q1_part(n, half, b):
                act.wait_ge(q1_psum, n + 1)
                nc.scalar.activation(q1_hi[:, b, half * 512:half * 512 + 512], T4[:, 2, :], ACT.Copy,
                                     scale=1.0 / SW).then_inc(q1_hi_done, 1)

            def k1_part(n, at, width, b):
                act.wait_ge(k1_psum, n + 1)
                nc.scalar.activation(k1[:, b, bass.ds(at, width)], T4[:, 2, 0:width], ACT.Copy,
                                     scale=1.0 / SW).then_inc(k1_hi_done, 1)

            def v1_part(n, t, b):
                act.wait_ge(v1_psum, n + 1)
                if t is None:
                    nc.scalar.activation(v1[b][0:LAST, KT - 1, 0:D1], T4[0:LAST, 3, 0:D1], ACT.Copy,
                                         scale=1.0 / (SA * SW)).then_inc(v1_done, 1)
                else:
                    nc.scalar.activation(v1[b][:, bass.ds(t, 2), 0:D1],
                                         T4[:, 3, 0:2 * D1].rearrange("p (t w) -> p t w", w=D1), ACT.Copy,
                                         scale=1.0 / (SA * SW)).then_inc(v1_done, 1)

            def proj1(h, b, tile=None):
                for half in range(2):
                    q1_part(2 * h + half, half, b)
                with act.Fori(0, KT // 2) as i:
                    k1_part(h * STEPS + i, 256 * i, 256, b)
                    v1_part(h * STEPS + i, 2 * i, b)
                    if tile:
                        for u in range(2):
                            tile(2 * i + u, u)
                k1_part(h * STEPS + STEPS - 1, (KT - 1) * P, P, b)
                v1_part(h * STEPS + STEPS - 1, None, b)
                if tile:
                    tile(KT - 1, KT - 1)

            act.sem_inc(exp_done[1], 2)

            def exp1(g, b):
                act.wait_ge(scores_ready[1], g + 1)
                act.wait_ge(pv_done[1], g + 1)
                nc.scalar.activation(probs[:, b, :], S[:, b, :], ACT.Exp,
                                     scale=1.0 / (SCORE * math.sqrt(D1))).then_inc(exp_done[1], 1)

            act.wait_ge(v1_const, 1)
            act.sem_inc(v1_done, 1)
            proj1(0, 0)
            with act.Fori(0, H // 2 - 1) as pair:
                for a in range(2):
                    h = 2 * pair + a
                    proj1(h + 1, (a + 1) % 2, lambda t, u: exp1(h * KT + t, (a * KT + u) % 2))
            proj1(H - 1, 1, lambda t, u: exp1((H - 2) * KT + t, u % 2))
            with act.Fori(0, KT // 2) as i:
                for u in range(2):
                    exp1((H - 1) * KT + 2 * i + u, (KT + u) % 2)
            exp1(H * KT - 1, (2 * KT - 1) % 2)
            for c in range(8):
                act.wait_ge(oT_ready, c + 1)
                nc.scalar.copy(oT[:, c, :], S[:, c % 2, :]).then_inc(oT_copied, 1)
            act_sqrt(act, 7, xstd, xvar)
            act.wait_ge(hatT_ready, 4)
            nc.scalar.copy(xT1, S[:, 0, :]).then_inc(hatT_copied, 1)
            act.wait_ge(gmax_done, 2)
            nc.scalar.activation(gate1[:, :, :], lg1[:, :, :], ACT.Exp).then_inc(gexp_done, 1)

        @block.tensor
        def _(pe):
            def transposes(n, src, dst):
                pe.wait_ge(hat_ready, n)
                for t in range(QT):
                    last = nc.tensor.transpose(dst[:, t * P:(t + 1) * P], src[:, t, :], ident)
                last.then_inc(hatT_ready, 1)

            def split_product(o, l_hi, l_lo, r_hi, r_lo, **kw):
                nc.tensor.matmul(o, l_hi, r_hi, start=True, stop=False, **kw)
                nc.tensor.matmul(o, l_lo, r_hi, start=False, stop=False, **kw)
                return nc.tensor.matmul(o, l_hi, r_lo, start=False, stop=True, **kw)

            pe.wait_ge(ld_cst, 16)
            transposes(1, xhat, S[:, 0, :])
            pe.wait_ge(hatT_copied, 2)
            pe.sem_inc(tr_done, 2)

            def ctx_transposes(c, b):
                pe.wait_ge(xb_ready, c + 1)
                pe.wait_ge(yf_ready, c + 1)
                for u in range(4):
                    last = nc.tensor.transpose(S4[:, b, u * P:(u + 1) * P], xb[:, b, u * P:(u + 1) * P], ident)
                last.then_inc(tr_done, 1)

            with pe.Fori(0, KC // 2) as i:
                for b in range(2):
                    ctx_transposes(2 * i + b, b)
            ctx_transposes(KC - 1, 0)

            pe.wait_ge(w0_split, 2)
            pe.wait_ge(cT_hi_ready, 5)
            pe.wait_ge(yf_ready, KC + 2)
            with pe.Fori(0, KC) as c:
                for g in range(QUADS):
                    pe.wait_ge(k0_f, 4 * c + g + 1)
                    chunk = bass.ds(512 * c, 512)
                    w = slice(512 + g * P, 512 + (g + 1) * P)
                    nc.tensor.matmul(S4[:, g, :], w0_hi[:, w], cT_hi[:, chunk], start=True, stop=False)
                    nc.tensor.matmul(S4[:, g, :], w0_lo[:, w], cT_hi[:, chunk], start=False, stop=False)
                    nc.tensor.matmul(S4[:, g, :], w0_hi[:, w], cT_lo[:, chunk], start=False, stop=False)
                    nc.tensor.matmul(S4[:, g, :], msel[:, bass.ds(P * c, P)], mask_rows, start=False,
                                     stop=True).then_inc(k0_psum, 1)
                for u in range(4):
                    pe.wait_ge(v0_done, 4 * c + u + 1)
                    tile = bass.ds(512 * c + u * P, P)
                    nc.tensor.matmul(T4[:, u, 0:D], cT_hi[:, tile], w0_hi[:, 1024:1024 + D], start=True, stop=False)
                    nc.tensor.matmul(T4[:, u, 0:D], cT_hi[:, tile], w0_lo[:, 1024:1024 + D], start=False, stop=False)
                    nc.tensor.matmul(T4[:, u, 0:D], cT_lo[:, tile], w0_hi[:, 1024:1024 + D], start=False,
                                     stop=True).then_inc(v0_psum, 1)
            pe.wait_ge(k0_f, 4 * KC + 4)
            for g in range(QUADS):
                if g >= 2:
                    pe.wait_ge(q0_f, g - 1)
                w = slice(g * P, (g + 1) * P)
                for half in range(2):
                    n = slice(half * 512, half * 512 + 512)
                    last = split_product(S[:, g % 2, n], w0_hi[:, w], w0_lo[:, w], xT_hi[:, n], xT_lo[:, n])
                last.then_inc(q0_psum, 1)
            pe.wait_ge(q0_f, QUADS)
            pe.wait_ge(q0_done, QUADS)
            pe.wait_ge(k0_done, 4 * KC + 4)
            with pe.Fori(0, H) as h:
                with pe.Fori(0, KC) as c:
                    for k in range(4):
                        pe.wait_ge(mx_read, (h * KC + c) * 4 + k + 1)
                        for m in range(2):
                            last = nc.tensor.matmul(S[:, k % 2, m * 512:m * 512 + 512],
                                                    qz[:, h, (2 * k + m) * P:(2 * k + m + 1) * P],
                                                    ks[:, h // 4, bass.ds(512 * c, 512)], start=True, stop=True)
                        last.then_inc(mx_psum, 1)
            for n in range(8):
                pe.wait_ge(maxsel_ready, n + 1)
                if n >= 4:
                    pe.wait_ge(maxT_read, n - 3)
                for u in range(4):
                    last = nc.tensor.transpose(S4[:, n % 4, u * P:(u + 1) * P], maxsel[:, n % 2, u, :], ident)
                last.then_inc(maxT_ready, 1)

            def scores0(g, b, quad, h, t):
                pe.wait_ge(exp_done[0], g + 1)
                for half in range(2):
                    last = nc.tensor.matmul(S[:, b, half * 512:half * 512 + 512], ks[:, quad, bass.ds(P * t, P)],
                                            qz[:, h, half * 512:half * 512 + 512], start=True, stop=True)
                last.then_inc(scores_ready[0], 1)

            def pv0(g, b, h, t, a, first=False):
                pe.wait_ge(exp_done[0], g + 3)
                for q in range(QT):
                    last = nc.tensor.matmul(T4[:, a, q * (W0 + 1):(q + 1) * (W0 + 1)],
                                            probs[:, b, q * P:(q + 1) * P], v0[:, t, h, :],
                                            start=False, stop=False, skip_group_check=True)
                last.then_inc(pv_done[0], 1)

            pe.sem_inc(pv_done[0], 2)
            pe.wait_ge(maxT_read, 8)
            pe.wait_ge(v0_done, 4 * KC + 4)
            pe.wait_ge(v0_ones, 1)
            pe.wait_ge(acc_zero[0], 1)
            scores0(0, 0, 0, 0, 0)

            def quad0(quad, last_quad):
                for j in range(4):
                    h = quad * 4 + j
                    g0 = h * KT
                    with pe.Fori(0, KT // 2) as i:
                        for u in range(2):
                            t = 2 * i + u
                            scores0(g0 + t + 1, (j * KT + u + 1) % 2, quad, h, t + 1)
                            pv0(g0 + t, (j * KT + u) % 2, h, t, j % 2)
                    pe.wait_ge(acc_zero[0], h + 2)
                    if j < 3:
                        scores0(g0 + KT, (j * KT + KT) % 2, quad, h + 1, 0)
                    elif not last_quad:
                        scores0(g0 + KT, (j * KT + KT) % 2, quad + 1, h + 1, 0)
                    pv0(g0 + KT - 1, (j * KT + KT - 1) % 2, h, KT - 1, j % 2)

            with pe.Fori(0, QUADS - 1) as quad:
                quad0(quad, False)
            quad0(QUADS - 1, True)
            transposes(2, xn, S[:, 0, :])
            pe.wait_ge(ld_ffn0, 64)
            pe.wait_ge(hatT_copied, 3)
            for t in range(QT):
                last = nc.tensor.matmul(T4[:, 2, t * E0:(t + 1) * E0], fT[:, t * P:(t + 1) * P], wg0s,
                                        start=True, stop=True)
            last.then_inc(logits_ready, 1)
            pe.wait_ge(gates_ready, 1)
            for t in range(QT):
                last = nc.tensor.transpose(S[0:E0, 0, t * P:(t + 1) * P], gate[:, t, :], ident)
            last.then_inc(gateT_ready, 1)
            pe.wait_ge(gateT_copied, 1)
            for t in range(QT):
                last = nc.tensor.matmul(T4[:, t // 4, (t % 4) * P:(t % 4 + 1) * P], gT[:, t * P:(t + 1) * P], b2s,
                                        start=True, stop=True)
            last.then_inc(b2_ready, 1)

            def expert_h(e, b, i):
                pe.wait_ge(ld_ew[b], 16 * i + 16)
                pe.wait_ge(h_read, e + 1)
                for ab in range(2):
                    for half in range(2):
                        n = slice(half * 512, half * 512 + 512)
                        last = nc.tensor.matmul(S[:, ab, n], ewb[:, b, ab * P:(ab + 1) * P], fT[:, n],
                                                start=True, stop=True)
                last.then_inc(h_ready, 1)

            def expert_y(e, b):
                pe.wait_ge(s_ready, e + 2)
                pe.wait_ge(y_added, e + 1)
                for t in range(QT):
                    last = nc.tensor.matmul(T4[:, t // 4, (t % 4) * P:(t % 4 + 1) * P], fs[:, t * P:(t + 1) * P],
                                            ewb[:, b, 2 * P:3 * P], start=True, stop=True)
                last.then_inc(y_ready, 1)

            expert_h(0, 0, 0)
            with pe.Fori(0, E0 // 2 - 1) as i:
                expert_h(2 * i + 1, 1, i)
                expert_y(2 * i, 0)
                expert_h(2 * i + 2, 0, i + 1)
                expert_y(2 * i + 1, 1)
            expert_h(E0 - 1, 1, E0 // 2 - 1)
            expert_y(E0 - 2, 0)
            expert_y(E0 - 1, 1)
            transposes(3, xn, S[:, 0, :])
            pe.wait_ge(w1_split, 1)
            pe.wait_ge(hatT_copied, 5)
            pe.wait_ge(v1_const, 1)

            def q1_proj(h, half):
                pe.wait_ge(k1_done, h * STEPS + 1)
                pe.wait_ge(q1_done, 2 * h + half + 1)
                n = slice(half * 512, half * 512 + 512)
                split_product(T4[:, 2, :], wq1_hi[:, h, :], wq1_lo[:, h, :], lat_hi[:, n], lat_lo[:, n])\
                    .then_inc(q1_psum, 1)

            def k1_proj(h, n, at, width):
                pe.wait_ge(q1_done, 2 * h + 3)
                pe.wait_ge(k1_done, n + 1)
                c = bass.ds(at, width)
                split_product(T4[:, 2, 0:width], wk1_hi[:, h, :], wk1_lo[:, h, :], cn_hi[:, c], cn_lo[:, c])\
                    .then_inc(k1_psum, 1)

            def v1_proj(h, n, at, tiles):
                pe.wait_ge(v1_done, n + 1)
                for u in range(tiles):
                    t = bass.ds(at + u * P, P)
                    o = T4[:, 3, u * D1:(u + 1) * D1]
                    nc.tensor.matmul(o, cn_hi[:, t], wv1_hi[:, h, :], start=(u == 0), stop=False, skip_group_check=True)
                    nc.tensor.matmul(o, cn_hi[:, t], wv1_lo[:, h, :], start=False, stop=False, skip_group_check=True)
                    last = nc.tensor.matmul(o, cn_lo[:, t], wv1_hi[:, h, :], start=False, stop=True,
                                            skip_group_check=True)
                last.then_inc(v1_psum, 1)

            def proj1(h, tile=None, end=None):
                for half in range(2):
                    q1_proj(h, half)
                with pe.Fori(0, KT // 2) as i:
                    k1_proj(h, h * STEPS + i, 256 * i, 256)
                    v1_proj(h, h * STEPS + i, 256 * i, 2)
                    if tile:
                        for u in range(2):
                            tile(2 * i + u, u)
                k1_proj(h, h * STEPS + STEPS - 1, (KT - 1) * P, P)
                v1_proj(h, h * STEPS + STEPS - 1, (KT - 1) * P, 1)
                if end:
                    end()

            def scores1(g, b, hb, t):
                pe.wait_ge(exp_done[1], g + 1)
                for half in range(2):
                    n = slice(half * 512, half * 512 + 512)
                    nc.tensor.matmul(S[:, b, n], k1[:, hb, bass.ds(P * t, P)], q1_hi[:, hb, n], start=True, stop=False)
                    last = nc.tensor.matmul(S[:, b, n], k1[:, hb, bass.ds(P * t, P)], q1_lo[:, hb, n],
                                            start=False, stop=True)
                last.then_inc(scores_ready[1], 1)

            def pv1(g, b, hb, t):
                pe.wait_ge(clipped, g + 1)
                for q in range(QT):
                    last = nc.tensor.matmul(T4[:, q // 7, (q % 7) * VW:(q % 7 + 1) * VW],
                                            probs[:, b, q * P:(q + 1) * P], v1[hb][:, t, :],
                                            start=False, stop=False, skip_group_check=True)
                last.then_inc(pv_done[1], 1)

            def first_tile(h, hb, b):
                pe.wait_ge(q1_done, 2 * h + 3)
                pe.wait_ge(k1_done, h * STEPS + STEPS + 1)
                pe.wait_ge(v1_done, h * STEPS + STEPS + 1)
                scores1(h * KT, b, hb, 0)

            pe.sem_inc(pv_done[1], 2)
            proj1(0)
            first_tile(0, 0, 0)

            def head1(h, hb, last_head=False):
                par = hb * KT

                def tile(t, u):
                    scores1(h * KT + t + 1, (par + u + 1) % 2, hb, t + 1)
                    pv1(h * KT + t, (par + u) % 2, hb, t)

                pe.wait_ge(acc_zero[1], h + 1)
                if last_head:
                    with pe.Fori(0, KT // 2) as i:
                        for u in range(2):
                            tile(2 * i + u, u)
                else:
                    proj1(h + 1, tile)
                    first_tile(h + 1, 1 - hb, (par + KT) % 2)
                pv1(h * KT + KT - 1, (par + KT - 1) % 2, hb, KT - 1)

            with pe.Fori(0, H // 2 - 1) as pair:
                for a in range(2):
                    head1(2 * pair + a, a)
            head1(H - 2, 0)
            head1(H - 1, 1, True)
            pe.wait_ge(acc_zero[1], H + 1)
            for c in range(8):
                if c >= 2:
                    pe.wait_ge(oT_copied, c - 1)
                for t in range(QT):
                    last = nc.tensor.transpose(S[:, c % 2, t * P:(t + 1) * P], o1[:, t, c * P:(c + 1) * P], ident)
                last.then_inc(oT_ready, 1)
            pe.wait_ge(ld_end, 64)
            pe.wait_ge(oT_copied, 8)
            for t in range(QT):
                for c in range(8):
                    last = nc.tensor.matmul(T4[:, t // 4, (t % 4) * P:(t % 4 + 1) * P], oT[:, c, t * P:(t + 1) * P],
                                            wos[:, c, :], start=(c == 0), stop=(c == 7))
            last.then_inc(proj_ready, 1)
            transposes(4, xhat, S[:, 0, :])
            pe.wait_ge(hatT_copied, 6)
            for t in range(QT):
                last = nc.tensor.matmul(T4[:, 2, t * E1:(t + 1) * E1], xT1[:, t * P:(t + 1) * P], wg1s,
                                        start=True, stop=True)
            last.then_inc(logits_ready, 1)
            for t in range(QT):
                if t >= 2:
                    pe.wait_ge(ex1_added, t - 1)
                for half in range(2):
                    last = nc.tensor.matmul(S[:, t % 2, half * 512:half * 512 + 512], xT1[:, t * P:(t + 1) * P],
                                            we1s[:, half * 512:half * 512 + 512], start=True, stop=True)
                last.then_inc(ex1_ready, 1)

        @block.vector
        def _(dve):
            steps = [0]
            norms = [0]

            def step(ins):
                steps[0] += 1
                ins.then_inc(dve_step, 1)
                dve.wait_ge(dve_step, steps[0])

            def finish_stats(st, tmp, mean, var):
                step(nc.vector.tensor_tensor(mean, st[:, :, 1], st[:, :, 4], ALU.add))
                step(nc.vector.tensor_tensor(tmp, st[:, :, 1], st[:, :, 4], ALU.subtract))
                step(nc.vector.tensor_scalar(mean, mean, 0.5, None, ALU.mult))
                step(nc.vector.tensor_scalar(tmp, tmp, 0.5, None, ALU.mult))
                step(nc.vector.tensor_tensor(tmp, tmp, tmp, ALU.mult))
                step(nc.vector.tensor_tensor(var, st[:, :, 2], st[:, :, 5], ALU.add))
                step(nc.vector.tensor_scalar(var, var, 1.0 / D, EPS, ALU.mult, ALU.add))
                return nc.vector.tensor_tensor(var, var, tmp, ALU.add)

            def row_stats(src):
                for t in range(QT):
                    last = nc.vector.bn_stats(bst[:, t, :], src[:, t, :])
                step(last)

            def rsqrt_var(ins, std, out_rstd):
                norms[0] += 1
                ins.then_inc(var_ready, 1)
                dve.wait_ge(std_ready, norms[0])
                step(nc.vector.reciprocal(out_rstd, std))

            def layer_norm(src, dst, ready=None):
                row_stats(src)
                rsqrt_var(finish_stats(bst, stat[:, 0:QT], xmean, xvar), xstd, xrstd)
                for t in range(QT):
                    last = nc.vector.tensor_scalar(dst[:, t, :], src[:, t, :], xmean[:, t:t + 1], xrstd[:, t:t + 1],
                                                   ALU.subtract, ALU.mult)
                if ready:
                    last.then_inc(ready, 1)
                else:
                    step(last)

            dve.wait_ge(ld_x, 16)
            layer_norm(xres, xhat, hat_ready)
            dve.wait_ge(ld_w0, 16)
            step(nc.vector.tensor_scalar(w0f, w0f, SW, None, ALU.mult))
            step(nc.vector.tensor_copy(w0_hi, w0f))
            nc.vector.tensor_tensor(w0_lo, w0f, w0_hi, ALU.subtract).then_inc(w0_split, 1)
            dve.wait_ge(ld_mask, 32)
            nc.vector.tensor_scalar(mask_rows, mask_i, -MASKED, MASKED, ALU.mult, ALU.add)
            nc.vector.tensor_copy(msel, msel_f).then_inc(w0_split, 1)
            dve.wait_ge(ld_b0, 32)
            dve.wait_ge(ld_cst, 16)
            for i, scale in ((0, SA / math.sqrt(W0)), (1, SA)):
                c = slice(i * QUADS, (i + 1) * QUADS)
                add = cst[:, C_ADD_Q if i == 0 else C_ADD_K:][:, 0:1]
                last = nc.vector.tensor_scalar(qkcol[:, c], b0s[:, c], scale, add, ALU.mult, ALU.add)
            step(nc.vector.tensor_scalar(ln1c, cst[:, C_LN:C_LN + 4], SA, None, ALU.mult))
            dve.wait_ge(hatT_copied, 1)
            nc.vector.scalar_tensor_tensor(out=xT_lo, in0=S[:, 0, :], scalar=SA, in1=xT_hi, op0=ALU.mult,
                                           op1=ALU.subtract).then_inc(hatT_copied, 1)
            dve.wait_ge(ld_ctx, 32)
            with dve.Fori(0, KC) as c:
                for u in range(4):
                    last = nc.vector.bn_stats(cbn[:, 4 * c + u, :], c_raw[:, 4 * c + u, :])
            step(nc.vector.memset(rec, 0.0))
            rsqrt_var(finish_stats(cbn, stat, cmean, cvar), cstd, crstd)
            dve.sem_inc(cn_done, 2)

            def normalized(c, b):
                dve.wait_ge(tr_done, c + 1)
                for u in range(4):
                    t = 4 * c + u
                    last = nc.vector.tensor_scalar(xb[:, b, u * P:(u + 1) * P], c_raw[:, t, :], cmean[:, bass.ds(t, 1)],
                                                   crstd[:, bass.ds(t, 1)], ALU.subtract, ALU.mult)
                last.then_inc(xb_ready, 1)

            def split(c, b):
                n = bass.ds(512 * c, 512)
                dve.wait_ge(yf_ready, c + 3)
                nc.vector.tensor_copy(cn_hi[:, n], yf[:, b, :]).then_inc(cn_hi_ready, 1)
                dve.wait_ge(cn_hi_ready, c + 1)
                nc.vector.tensor_tensor(cn_lo[:, n], yf[:, b, :], cn_hi[:, n], ALU.subtract).then_inc(cn_done, 1)

            normalized(0, 0)
            with dve.Fori(0, KC // 2) as i:
                normalized(2 * i + 1, 1)
                split(2 * i, 0)
                normalized(2 * i + 2, 0)
                split(2 * i + 1, 1)
            split(KC - 1, 0)
            for i in range(4):
                n = slice(i * PIECE, (i + 1) * PIECE)
                dve.wait_ge(cT_hi_ready, i + 1)
                last = nc.vector.scalar_tensor_tensor(out=cT_lo[:, n], in0=cT[:, n], scalar=SA, in1=cT_hi[:, n],
                                                      op0=ALU.mult, op1=ALU.subtract)
            last.then_inc(cT_hi_ready, 1)
            dve.wait_ge(cT_hi_ready, 5)
            dve.sem_inc(k0_done, 4)
            with dve.Fori(0, KC) as c:
                for g in range(QUADS):
                    n = bass.ds(512 * c, 512)
                    dve.wait_ge(k0_f, 4 * c + g + 5)
                    nc.vector.tensor_copy(ks[:, g, n], kf[:, g, :]).then_inc(k0_hi, 1)
                    dve.wait_ge(k0_hi, 4 * c + g + 1)
                    nc.vector.scalar_tensor_tensor(out=ks[:, g, n], in0=ks[:, g, n], scalar=cst[:, C_NLOW_K:C_NLOW_K + 1],
                                                   in1=kf[:, g, :], op0=ALU.mult, op1=ALU.add).then_inc(k0_done, 1)
            for g in range(QUADS):
                dve.wait_ge(q0_f, g + 1)
                if g:
                    dve.wait_ge(q0_done, g)
                step(nc.vector.tensor_copy(qtmp, probs[:, g % 2, :]))
                step(nc.vector.scalar_tensor_tensor(out=qtmp, in0=qtmp, scalar=cst[:, C_NLOW_Q:C_NLOW_Q + 1],
                                                    in1=probs[:, g % 2, :], op0=ALU.mult, op1=ALU.add))
                for j in range(4):
                    last = nc.vector.tensor_scalar(qz[:, 4 * g + j, :], qtmp, rowsel(j), None, ALU.mult)
                last.then_inc(q0_done, 1)
            dve.wait_ge(q0_done, QUADS)
            dve.sem_inc(mx_read, 2)
            with dve.Fori(0, H) as h:
                with dve.Fori(0, KC) as c:
                    for k in range(4):
                        n = (h * KC + c) * 4 + k
                        dve.wait_ge(mx_psum, n + 1)
                        nc.vector.tensor_reduce(mp[:, c, h, 2 * k:2 * k + 2],
                                                S[:, k % 2, :].rearrange("p (m n) -> p m n", m=2), AX.X, ALU.max)\
                            .then_inc(mx_read, 1)
            dve.wait_ge(mx_read, 4 * KC * H + 2)
            step(nc.vector.tensor_reduce(mx, mp.rearrange("p c h q -> p (h q) c"), AX.X, ALU.max))
            step(nc.vector.memset(maxsel, 0.0))
            for n in range(8):
                g, half = n // 2, n % 2
                if n >= 2:
                    dve.wait_ge(maxT_ready, n - 1)
                m = mx[:, 4 * g * QT:4 * (g + 1) * QT].rearrange("p (j q) -> p q j", j=4)[:, 4 * half:4 * half + 4, :]
                nc.vector.tensor_scalar(maxsel[:, n % 2, :, MAX_ROW::32], m, -1.0 / SCORE, None, ALU.mult)\
                    .then_inc(maxsel_ready, 1)
                dve.wait_ge(maxT_ready, n + 1)
                for j in range(4):
                    o = qz[:, 4 * g + j, half * 512:half * 512 + 512]
                    last = nc.vector.scalar_tensor_tensor(out=o, in0=S4[:, n % 4, :], scalar=rowsel(j), in1=o,
                                                          op0=ALU.mult, op1=ALU.add)
                last.then_inc(maxT_read, 1)
            for a in range(2):
                last = nc.vector.memset(T4[:, a, 0:QT * (W0 + 1)], 0.0)
                last.then_inc(acc_zero[0], 1)
            with dve.Fori(0, QUADS) as quad:
                for j in range(4):
                    h = quad * 4 + j
                    acc = T4[:, j % 2, 0:QT * (W0 + 1)].rearrange("p (q w) -> p q w", w=W0 + 1)
                    dve.wait_ge(pv_done[0], (h + 1) * KT + 2)
                    nc.vector.reciprocal(rec, acc[:, :, W0]).then_inc(acc_read[0], 1)
                    dve.wait_ge(acc_read[0], 2 * h + 1)
                    nc.vector.tensor_tensor(h0[:, :, bass.ds(W0 * h, W0)], acc[:, :, 0:W0],
                                            rec.unsqueeze(2).to_broadcast([P, QT, W0]), ALU.mult)\
                        .then_inc(acc_read[0], 1)
                    dve.wait_ge(acc_read[0], 2 * h + 2)
                    nc.vector.memset(T4[:, j % 2, 0:QT * (W0 + 1)], 0.0).then_inc(acc_zero[0], 1)
            dve.wait_ge(acc_zero[0], H + 2)
            step(nc.vector.tensor_tensor(xres[:, :, :], xres[:, :, :], h0[:, :, :], ALU.add))
            nc.vector.tensor_tensor(xres[:, :, :], xres[:, :, :], bvs.unsqueeze(1).to_broadcast([P, QT, D]), ALU.add)\
                .then_inc(attn0_done, 1)
            dve.wait_ge(attn0_done, 1)
            layer_norm(xres, xhat)
            row_stats(xhat)
            step(finish_stats(bst, stat[:, 0:QT], xmean, xvar))
            step(nc.vector.tensor_tensor(xmean, xmean, xmean, ALU.mult))
            rsqrt_var(nc.vector.tensor_tensor(xvar, xvar, xmean, ALU.add), xstd, xrstd)
            dve.wait_ge(ld_ffn0, 64)
            for t in range(QT):
                last = nc.vector.scalar_tensor_tensor(out=xn[:, t, :], in0=xhat[:, t, :], scalar=xrstd[:, t:t + 1],
                                                      in1=nscale, op0=ALU.mult, op1=ALU.mult)
            last.then_inc(hat_ready, 1)
            step(nc.vector.tensor_tensor(xres[:, :, :], xres[:, :, :], xhat[:, :, :], ALU.add))

            def ranks(src, n, rk, buf, k):
                gt = buf[:, 0:QT * n * n].rearrange("p (t e f) -> p t e f", e=n, f=n)
                eq = buf[:, QT * n * n:2 * QT * n * n].rearrange("p (t e f) -> p t e f", e=n, f=n)
                tri = cst[:, C_TRI:C_TRI + E0 * E0].rearrange("p (e f) -> p e f", e=E0)[:, 0:n, 0:n]
                for t in range(QT):
                    of = src[:, t, :].unsqueeze(1).to_broadcast([P, n, n])
                    to = src[:, t, :].unsqueeze(2).to_broadcast([P, n, n])
                    nc.vector.tensor_tensor(gt[:, t, :, :], of, to, ALU.is_gt)
                    last = nc.vector.tensor_tensor(eq[:, t, :, :], of, to, ALU.is_equal)
                step(last)
                for t in range(QT):
                    last = nc.vector.tensor_tensor(eq[:, t, :, :], eq[:, t, :, :], tri, ALU.mult)
                step(last)
                step(nc.vector.tensor_tensor(gt, gt, eq, ALU.add))
                step(nc.vector.tensor_reduce(rk, gt, AX.X, ALU.add))
                step(nc.vector.tensor_scalar(rk, rk, k - 0.5, None, ALU.is_lt))

            dve.wait_ge(logits_ready, 1)
            step(nc.vector.tensor_tensor(lg[:, :, :], T4[:, 2, 0:QT * E0].rearrange("p (t e) -> p t e", e=E0),
                                         bg0s.unsqueeze(1).to_broadcast([P, QT, E0]), ALU.add))
            ranks(lg, E0, rank, fab, TOP0)
            step(nc.vector.tensor_reduce(gmax, lg[:, :, :], AX.X, ALU.max))
            nc.vector.tensor_tensor(lg[:, :, :], lg[:, :, :], gmax.unsqueeze(2).to_broadcast([P, QT, E0]),
                                    ALU.subtract).then_inc(gmax_done, 1)
            dve.wait_ge(gexp_done, 1)
            step(nc.vector.tensor_tensor(gate[:, :, :], gate[:, :, :], rank[:, :, :], ALU.mult))
            step(nc.vector.tensor_reduce(gsum, gate[:, :, :], AX.X, ALU.add))
            step(nc.vector.reciprocal(grec, gsum))
            nc.vector.tensor_tensor(gate[:, :, :], gate[:, :, :], grec.unsqueeze(2).to_broadcast([P, QT, E0]),
                                    ALU.mult).then_inc(gates_ready, 1)
            y8 = T4[:, 0:2, :].rearrange("p b (t d) -> p (b t) d", d=D)
            dve.wait_ge(b2_ready, 1)
            step(nc.vector.tensor_tensor(xres[:, :, :], xres[:, :, :], y8, ALU.add))
            dve.sem_inc(h_read, 1)
            dve.sem_inc(y_added, 1)
            dve.sem_inc(s_ready, 1)

            def expert_front(e, b):
                dve.wait_ge(h_ready, e + 1)
                dve.wait_ge(sig_ready, e + 1)
                dve.wait_ge(s_ready, e + 1)
                nc.vector.tensor_scalar(fa, S[:, 0, :], ewb[:, b, 3 * P:3 * P + 1], LIMIT, ALU.add, ALU.min)\
                    .then_inc(a_ready, 1)
                nc.vector.tensor_scalar(fb, S[:, 1, :], ewb[:, b, 3 * P + 1:3 * P + 2], LIMIT, ALU.add, ALU.min)\
                    .then_inc(h_read, 1)

            def expert_back(e):
                dve.wait_ge(h_read, e + 2)
                nc.vector.tensor_scalar(fb, fb, -LIMIT, 1.0, ALU.max, ALU.add).then_inc(glu_done, 1)
                dve.wait_ge(sig_ready, e + 2)
                nc.vector.tensor_tensor(fsig, fsig, fa, ALU.mult).then_inc(glu_done, 1)
                dve.wait_ge(glu_done, 2 * e + 2)

            def expert_s(e):
                nc.vector.tensor_tensor(fs, fsig, fb, ALU.mult).then_inc(s_ready, 1)

            def expert_add(e):
                dve.wait_ge(y_ready, e + 1)
                for t in range(QT):
                    last = nc.vector.scalar_tensor_tensor(out=xres[:, t, :], in0=y8[:, t, :],
                                                          scalar=gate[:, t, bass.ds(e, 1)], in1=xres[:, t, :],
                                                          op0=ALU.mult, op1=ALU.add)
                last.then_inc(y_added, 1)

            expert_front(0, 0)
            expert_back(0)
            expert_s(0)
            expert_front(1, 1)
            expert_add(0)
            expert_back(1)
            expert_s(1)
            with dve.Fori(1, E0 // 2) as i:
                for b in range(2):
                    e = 2 * i + b
                    expert_front(e, b)
                    expert_add(e - 1)
                    expert_back(e)
                    expert_s(e)
            expert_add(E0 - 1)
            dve.wait_ge(y_added, E0 + 1)
            layer_norm(xres, xhat)
            layer_norm(xhat, xn, hat_ready)
            dve.wait_ge(hat_ready, 3)
            dve.wait_ge(hatT_ready, 3)
            nc.vector.memset(v1[0], 0.0)
            step(nc.vector.memset(v1[1], 0.0))
            for b in range(2):
                nc.vector.memset(v1[b][:, 0:KT - 1, D1:VW], 1.0)
                last = nc.vector.memset(v1[b][0:LAST, KT - 1, D1:VW], 1.0)
            last.then_inc(v1_const, 1)
            dve.wait_ge(latf_ready, 1)
            step(nc.vector.tensor_copy(lat_hi, probs[:, 0, :]))
            nc.vector.tensor_tensor(lat_lo, probs[:, 0, :], lat_hi, ALU.subtract).then_inc(hatT_copied, 2)
            for a in range(2):
                last = nc.vector.memset(T4[:, a, :], 0.0)
            last.then_inc(acc_zero[1], 1)
            dve.sem_inc(q1_done, 1)
            dve.sem_inc(k1_done, 1)

            def q1_part(n, half, b):
                dve.wait_ge(q1_hi_done, n + 1)
                o = q1_lo[:, b, half * 512:half * 512 + 512]
                nc.vector.scalar_tensor_tensor(out=o, in0=T4[:, 2, :], scalar=1.0 / SW,
                                               in1=q1_hi[:, b, half * 512:half * 512 + 512], op0=ALU.mult,
                                               op1=ALU.subtract).then_inc(q1_done, 1)

            def k1_part(n, at, width, b):
                dve.wait_ge(k1_hi_done, n + 1)
                o = k1[D1:P, b, bass.ds(at, width)]
                nc.vector.scalar_tensor_tensor(out=o, in0=T4[D1:P, 2, 0:width], scalar=1.0 / SW, in1=o, op0=ALU.mult,
                                               op1=ALU.subtract).then_inc(k1_done, 1)

            def proj1(h, b, tile=None):
                for half in range(2):
                    q1_part(2 * h + half, half, b)
                with dve.Fori(0, KT // 2) as i:
                    k1_part(h * STEPS + i, 256 * i, 256, b)
                    if tile:
                        for u in range(2):
                            tile(2 * i + u, u)
                k1_part(h * STEPS + STEPS - 1, (KT - 1) * P, P, b)
                if tile:
                    tile(KT - 1, KT - 1)

            def clip(g, b):
                dve.wait_ge(exp_done[1], g + 3)
                nc.vector.tensor_scalar(probs[:, b, :], probs[:, b, :], EXP_HI, EXP_LO, ALU.min, ALU.max)\
                    .then_inc(clipped, 1)

            def output1(h):
                accs = T4[:, 0, 0:7 * VW].rearrange("p (q w) -> p q w", w=VW), T4[:, 1, 0:VW].unsqueeze(1)
                dve.wait_ge(pv_done[1], (h + 1) * KT + 2)
                nc.vector.reciprocal(rec[:, 0:7], accs[0][:, :, D1])
                nc.vector.reciprocal(rec[:, 7:8], accs[1][:, :, D1]).then_inc(acc_read[1], 1)
                dve.wait_ge(acc_read[1], 2 * h + 1)
                for q0, q1, acc in ((0, 7, accs[0]), (7, 8, accs[1])):
                    last = nc.vector.tensor_tensor(o1[:, q0:q1, bass.ds(D1 * h, D1)], acc[:, :, 0:D1],
                                                   rec[:, q0:q1].unsqueeze(2).to_broadcast([P, q1 - q0, D1]), ALU.mult)
                last.then_inc(acc_read[1], 1)
                dve.wait_ge(acc_read[1], 2 * h + 2)
                nc.vector.memset(T4[:, 0, 0:7 * VW], 0.0)
                nc.vector.memset(T4[:, 1, 0:VW], 0.0).then_inc(acc_zero[1], 1)

            proj1(0, 0)
            with dve.Fori(0, H // 2 - 1) as pair:
                for a in range(2):
                    h = 2 * pair + a
                    proj1(h + 1, (a + 1) % 2, lambda t, u: clip(h * KT + t, (a * KT + u) % 2))
                    output1(h)
            proj1(H - 1, 1, lambda t, u: clip((H - 2) * KT + t, u % 2))
            output1(H - 2)
            with dve.Fori(0, KT // 2) as i:
                for u in range(2):
                    clip((H - 1) * KT + 2 * i + u, (KT + u) % 2)
            clip(H * KT - 1, (2 * KT - 1) % 2)
            output1(H - 1)
            dve.wait_ge(proj_ready, 1)
            dve.wait_ge(ld_end, 64)
            step(nc.vector.tensor_tensor(xres[:, :, :], xres[:, :, :], y8, ALU.add))
            step(nc.vector.tensor_tensor(xres[:, :, :], xres[:, :, :], bo1.unsqueeze(1).to_broadcast([P, QT, D]),
                                         ALU.add))
            layer_norm(xres, xhat, hat_ready)
            dve.wait_ge(logits_ready, 2)
            step(nc.vector.tensor_copy(lg1[:, :, :], T4[:, 2, 0:QT * E1].rearrange("p (t e) -> p t e", e=E1)))
            step(nc.vector.tensor_reduce(gmax, lg1[:, :, :], AX.X, ALU.max))
            nc.vector.tensor_tensor(lg1[:, :, :], lg1[:, :, :], gmax.unsqueeze(2).to_broadcast([P, QT, E1]),
                                    ALU.subtract).then_inc(gmax_done, 1)
            dve.wait_ge(gexp_done, 2)
            for passes in range(2):
                step(nc.vector.tensor_reduce(gsum, gate1[:, :, :], AX.X, ALU.add))
                if passes == 1:
                    step(nc.vector.tensor_scalar(gsum, gsum, 1e-9, None, ALU.add))
                step(nc.vector.reciprocal(grec, gsum))
                step(nc.vector.tensor_tensor(gate1[:, :, :], gate1[:, :, :],
                                             grec.unsqueeze(2).to_broadcast([P, QT, E1]), ALU.mult))
                if passes == 0:
                    ranks(gate1, E1, rank1, probs[:, 0, :], TOP1)
                    step(nc.vector.tensor_tensor(gate1[:, :, :], gate1[:, :, :], rank1[:, :, :], ALU.mult))
            for t in range(QT):
                dve.wait_ge(ex1_ready, t + 1)
                for e in range(E1):
                    last = nc.vector.scalar_tensor_tensor(
                        out=xres[:, t, :], in0=S[:, t % 2, e * P:(e + 1) * P], scalar=gate1[:, t, e:e + 1],
                        in1=xres[:, t, :], op0=ALU.mult, op1=ALU.add)
                    if e < E1 - 1:
                        step(last)
                last.then_inc(ex1_added, 1)
            dve.wait_ge(ex1_added, QT)
            nc.vector.memset(rec, 0.0).then_inc(out_ready, 1)


def kernel(**inputs):
    import numpy as np
    import concourse.bacc as bacc
    from concourse.bass_utils import run_bass_kernel_spmd

    a = {k: np.asarray(v) for k, v in inputs.items()}
    f32 = np.float32

    def rows0(w):
        t = np.zeros((D, H, 4, W0), f32)
        t[:, :, 0:3, :] = w.T.reshape(D, H, 1, W0)
        return t.reshape(D, H * 32)

    def col0(b):
        t = np.zeros((H, 4, W0), f32)
        t[:, 0:3, :] = b.reshape(H, 1, W0)
        return t.reshape(QUADS, P).T

    def twice(w):
        t = np.zeros((D, H, 2, D1), f32)
        t[...] = w.reshape(D, H, 1, D1)
        return t.reshape(D, H * 2 * D1)

    def bcast(v):
        return np.broadcast_to(v, (P, v.shape[-1]))

    row = np.arange(P) % 32
    cst = np.zeros((P, C_N), f32)
    cst[:, C_ID:C_ID + P] = np.eye(P)
    for j in range(4):
        cst[32 * j:32 * j + 32, C_ROWSEL + j] = 1.0
    cst[:, C_NLOW_K] = np.where((row >= 16) & (row < 24), -1.0, 0.0)
    cst[:, C_NLOW_Q] = np.where((row >= 8) & (row < 16), -1.0, 0.0)
    cst[:, C_ADD_K] = np.where(row == MAX_ROW, SCORE, 0.0)
    cst[:, C_ADD_Q] = np.where(row == MASK_ROW, SCORE, 0.0)
    cst[:, C_TRI:C_TRI + E0 * E0] = np.tril(np.ones((E0, E0)), -1).reshape(1, -1)
    for n, name in enumerate(("L1_xattn_ln_l_w", "L1_xattn_ln_l_b", "L1_xattn_ln_c_w", "L1_xattn_ln_c_b")):
        cst[:, C_LN + n] = a[name]
    sel = np.zeros((KC, KC, P), f32)
    for c in range(KC):
        sel[c, c, MASK_ROW::32] = SW
    mask = np.full((KC * 512,), 1 + int(NO_KEY - 0) // 10000, np.int32)
    mask[0:SK] = a["mask_BxS2_ik0"].reshape(-1)
    ctx = a["ctx_1024"].reshape(SK, D)
    ctx_t = np.zeros((D, KPAD), f32)
    ctx_t[:, 0:SK] = ctx.T
    w1 = a["L0_ffn_w1"]
    b1 = a["L0_ffn_b1"]
    ew = np.concatenate([w1[:, :, 0::2], w1[:, :, 1::2], a["L0_ffn_w2"], b1[:, 0::2, None], b1[:, 1::2, None]], axis=2)
    arrays = {
        "x": a["x"].reshape(SQ, D),
        "ctx": ctx,
        "ctx_t": ctx_t,
        "mask": mask.reshape(KC, 512),
        "consts": cst,
        "mask_sel": sel.reshape(KC, KC * P),
        "w0": np.concatenate([rows0(a["L0_xattn_Wq"]), rows0(a["L0_xattn_Wk"]), a["L0_xattn_Wv"].T], axis=1),
        "b0": np.concatenate([col0(a["L0_xattn_bq"]), col0(a["L0_xattn_bk"])], axis=1),
        "bv0": bcast(a["L0_xattn_bv"]),
        "norm_scale": bcast(a["L0_ffn_norm_scale"]),
        "wg0": a["L0_ffn_wg"],
        "bg0": bcast(a["L0_ffn_bg"]),
        "ew0": ew,
        "b2": a["L0_ffn_b2"],
        "ln1": cst[:, C_LN:C_LN + 4],
        "w1": np.concatenate([twice(a["L1_xattn_Wkv"][:, 0:H * D1]), twice(a["L1_xattn_Wq"]),
                              a["L1_xattn_Wkv"][:, H * D1:]], axis=1),
        "wo": a["L1_xattn_Wo"].reshape(8, P, D).transpose(1, 0, 2),
        "bo": bcast(a["L1_xattn_bo"]),
        "wg1": a["L1_ffn_Wg"],
        "we1": a["L1_ffn_We"].transpose(1, 0, 2).reshape(D, E1 * D),
    }
    arrays = {k: np.ascontiguousarray(v) for k, v in arrays.items()}
    nc = bacc.Bacc("TRN2", target_bir_lowering=False, num_devices=1)
    args = {k: nc.dram_tensor(f"in_{k}", v.shape, mybir.dt.from_np(v.dtype), kind="ExternalInput").ap()
            for k, v in arrays.items()}
    out = nc.dram_tensor("out_x", (SQ, D), F32, kind="ExternalOutput").ap()
    build(nc, out=out, **args)
    r = run_bass_kernel_spmd(nc, [{f"in_{k}": v for k, v in arrays.items()}], core_ids=[0])
    return r.results[0]["out_x"].reshape(1, SQ, D)
```

```python
import math
from contextlib import ExitStack

import concourse.bass as bass
from concourse import mybir

F32 = mybir.dt.float32
F16 = mybir.dt.float16
BF16 = mybir.dt.bfloat16
I32 = mybir.dt.int32
ALU = mybir.AluOpType
ACT = mybir.ActivationFunctionType
AX = mybir.AxisListType

P = 128
SQ = 1024
QT = SQ // P
SK = 6404
KT = -(-SK // P)
KC = -(-SK // 512)
KT4 = 4 * KC
KPAD = KT4 * P
LAST = SK - (KT - 1) * P
D = 128
H = 16
W0 = 8
QUADS = H // 4
D1 = 64
VW = 2 * D1 + 1
VW0 = 2 * W0 + 1
SHIFT0 = 5.5
SHIFT1 = 5.5
E0 = 16
TOP0 = 4
E1 = 8
TOP1 = 2
EPS = 1e-5
LIMIT = 7.0
ALPHA = 1.702
MASKED = -10000.0
NO_KEY = -30000.0
CLIP = 11.0

SA = 16.0
SW = 256.0
SCORE = SA * SA
MASK_ROW = 24
MAX_ROW = 25

EXP_HI = math.exp(CLIP + SHIFT1)
EXP_LO = math.exp(-CLIP + SHIFT1)

WINDOW = 4
SPREAD = -MASKED - 200.0
ENTRY_SPREAD = 0.98 * SPREAD / 2 * SCORE / W0

C_ID = 0
C_ROWSEL = C_ID + P
C_NLOW_K = C_ROWSEL + 4
C_NLOW_Q = C_NLOW_K + 1
C_ADD_K = C_NLOW_Q + 1
C_ADD_Q = C_ADD_K + 1
C_MASKROW = C_ADD_Q + 1
C_TRI = C_MASKROW
C_LN = C_TRI + E0 * E0
C_VROW = C_LN + 4
C_N = C_VROW + 1
EW = 3 * P + 2
EWBUF = 4
ARENA = 39984
W1_AT = 18240
PROJ = 3 * KC + 2
AHEAD = 3




def build(nc, x, ctx, ctx_t, mask, consts, mask_sel, w0, b0, bv0, norm_scale, wg0, bg0, ew0, b2,
          ln1, w1, wo, bo, wg1, we1, out):
    with ExitStack() as stack:
        def sb(name, shape, dt):
            return stack.enter_context(nc.sbuf_tensor(name, shape, dt))

        def psum(name, shape, dt):
            return stack.enter_context(nc.psum_tensor(name, shape, dt))

        def sem(name):
            return stack.enter_context(nc.semaphore(name))

        cst = sb("cst", [P, C_N], F32)
        cn_hi = sb("cn_hi", [P, KPAD], F16)
        cn_lo = sb("cn_lo", [P, KPAD], F16)
        probs = sb("probs", [P, 2, SQ], F32)
        xres = sb("xres", [P, QT, D], F32)
        xhat = sb("xhat", [P, QT, D], F32)
        small = sb("small", [P, 1792], F32)
        arena = sb("arena", [P, ARENA], F32)

        class Region:

            def __init__(self, of, at=0):
                self.of, self.at = of, at

            def take(self, n, dt=F32):
                words = n if dt in (F32, I32) else -(-n // 2)
                v = self.of[:, self.at:self.at + words]
                self.at += words
                return v if dt == F32 else v.bitcast(dt)

        r = Region(arena)
        cT_hi = r.take(KPAD, F16)
        cT_lo = r.take(KPAD, F16)
        v0_at = r.at
        v0 = r.take(KT4 * H * (VW0 + 1), F16).rearrange("p (t h w) -> p t h w", h=H, w=VW0 + 1)
        w0_hi = r.take(2 * 512 + D, F16)
        w0_lo = r.take(2 * 512 + D, F16)
        xT_hi = r.take(SQ, F16)
        xT_lo = r.take(SQ, F16)
        msel = r.take(KC * P, F16)[0:KC, :]
        mask_rows = r.take(512, F16)[0:KC, :]
        qz_at = r.at
        qz = r.take(H * SQ, F16).rearrange("p (h n) -> p h n", h=H)
        ks_at = r.at
        ks = r.take(QUADS * KPAD, F16).rearrange("p (g n) -> p g n", g=QUADS)
        assert r.at <= ARENA
        r = Region(arena, ks_at)
        c_raw = r.take(KT4 * D).rearrange("p (t d) -> p t d", d=D)
        cT = r.take(KPAD)
        r = Region(arena, qz_at)
        xb = r.take(2 * 512).rearrange("p (b n) -> p b n", b=2)
        yf = r.take(2 * 512).rearrange("p (b n) -> p b n", b=2)
        cbn = r.take(KT4 * 6).rearrange("p (t s) -> p t s", s=6)
        r = Region(arena, v0_at)
        mask_i = r.take(512, I32)[0:KC, :]
        msel_f = r.take(KC * P)[0:KC, :]
        r = Region(arena)
        probs0 = [probs[:, 0, :], probs[:, 1, :], r.take(SQ), r.take(SQ)]
        plow0 = [r.take(SQ, F16), r.take(SQ, F16)]
        w0f = probs[:, :, :].rearrange("p b n -> p (b n)")[:, 0:2 * 512 + D]
        kf = probs[:, :, :].rearrange("p b (c n) -> p (b c) n", n=512)
        qtmp = xhat[:, 0:4, :].rearrange("p t d -> p (t d)").bitcast(F16)
        mp = probs[:, :, :].rearrange("p b n -> p (b n)")[:, 0:KC * H * QT].rearrange(
            "p (c h q) -> p c h q", h=H, q=QT)
        maxsel = xhat[:, :, :].rearrange("p (b t) d -> p b t d", b=2)
        h0 = xhat
        r = Region(arena)
        fT = r.take(SQ)
        ewb = r.take(EWBUF * EW).rearrange("p (b n) -> p b n", b=EWBUF)
        fab = r.take(7 * SQ)
        fa, fb, fsig = ([fab[:, (2 * i + j) * SQ:(2 * i + j + 1) * SQ] for j in range(2)] for i in range(3))
        fs = fab[:, 6 * SQ:7 * SQ]
        xn = r.take(QT * D).rearrange("p (t d) -> p t d", d=D)
        gT = r.take(SQ)[0:E0, :]
        b2s = r.take(D)[0:E0, :]
        nscale = r.take(D)
        wg0s = r.take(E0)
        bg0s = r.take(E0)
        bos = r.take(D)
        assert r.at <= W1_AT
        r = Region(arena, W1_AT)
        w1_hi = r.take(2 * H * P + H * D1, F16)
        w1_lo = r.take(2 * H * P + H * D1, F16)
        w1f_at = r.at
        w1f = r.take(2 * H * P + H * D1)
        r = Region(arena, w1f_at)
        wos = r.take(8 * D).rearrange("p (c n) -> p c n", c=8)
        we1s = r.take(E1 * D)
        xT1 = r.take(SQ)
        bo1 = r.take(D)
        wg1s = r.take(E1)
        r = Region(arena, w1f_at + 2 * H * P + H * D1)
        lat_hi = r.take(SQ, F16)
        lat_lo = r.take(SQ, F16)
        q1_hi = r.take(2 * SQ, F16).rearrange("p (b n) -> p b n", b=2)
        q1_lo = r.take(2 * SQ, F16).rearrange("p (b n) -> p b n", b=2)
        v1b = r.take(KT4 * (VW + 1), F16).rearrange("p (t w) -> p t w", w=VW + 1)
        probs1 = [probs[:, 0, :], probs[:, 1, :], r.take(SQ), r.take(SQ)]
        proj_f = r.take(4 * 256).rearrange("p (b n) -> p b n", b=4)
        acc_f = r.take(QT * VW).rearrange("p (q w) -> p q w", w=VW)
        acc_s = r.take(QT * D1).rearrange("p (q w) -> p q w", w=D1)
        assert r.at <= ARENA, r.at
        plow1 = [xhat[:, 4 * b:4 * b + 4, :].rearrange("p t d -> p (t d)").bitcast(F16) for b in range(2)]
        r = Region(arena)
        k1 = r.take(2 * KPAD, F16).rearrange("p (b n) -> p b n", b=2)
        v1a = r.take(KT4 * (VW + 1), F16).rearrange("p (t w) -> p t w", w=VW + 1)
        o1 = r.take(QT * H * D1).rearrange("p (t n) -> p t n", t=QT)
        assert r.at <= W1_AT, r.at
        v1 = [v1a, v1b]
        oT = arena[:, 0:8 * SQ].rearrange("p (c n) -> p c n", c=8)
        wk1_hi, wk1_lo = (w[:, 0:H * P].rearrange("p (h n) -> p h n", h=H) for w in (w1_hi, w1_lo))
        wq1_hi, wq1_lo = (w[:, H * P:2 * H * P].rearrange("p (h n) -> p h n", h=H) for w in (w1_hi, w1_lo))
        wv1_hi, wv1_lo = (w[:, 2 * H * P:].rearrange("p (h n) -> p h n", h=H) for w in (w1_hi, w1_lo))

        r = Region(small)
        b0s = r.take(2 * QUADS)
        qkcol = r.take(2 * QUADS)
        bst = r.take(QT * 6).rearrange("p (t s) -> p t s", s=6)
        xmean = r.take(QT)
        xvar = r.take(QT)
        xstd = r.take(QT)
        xrstd = r.take(QT)
        stat = r.take(KT4)
        cmean = r.take(KT4)
        cvar = r.take(KT4)
        cstd = r.take(KT4)
        crstd = r.take(KT4)
        mx = r.take(H * QT)
        rec = r.take(QT)
        shift1 = r.take(1)
        gate = r.take(QT * E0).rearrange("p (t e) -> p t e", e=E0)
        lg = r.take(QT * E0).rearrange("p (t e) -> p t e", e=E0)
        rank = r.take(QT * E0).rearrange("p (t e) -> p t e", e=E0)
        gmax = r.take(QT)
        gsum = r.take(QT)
        grec = r.take(QT)
        bvs = r.take(D)
        ln1s = r.take(4)
        ln1c = r.take(4)
        gate1 = r.take(QT * E1).rearrange("p (t e) -> p t e", e=E1)
        lg1 = r.take(QT * E1).rearrange("p (t e) -> p t e", e=E1)
        rank1 = r.take(QT * E1).rearrange("p (t e) -> p t e", e=E1)
        qbound = r.take(QUADS)
        wmax = r.take(1)
        cmax = r.take(1)
        bounds = r.take(4)
        decide = r.take(8)
        window = r.take(1, I32)
        assert r.at <= 1792, r.at

        ident = cst[:, C_ID:C_ID + P]

        def rowsel(j):
            return cst[:, C_ROWSEL + j:C_ROWSEL + j + 1]

        S = psum("S", [P, 2, SQ], F32)
        A = psum("A", [P, 4, 512], F32)
        S4 = S[:, :, :].rearrange("p b (c n) -> p (b c) n", n=512)
        T4 = A[:, :, :]
        M4 = [S4[:, 0:2, :], S4[:, 2:4, :], T4[:, 0:2, :], T4[:, 2:4, :]]

        ld_cst = sem("ld_cst")
        ld_x = sem("ld_x")
        ld_ctx = sem("ld_ctx")
        ld_ctx_t = sem("ld_ctx_t")
        ld_mask = sem("ld_mask")
        ld_w0 = sem("ld_w0")
        ld_b0 = sem("ld_b0")
        ld_ffn0 = sem("ld_ffn0")
        ld_ew = [sem(f"ld_ew{b}") for b in range(EWBUF)]
        ld_w1 = sem("ld_w1")
        ld_end = sem("ld_end")
        stored = sem("stored")
        raw_zeroed = sem("raw_zeroed")
        dve_step = sem("dve_step")
        pool_step = sem("pool_step")
        w0_split = sem("w0_split")
        var_ready = sem("var_ready")
        std_ready = sem("std_ready")
        hat_ready = sem("hat_ready")
        hatT_ready = sem("hatT_ready")
        hatT_copied = sem("hatT_copied")
        latf_ready = sem("latf_ready")
        cT_hi_ready = sem("cT_hi_ready")
        xb_ready = sem("xb_ready")
        tr_done = sem("tr_done")
        yf_ready = sem("yf_ready")
        cn_done = sem("cn_done")
        k0_psum = sem("k0_psum")
        k0_f = sem("k0_f")
        k0_hi = sem("k0_hi")
        k0_done = sem("k0_done")
        v0_psum = sem("v0_psum")
        v0_done = sem("v0_done")
        v0_hi = sem("v0_hi")
        v0_ones = sem("v0_ones")
        q0_psum = sem("q0_psum")
        q0_f = sem("q0_f")
        q0_done = sem("q0_done")
        bounds_ready = sem("bounds_ready")
        boundsT_ready = sem("boundsT_ready")
        window_ready = sem("window_ready")
        mx_psum = sem("mx_psum")
        mx_read = sem("mx_read")
        maxsel_ready = sem("maxsel_ready")
        maxT_ready = sem("maxT_ready")
        maxT_read = sem("maxT_read")
        scores_ready = [sem("scores_ready0"), sem("scores_ready1")]
        exp_done = [sem("exp_done0"), sem("exp_done1")]
        clipped = sem("clipped")
        low_ready = [sem("low_ready0"), sem("low_ready1")]
        pv_done = [sem("pv_done0"), sem("pv_done1")]
        acc_zero = sem("acc_zero")
        acc_read = sem("acc_read")
        acc_copied = sem("acc_copied")
        acc_rec = sem("acc_rec")
        acc_summed = sem("acc_summed")
        head_done = sem("head_done")
        v1_last = sem("v1_last")
        w1_split = sem("w1_split")
        v1_const = sem("v1_const")
        proj_psum = sem("proj_psum")
        proj_hi = sem("proj_hi")
        proj_read = sem("proj_read")
        proj_done = sem("proj_done")
        logits_ready = sem("logits_ready")
        gmax_done = sem("gmax_done")
        gexp_done = sem("gexp_done")
        gates_ready = sem("gates_ready")
        gateT_ready = sem("gateT_ready")
        gateT_copied = sem("gateT_copied")
        b2_ready = sem("b2_ready")
        ffn_base = sem("ffn_base")
        h_ready = sem("h_ready")
        a_raw = sem("a_raw")
        a_ready = sem("a_ready")
        b_ready = sem("b_ready")
        h_read = sem("h_read")
        sig_ready = sem("sig_ready")
        glu_done = sem("glu_done")
        s_ready = sem("s_ready")
        y_ready = sem("y_ready")
        y_added = sem("y_added")
        x2_ready = sem("x2_ready")
        oT_ready = sem("oT_ready")
        oT_copied = sem("oT_copied")
        proj_ready = sem("proj_ready")
        ex1_ready = sem("ex1_ready")
        ex1_added = sem("ex1_added")
        out_ready = sem("out_ready")
        attn0_done = sem("attn0_done")

        PIECE = KPAD // 4
        block = stack.enter_context(nc.Block())

        @block.sync
        def _(sp):
            sp.dma_start(cst[:, :], consts).then_inc(ld_cst, 16)
            sp.dma_start(xres[:, :, :], x.rearrange("(t p) d -> p t d", p=P)).then_inc(ld_x, 16)
            full = (KT - 1) * P
            sp.dma_start(c_raw[:, 0:KT - 1, :], ctx[0:full, :].rearrange("(t p) d -> p t d", p=P)).then_inc(ld_ctx, 16)
            sp.wait_ge(raw_zeroed, 1)
            sp.dma_start(c_raw[0:LAST, KT - 1, :], ctx[full:SK, :]).then_inc(ld_ctx, 16)
            sp.wait_ge(attn0_done, 1)
            for dst, src in ((b2s, b2), (nscale, norm_scale), (wg0s, wg0), (bg0s, bg0)):
                sp.dma_start(dst, src).then_inc(ld_ffn0, 16)
            for b in range(EWBUF):
                sp.dma_start(ewb[:, b, :], ew0[b, :, :]).then_inc(ld_ew[b], 16)
            sp.dma_start(w1f, w1).then_inc(ld_w1, 16)
            sp.dma_start(ln1s, ln1).then_inc(ld_w1, 16)
            with sp.Fori(0, E0 // EWBUF - 1) as i:
                for b in range(EWBUF):
                    sp.wait_ge(y_ready, EWBUF * i + b + 1)
                    sp.dma_start(ewb[:, b, :], ew0[EWBUF * i + EWBUF + b, :, :]).then_inc(ld_ew[b], 16)
            sp.wait_ge(w1_split, 1)
            for dst, src in ((wos, wo), (we1s, we1), (bo1, bo), (wg1s, wg1)):
                sp.dma_start(dst, src).then_inc(ld_end, 16)
            sp.wait_ge(out_ready, 1)
            sp.dma_start(out.rearrange("(t p) d -> p t d", p=P), xres[:, :, :]).then_inc(stored, 16)
            sp.wait_ge(stored, 16)

        @block.gpsimd
        def _(pool):
            steps = [0]

            def step(ins):
                steps[0] += 1
                ins.then_inc(pool_step, 1)
                pool.wait_ge(pool_step, steps[0])

            nc.gpsimd.memset(c_raw[:, KT - 1:KT4, :], 0.0).then_inc(raw_zeroed, 1)
            pool.sem_inc(cn_done, 2)

            def cn_low(c, b):
                n = bass.ds(512 * c, 512)
                pool.wait_ge(yf_ready, c + 3)
                pool.wait_ge(cn_done, c + 2)
                nc.gpsimd.tensor_tensor(cn_lo[:, n], yf[:, b, :], cn_hi[:, n], ALU.subtract).then_inc(cn_done, 1)

            with pool.Fori(0, KC // 2) as i:
                for b in range(2):
                    cn_low(2 * i + b, b)
            cn_low(KC - 1, 0)
            pool.wait_ge(w0_split, 2)
            nc.gpsimd.memset(v0[:, :, :, 2 * W0:VW0], 1.0).then_inc(v0_ones, 1)
            pool.wait_ge(ld_w1, 32)
            step(nc.gpsimd.tensor_scalar(w1f, w1f, SW, None, ALU.mult))
            step(nc.gpsimd.tensor_copy(w1_hi, w1f))
            nc.gpsimd.tensor_tensor(w1_lo, w1f, w1_hi, ALU.subtract).then_inc(w1_split, 1)
            pool.sem_inc(proj_done, 3)

            def low(n, o, f, h):
                pool.wait_ge(proj_done, n + 3)
                pool.wait_ge(proj_read, n + 2)
                nc.gpsimd.tensor_tensor(o, f, h, ALU.subtract).then_inc(proj_done, 1)

            def slots1(h, b, c, u, first=None, last=False):
                n = h * PROJ + 3 * c + (2 if first is None else first)
                flat = proj_f.rearrange("p b n -> p (b n)")
                if u < 2:
                    k = k1[D1:P, b, bass.ds(512 * c + 256 * u, 256)]
                    low(n + u, k, proj_f[D1:P, u, :], k)
                elif u == 2 and not last:
                    v = v1[b][:, bass.ds(4 * c, 4), :]
                    low(n + 2, v[:, :, 0:D1], proj_f[:, 2, :].rearrange("p (t w) -> p t w", w=D1), v[:, :, D1:2 * D1])
                elif u == 2:
                    v = v1[b][:, 4 * c:4 * c + 2, :]
                    pool.wait_ge(proj_done, n + 5)
                    pool.wait_ge(proj_read, n + 4)
                    nc.gpsimd.tensor_tensor(v[:, :, 0:D1], proj_f[:, 2, 0:2 * D1].rearrange("p (t w) -> p t w", w=D1),
                                            v[:, :, D1:2 * D1], ALU.subtract).then_inc(v1_last, 1)
                    pool.wait_ge(v1_last, h + 1)
                    v = v1[b][0:LAST, 4 * c + 2, :]
                    nc.gpsimd.tensor_tensor(v[:, 0:D1], proj_f[0:LAST, 2, 2 * D1:3 * D1], v[:, D1:2 * D1],
                                            ALU.subtract).then_inc(proj_done, 1)
                elif first is not None:
                    q = slice(first * 512, first * 512 + 512)
                    low(n + 3, q1_lo[:, b, q], flat[:, 0:512], q1_hi[:, b, q])

            def output1(h):
                if isinstance(h, int) and h >= H - 2:
                    pool.wait_ge(proj_done, H * PROJ + 3)
                    pool.wait_ge(head_done, h + 1)
                else:
                    pool.wait_ge(proj_done, (h + 2) * PROJ + 8 + 3)
                pool.wait_ge(acc_copied, h + 1)
                nc.gpsimd.tensor_tensor(acc_s, acc_f[:, :, 0:D1], acc_f[:, :, D1:2 * D1], ALU.add)\
                    .then_inc(acc_summed, 1)
                pool.wait_ge(acc_summed, h + 1)
                pool.wait_ge(acc_rec, 2 * h + 2)
                nc.gpsimd.tensor_tensor(o1[:, :, bass.ds(D1 * h, D1)], acc_s,
                                        rec.unsqueeze(2).to_broadcast([P, QT, D1]), ALU.mult).then_inc(head_done, 1)

            def projections1(h, b, out_head=None):
                for c in range(2):
                    for u in range(4):
                        slots1(h, b, c, u, c)
                if out_head is not None:
                    output1(out_head)
                with pool.Fori(2, KC - 1) as c:
                    for u in range(3):
                        if u == 0 and out_head is not None:
                            pool.wait_ge(head_done, out_head + 2)
                        slots1(h, b, c, u)
                for u in range(3):
                    slots1(h, b, KC - 1, u, last=True)

            projections1(0, 0)
            projections1(1, 1)
            projections1(2, 0, 0)
            with pool.Fori(1, H // 2 - 1) as pair:
                projections1(2 * pair + 1, 1, 2 * pair - 1)
                projections1(2 * pair + 2, 0, 2 * pair)
            projections1(H - 1, 1, H - 3)
            output1(H - 2)
            output1(H - 1)

        def act_sqrt(act, n, std, var):
            act.wait_ge(var_ready, n)
            nc.scalar.activation(std, var, ACT.Sqrt).then_inc(std_ready, 1)

        @block.scalar
        def _(act):
            for dst, src, s in ((w0f, w0, ld_w0), (b0s, b0, ld_b0), (bvs, bv0, ld_b0),
                                (mask_i, mask, ld_mask), (msel_f, mask_sel, ld_mask), (cT, ctx_t, ld_ctx_t)):
                act.dma_start(dst, src).then_inc(s, 16)
            act_sqrt(act, 1, xstd, xvar)
            act.wait_ge(hatT_ready, 1)
            nc.scalar.activation(xT_hi, S[:, 0, :], ACT.Copy, scale=SA).then_inc(hatT_copied, 1)
            act.wait_ge(ld_ctx_t, 16)
            for i in range(4):
                nc.scalar.activation(cT_hi[:, i * PIECE:(i + 1) * PIECE], cT[:, i * PIECE:(i + 1) * PIECE],
                                     ACT.Copy, scale=SA).then_inc(cT_hi_ready, 1)
            act_sqrt(act, 2, cstd, cvar)
            act.sem_inc(yf_ready, 2)

            def scaled(c, b):
                act.wait_ge(tr_done, c + 3)
                act.wait_ge(cn_done, c + 1)
                nc.scalar.activation(cn_hi[:, bass.ds(512 * c, 512)], S4[:, b, :], ACT.Identity, bias=ln1c[:, 3:4],
                                     scale=ln1c[:, 2:3])
                nc.scalar.activation(yf[:, b, :], S4[:, b, :], ACT.Identity, bias=ln1c[:, 3:4],
                                     scale=ln1c[:, 2:3]).then_inc(yf_ready, 1)

            with act.Fori(0, KC // 2) as i:
                for b in range(2):
                    scaled(2 * i + b, b)
            scaled(KC - 1, 0)
            for g in range(QUADS):
                act.wait_ge(q0_psum, g + 1)
                if g >= 2:
                    act.wait_ge(q0_done, g - 1)
                nc.scalar.activation(probs[:, g % 2, :], S[:, g % 2, :], ACT.Identity, bias=qkcol[:, g:g + 1],
                                     scale=SA / (SA * SW * math.sqrt(W0))).then_inc(q0_f, 1)
            act.sem_inc(k0_f, 4)
            act.sem_inc(exp_done[0], 2)

            def attention0(C0, NC):
                with act.Fori(0, NC) as c:
                    for g in range(QUADS):
                        act.wait_ge(k0_psum, 4 * c + g + 1)
                        act.wait_ge(k0_done, 4 * c + g + 1)
                        nc.scalar.activation(kf[:, g, :], S4[:, g, :], ACT.Identity, bias=qkcol[:, QUADS + g:QUADS + g + 1],
                                             scale=1.0 / SW).then_inc(k0_f, 1)
                    for u in range(4):
                        act.wait_ge(v0_psum, 4 * c + u + 1)
                        nc.scalar.activation(v0[:, 4 * (C0 + c) + u, :, W0:2 * W0],
                                             T4[:, u, 0:D].rearrange("p (h w) -> p h w", w=W0),
                                             ACT.Copy, scale=1.0 / SW).then_inc(v0_hi, 1)
                nc.scalar.preload_act_table(ACT.Exp)
                act.wait_ge(mx_read, 4 * NC * H + 4)
                act.wait_ge(maxT_read, 8)
                with act.Fori(0, NC * H) as n:
                    for u in range(4):
                        g = 4 * n + u
                        act.wait_ge(scores_ready[0], g + 1)
                        act.wait_ge(pv_done[0], g + 1)
                        nc.scalar.activation(probs0[u], S[:, u % 2, :], ACT.Exp, scale=1.0 / SCORE)\
                            .then_inc(exp_done[0], 1)

            act.wait_ge(q0_done, QUADS)
            act.wait_ge(window_ready, 1)
            with act.If(act.value_load(window[0:1, :], min_val=0, max_val=1) > 0):
                attention0(KC - WINDOW, WINDOW)
            with act.Else():
                attention0(0, KC)
            act_sqrt(act, 3, xstd, xvar)
            act_sqrt(act, 4, xstd, xvar)
            act.wait_ge(hatT_ready, 2)
            nc.scalar.copy(fT, S[:, 0, :]).then_inc(hatT_copied, 1)
            act.wait_ge(gmax_done, 1)
            nc.scalar.activation(gate[:, :, :], lg[:, :, :], ACT.Exp).then_inc(gexp_done, 1)
            act.wait_ge(gateT_ready, 1)
            nc.scalar.copy(gT, S[0:E0, 0, :]).then_inc(gateT_copied, 1)
            nc.scalar.preload_act_table(ACT.Sigmoid)
            with act.Fori(0, E0 // EWBUF) as i:
                for b in range(EWBUF):
                    e = EWBUF * i + b
                    act.wait_ge(h_ready, e + 1)
                    act.wait_ge(glu_done, e + 1)
                    nc.scalar.activation(fa[b % 2], S[:, 0, :], ACT.Identity, bias=ewb[:, b, 3 * P:3 * P + 1])\
                        .then_inc(a_raw, 1)
                    act.wait_ge(s_ready, e + 1)
                    nc.scalar.activation(fb[b % 2], S[:, 1, :], ACT.Identity, bias=ewb[:, b, 3 * P + 1:3 * P + 2])\
                        .then_inc(h_read, 1)
                    act.wait_ge(a_ready, e + 1)
                    nc.scalar.activation(fsig[b % 2], fa[b % 2], ACT.Sigmoid, scale=ALPHA).then_inc(sig_ready, 1)
            act_sqrt(act, 5, xstd, xvar)
            act_sqrt(act, 6, xstd, xvar)
            act.wait_ge(hatT_ready, 3)
            nc.scalar.activation(probs[:, 0, :], S[:, 0, :], ACT.Identity, bias=ln1c[:, 1:2],
                                 scale=ln1c[:, 0:1]).then_inc(latf_ready, 1)
            nc.scalar.preload_act_table(ACT.Exp)

            def evacuate(n, out_hi, scale, width, at, bank, rows=P):
                act.wait_ge(proj_psum, n + 1)
                src = T4[0:rows, bank, 0:width]
                f = proj_f[0:rows, :, :].rearrange("p b n -> p (b n)")[:, at:at + width]
                nc.scalar.activation(out_hi, src if len(out_hi.shape) == 2 else src.rearrange(
                    "p (t w) -> p t w", w=D1), ACT.Copy, scale=scale).then_inc(proj_hi, 1)
                nc.scalar.activation(f, src, ACT.Copy, scale=scale).then_inc(proj_read, 1)

            def k1_slot(n, c, half, b, bank):
                act.wait_ge(proj_done, n + 3 - half)
                evacuate(n, k1[:, b, bass.ds(512 * c + 256 * half, 256)], 1.0 / SW, 256, 256 * half,
                         bank)

            def v1_slot(n, c, b, last, bank):
                act.wait_ge(proj_done, n + 1)
                if not last:
                    evacuate(n, v1[b][:, bass.ds(4 * c, 4), D1:2 * D1], 1.0 / SW, 4 * D1, 512, bank)
                    return
                act.wait_ge(proj_psum, n + 1)
                o = v1[b]
                nc.scalar.activation(o[:, 4 * c:4 * c + 2, D1:2 * D1], T4[:, bank, 0:2 * D1].rearrange(
                    "p (t w) -> p t w", w=D1), ACT.Copy, scale=1.0 / SW)
                nc.scalar.activation(o[0:LAST, 4 * c + 2, D1:2 * D1], T4[0:LAST, bank, 2 * D1:3 * D1], ACT.Copy,
                                     scale=1.0 / SW).then_inc(proj_hi, 1)
                nc.scalar.activation(proj_f[:, 2, 0:3 * D1], T4[:, bank, 0:3 * D1], ACT.Copy,
                                     scale=1.0 / SW).then_inc(proj_read, 1)

            def q1_slot(n, half, b, bank):
                act.wait_ge(proj_done, n + 3)
                evacuate(n, q1_hi[:, b, half * 512:half * 512 + 512], 1.0 / SW, 512, 0, bank)

            def slots1(h, b, c, u, first=None, last=False, early=False):
                n = h * PROJ + 3 * c + (2 if first is None else first)
                bank = 3 - u if early else 3
                if u < 2:
                    k1_slot(n + u, c, u, b, bank)
                elif u == 2:
                    v1_slot(n + 2, c, b, last, bank)
                elif first is not None:
                    q1_slot(n + 3, first, b, bank)

            def exp1(g, u):
                act.wait_ge(scores_ready[1], g + 1)
                act.wait_ge(pv_done[1], g + 1)
                nc.scalar.activation(probs1[u % 4], S[:, u % 2, :], ACT.Exp, bias=shift1,
                                     scale=1.0 / (SCORE * math.sqrt(D1))).then_inc(exp_done[1], 1)

            def copy_sums(h):
                act.wait_ge(pv_done[1], (h + 1) * KT4 + 4)
                act.wait_ge(head_done, h + 1)
                for k in range(3):
                    q = slice(3 * k, min(3 * k + 3, QT))
                    w = (q.stop - q.start) * VW
                    last = nc.scalar.copy(acc_f[:, q, :], T4[:, k, 0:w].rearrange("p (q w) -> p q w", w=VW))
                last.then_inc(acc_copied, 1)

            def head1(h, hb, first_head=False, last_head=False):
                def chunk(c, first=None, last=False):
                    for u in range(4):
                        if first == 0 and u == 0 and not first_head:
                            copy_sums(h - 1)
                        if not last_head:
                            slots1(h + 1, 1 - hb, c, u, first, last)
                        if not (last and last_head and u >= 4 - AHEAD):
                            exp1(h * KT4 + 4 * c + u + AHEAD, u + AHEAD)

                chunk(0, 0)
                chunk(1, 1)
                with act.Fori(2, KC - 1) as c:
                    chunk(c)
                chunk(KC - 1, last=True)

            act.sem_inc(exp_done[1], 2)
            act.wait_ge(v1_const, 1)
            for c in range(2):
                for u in range(4):
                    slots1(0, 0, c, u, c, early=True)
            with act.Fori(2, KC - 1) as c:
                for u in range(3):
                    slots1(0, 0, c, u, early=True)
            for u in range(3):
                slots1(0, 0, KC - 1, u, last=True, early=True)
            for u in range(AHEAD):
                exp1(u, u)
            head1(0, 0, first_head=True)
            head1(1, 1)
            with act.Fori(1, H // 2 - 1) as pair:
                for a in range(2):
                    head1(2 * pair + a, a)
            head1(H - 2, 0)
            head1(H - 1, 1, last_head=True)
            copy_sums(H - 1)
            for c in range(8):
                act.wait_ge(oT_ready, c + 1)
                nc.scalar.copy(oT[:, c, :], S[:, c % 2, :]).then_inc(oT_copied, 1)
            act_sqrt(act, 7, xstd, xvar)
            act.wait_ge(hatT_ready, 4)
            nc.scalar.copy(xT1, S[:, 0, :]).then_inc(hatT_copied, 1)
            act.wait_ge(gmax_done, 2)
            nc.scalar.activation(gate1[:, :, :], lg1[:, :, :], ACT.Exp).then_inc(gexp_done, 1)

        @block.tensor
        def _(pe):
            def transposes(n, src, dst):
                pe.wait_ge(hat_ready, n)
                for t in range(QT):
                    last = nc.tensor.transpose(dst[:, t * P:(t + 1) * P], src[:, t, :], ident)
                last.then_inc(hatT_ready, 1)

            def split_product(o, l_hi, l_lo, r_hi, r_lo, **kw):
                nc.tensor.matmul(o, l_hi, r_hi, start=True, stop=False, **kw)
                nc.tensor.matmul(o, l_lo, r_hi, start=False, stop=False, **kw)
                return nc.tensor.matmul(o, l_hi, r_lo, start=False, stop=True, **kw)

            pe.wait_ge(ld_cst, 16)
            transposes(1, xhat, S[:, 0, :])
            pe.wait_ge(hatT_copied, 2)
            pe.sem_inc(tr_done, 2)

            def ctx_transposes(c, b):
                pe.wait_ge(xb_ready, c + 1)
                pe.wait_ge(yf_ready, c + 1)
                for u in range(4):
                    last = nc.tensor.transpose(S4[:, b, u * P:(u + 1) * P], xb[:, b, u * P:(u + 1) * P], ident)
                last.then_inc(tr_done, 1)

            with pe.Fori(0, KC // 2) as i:
                for b in range(2):
                    ctx_transposes(2 * i + b, b)
            ctx_transposes(KC - 1, 0)

            pe.wait_ge(w0_split, 2)
            pe.wait_ge(yf_ready, KC + 2)
            for g in range(QUADS):
                if g >= 2:
                    pe.wait_ge(q0_f, g - 1)
                w = slice(g * P, (g + 1) * P)
                for half in range(2):
                    n = slice(half * 512, half * 512 + 512)
                    last = split_product(S[:, g % 2, n], w0_hi[:, w], w0_lo[:, w], xT_hi[:, n], xT_lo[:, n])
                last.then_inc(q0_psum, 1)
            pe.wait_ge(q0_f, QUADS)
            pe.wait_ge(q0_done, QUADS)
            def hi(p, q):
                return p[:, q * P:(q + 1) * P].bitcast(BF16)[:, 1::2]

            pe.wait_ge(bounds_ready, 1)
            for j in range(4):
                last = nc.tensor.transpose(S4[0:1, 0, j * P:(j + 1) * P], bounds[:, j:j + 1], ident)
            last.then_inc(boundsT_ready, 1)

            def attention0(C0, NC):
                pe.wait_ge(cT_hi_ready, 5)
                with pe.Fori(0, NC) as c:
                    for g in range(QUADS):
                        pe.wait_ge(k0_f, 4 * c + g + 1)
                        chunk = bass.ds(512 * (C0 + c), 512)
                        w = slice(512 + g * P, 512 + (g + 1) * P)
                        nc.tensor.matmul(S4[:, g, :], w0_hi[:, w], cT_hi[:, chunk], start=True, stop=False)
                        nc.tensor.matmul(S4[:, g, :], w0_lo[:, w], cT_hi[:, chunk], start=False, stop=False)
                        nc.tensor.matmul(S4[:, g, :], w0_hi[:, w], cT_lo[:, chunk], start=False, stop=False)
                        nc.tensor.matmul(S4[:, g, :], msel[:, bass.ds(P * (C0 + c), P)], mask_rows, start=False,
                                         stop=True).then_inc(k0_psum, 1)
                    for u in range(4):
                        pe.wait_ge(v0_done, 4 * c + u + 1)
                        tile = bass.ds(512 * (C0 + c) + u * P, P)
                        nc.tensor.matmul(T4[:, u, 0:D], cT_hi[:, tile], w0_hi[:, 1024:1024 + D], start=True, stop=False)
                        nc.tensor.matmul(T4[:, u, 0:D], cT_hi[:, tile], w0_lo[:, 1024:1024 + D], start=False, stop=False)
                        nc.tensor.matmul(T4[:, u, 0:D], cT_lo[:, tile], w0_hi[:, 1024:1024 + D], start=False,
                                         stop=True).then_inc(v0_psum, 1)
                pe.wait_ge(k0_done, 4 * NC + 4)
                with pe.Fori(0, H) as h:
                    with pe.Fori(0, NC) as c:
                        for k in range(4):
                            pe.wait_ge(mx_read, (h * NC + c) * 4 + k + 1)
                            for m in range(2):
                                last = nc.tensor.matmul(M4[k][:, m, :], qz[:, h, (2 * k + m) * P:(2 * k + m + 1) * P],
                                                        ks[:, h // 4, bass.ds(512 * (C0 + c), 512)], start=True, stop=True)
                            last.then_inc(mx_psum, 1)
                for n in range(8):
                    pe.wait_ge(maxsel_ready, n + 1)
                    if n >= 4:
                        pe.wait_ge(maxT_read, n - 3)
                    for u in range(4):
                        last = nc.tensor.transpose(S4[:, n % 4, u * P:(u + 1) * P], maxsel[:, n % 2, u, :], ident)
                    last.then_inc(maxT_ready, 1)

                def scores0(g, u, quad, h, t):
                    pe.wait_ge(exp_done[0], g + 1)
                    for half in range(2):
                        last = nc.tensor.matmul(S[:, u % 2, half * 512:half * 512 + 512], ks[:, quad, bass.ds(P * t, P)],
                                                qz[:, h, half * 512:half * 512 + 512], start=True, stop=True)
                    last.then_inc(scores_ready[0], 1)

                def pv0(g, u, h, t, a):
                    pe.wait_ge(low_ready[0], g + 1)
                    for q in range(QT):
                        o = T4[:, a, q * VW0:(q + 1) * VW0]
                        nc.tensor.matmul(o, hi(probs0[u], q), v0[:, t, h, 0:VW0], start=False, stop=False,
                                         skip_group_check=True)
                        last = nc.tensor.matmul(o[:, W0:VW0], plow0[u % 2][:, q * P:(q + 1) * P], v0[:, t, h, W0:VW0],
                                                start=False, stop=False, skip_group_check=True)
                    last.then_inc(pv_done[0], 1)

                pe.sem_inc(pv_done[0], 4)
                pe.wait_ge(maxT_read, 8)
                pe.wait_ge(v0_done, 4 * NC + 4)
                pe.wait_ge(v0_ones, 1)
                for u in range(AHEAD):
                    scores0(u, u, 0, 0, 4 * C0 + u)

                def quad0(quad, last_quad):
                    for j in range(4):
                        h = quad * 4 + j

                        def chunk(c, last):
                            for u in range(4):
                                g = 4 * (h * NC + c) + u
                                t = 4 * (C0 + c) + u
                                if not last or u < 4 - AHEAD:
                                    scores0(g + AHEAD, u + AHEAD, quad, h, t + AHEAD)
                                elif j < 3 or not last_quad:
                                    scores0(g + AHEAD, u + AHEAD, quad + (j == 3), h + 1, 4 * C0 + u + AHEAD - 4)
                                if not last and u == 0:
                                    pe.wait_ge(acc_zero, h + 1)
                                pv0(g, u, h, t, j % 2)

                        with pe.Fori(0, NC - 1) as c:
                            chunk(c, False)
                        chunk(NC - 1, True)

                with pe.Fori(0, QUADS - 1) as quad:
                    quad0(quad, False)
                quad0(QUADS - 1, True)

            pe.wait_ge(window_ready, 1)
            with pe.If(pe.value_load(window[0:1, :], min_val=0, max_val=1) > 0):
                attention0(KC - WINDOW, WINDOW)
            with pe.Else():
                attention0(0, KC)
            transposes(2, xn, S[:, 0, :])
            pe.wait_ge(ld_ffn0, 64)
            pe.wait_ge(hatT_copied, 3)
            for t in range(QT):
                last = nc.tensor.matmul(T4[:, 2, t * E0:(t + 1) * E0], fT[:, t * P:(t + 1) * P], wg0s,
                                        start=True, stop=True)
            last.then_inc(logits_ready, 1)
            pe.wait_ge(gates_ready, 1)
            for t in range(QT):
                last = nc.tensor.transpose(S[0:E0, 0, t * P:(t + 1) * P], gate[:, t, :], ident)
            last.then_inc(gateT_ready, 1)
            pe.wait_ge(gateT_copied, 1)
            for t in range(QT):
                last = nc.tensor.matmul(T4[:, t // 4, (t % 4) * P:(t % 4 + 1) * P], gT[:, t * P:(t + 1) * P], b2s,
                                        start=True, stop=True)
            last.then_inc(b2_ready, 1)

            def expert_h(e, b, i):
                pe.wait_ge(ld_ew[b], 16 * i + 16)
                pe.wait_ge(h_read, e + 1)
                for ab in range(2):
                    for half in range(2):
                        n = slice(half * 512, half * 512 + 512)
                        last = nc.tensor.matmul(S[:, ab, n], ewb[:, b, ab * P:(ab + 1) * P], fT[:, n],
                                                start=True, stop=True)
                last.then_inc(h_ready, 1)

            def expert_y(e, b):
                pe.wait_ge(s_ready, e + 3)
                pe.wait_ge(y_added, e + 1)
                for t in range(QT):
                    last = nc.tensor.matmul(T4[:, t // 4, (t % 4) * P:(t % 4 + 1) * P], fs[:, t * P:(t + 1) * P],
                                            ewb[:, b, 2 * P:3 * P], start=True, stop=True)
                last.then_inc(y_ready, 1)

            expert_h(0, 0, 0)
            with pe.Fori(0, E0 // EWBUF - 1) as i:
                for b in range(EWBUF):
                    e = EWBUF * i + b
                    expert_h(e + 1, (b + 1) % EWBUF, i + (b + 1) // EWBUF)
                    expert_y(e, b)
            for b in range(EWBUF):
                e = E0 - EWBUF + b
                if b < EWBUF - 1:
                    expert_h(e + 1, b + 1, E0 // EWBUF - 1)
                expert_y(e, b)
            transposes(3, xn, S[:, 0, :])
            pe.wait_ge(w1_split, 1)
            pe.wait_ge(hatT_copied, 5)
            pe.wait_ge(v1_const, 1)

            def free_bank(n, u, early):
                if not early:
                    pe.wait_ge(proj_read, n + 1)
                elif isinstance(n, int) and n < 3:
                    pe.wait_ge(proj_read, 1)
                else:
                    pe.wait_ge(proj_read, n - 1)
                return T4[:, 3 - u if early else 3, :]

            def k1_slot(h, n, c, half, early):
                bank = free_bank(n, half, early)
                k = bass.ds(512 * c + 256 * half, 256)
                split_product(bank[:, 0:256], wk1_hi[:, h, :], wk1_lo[:, h, :], cn_hi[:, k], cn_lo[:, k])\
                    .then_inc(proj_psum, 1)

            def v1_slot(h, n, c, last, early):
                bank = free_bank(n, 2, early)
                for u in range(3 if last else 4):
                    t = bass.ds(512 * c + P * u, P)
                    o = bank[:, u * D1:(u + 1) * D1]
                    nc.tensor.matmul(o, cn_hi[:, t], wv1_hi[:, h, :], start=(u == 0), stop=False, skip_group_check=True)
                    nc.tensor.matmul(o, cn_hi[:, t], wv1_lo[:, h, :], start=False, stop=False, skip_group_check=True)
                    end = nc.tensor.matmul(o, cn_lo[:, t], wv1_hi[:, h, :], start=False, stop=True,
                                           skip_group_check=True)
                end.then_inc(proj_psum, 1)

            def q1_slot(h, n, half, early):
                bank = free_bank(n, 3, early)
                k = slice(half * 512, half * 512 + 512)
                split_product(bank, wq1_hi[:, h, :], wq1_lo[:, h, :], lat_hi[:, k], lat_lo[:, k])\
                    .then_inc(proj_psum, 1)

            def slots1(h, c, u, first=None, last=False, early=False):
                n = h * PROJ + 3 * c + (2 if first is None else first)
                if u < 2:
                    k1_slot(h, n + u, c, u, early)
                elif u == 2:
                    v1_slot(h, n + 2, c, last, early)
                elif first is not None:
                    q1_slot(h, n + 3, first, early)

            def scores1(g, u, hb, t):
                pe.wait_ge(exp_done[1], g + 1)
                for half in range(2):
                    n = slice(half * 512, half * 512 + 512)
                    k = k1[:, hb, bass.ds(P * t, P)]
                    nc.tensor.matmul(S[:, u % 2, n], k, q1_hi[:, hb, n], start=True, stop=False)
                    last = nc.tensor.matmul(S[:, u % 2, n], k, q1_lo[:, hb, n], start=False, stop=True)
                last.then_inc(scores_ready[1], 1)

            def pv1(g, u, hb, t, first):
                pe.wait_ge(low_ready[1], g + 1)
                for q in range(QT):
                    at = (q % 3) * VW
                    o = T4[:, q // 3, at:at + VW]
                    nc.tensor.matmul(o, hi(probs1[u], q), v1[hb][:, t, 0:VW], start=(first and q % 3 == 0),
                                     stop=False, skip_group_check=True)
                    last = nc.tensor.matmul(o[:, D1:VW], plow1[u % 2][:, q * P:(q + 1) * P], v1[hb][:, t, D1:VW],
                                            start=False, stop=False, skip_group_check=True)
                last.then_inc(pv_done[1], 1)

            def head1(h, hb, first_head=False, last_head=False):
                def chunk(c, first=None, last=False):
                    for u in range(4):
                        t = 4 * c + u
                        if not last_head:
                            slots1(h + 1, c, u, first, last)
                        if not last or u < 4 - AHEAD:
                            scores1(h * KT4 + t + AHEAD, u + AHEAD, hb, t + AHEAD)
                        elif not last_head:
                            pe.wait_ge(proj_done, (h + 1) * PROJ + 8 + 3)
                            scores1(h * KT4 + t + AHEAD, u + AHEAD, 1 - hb, u + AHEAD - 4)
                        if first == 0 and u == 0:
                            pe.wait_ge(proj_done, (h + 1) * PROJ + 3)
                            if not first_head:
                                pe.wait_ge(acc_copied, h)
                        pv1(h * KT4 + t, u, hb, t, first == 0 and u == 0)

                chunk(0, 0)
                chunk(1, 1)
                with pe.Fori(2, KC - 1) as c:
                    chunk(c)
                chunk(KC - 1, last=True)

            pe.sem_inc(pv_done[1], 4)
            for c in range(2):
                for u in range(4):
                    slots1(0, c, u, c, early=True)
            with pe.Fori(2, KC - 1) as c:
                for u in range(3):
                    slots1(0, c, u, early=True)
            for u in range(3):
                slots1(0, KC - 1, u, last=True, early=True)
            pe.wait_ge(proj_done, 8 + 3)
            for u in range(AHEAD):
                scores1(u, u, 0, u)
            head1(0, 0, first_head=True)
            head1(1, 1)
            with pe.Fori(1, H // 2 - 1) as pair:
                for a in range(2):
                    head1(2 * pair + a, a)
            head1(H - 2, 0)
            head1(H - 1, 1, last_head=True)
            pe.wait_ge(head_done, H + 1)
            for c in range(8):
                if c >= 2:
                    pe.wait_ge(oT_copied, c - 1)
                for t in range(QT):
                    last = nc.tensor.transpose(S[:, c % 2, t * P:(t + 1) * P], o1[:, t, c * P:(c + 1) * P], ident)
                last.then_inc(oT_ready, 1)
            pe.wait_ge(ld_end, 64)
            pe.wait_ge(oT_copied, 8)
            for t in range(QT):
                for c in range(8):
                    last = nc.tensor.matmul(T4[:, t // 4, (t % 4) * P:(t % 4 + 1) * P], oT[:, c, t * P:(t + 1) * P],
                                            wos[:, c, :], start=(c == 0), stop=(c == 7))
            last.then_inc(proj_ready, 1)
            transposes(4, xhat, S[:, 0, :])
            pe.wait_ge(hatT_copied, 6)
            for t in range(QT):
                last = nc.tensor.matmul(T4[:, 2, t * E1:(t + 1) * E1], xT1[:, t * P:(t + 1) * P], wg1s,
                                        start=True, stop=True)
            last.then_inc(logits_ready, 1)
            for t in range(QT):
                if t >= 2:
                    pe.wait_ge(ex1_added, t - 1)
                for half in range(2):
                    last = nc.tensor.matmul(S[:, t % 2, half * 512:half * 512 + 512], xT1[:, t * P:(t + 1) * P],
                                            we1s[:, half * 512:half * 512 + 512], start=True, stop=True)
                last.then_inc(ex1_ready, 1)

        @block.vector
        def _(dve):
            steps = [0]
            norms = [0]

            def step(ins):
                steps[0] += 1
                ins.then_inc(dve_step, 1)
                dve.wait_ge(dve_step, steps[0])

            def finish_stats(st, tmp, mean, var):
                step(nc.vector.tensor_tensor(mean, st[:, :, 1], st[:, :, 4], ALU.add))
                step(nc.vector.tensor_tensor(tmp, st[:, :, 1], st[:, :, 4], ALU.subtract))
                step(nc.vector.tensor_scalar(mean, mean, 0.5, None, ALU.mult))
                step(nc.vector.tensor_scalar(tmp, tmp, 0.5, None, ALU.mult))
                step(nc.vector.tensor_tensor(tmp, tmp, tmp, ALU.mult))
                step(nc.vector.tensor_tensor(var, st[:, :, 2], st[:, :, 5], ALU.add))
                step(nc.vector.tensor_scalar(var, var, 1.0 / D, EPS, ALU.mult, ALU.add))
                return nc.vector.tensor_tensor(var, var, tmp, ALU.add)

            def row_stats(src):
                for t in range(QT):
                    last = nc.vector.bn_stats(bst[:, t, :], src[:, t, :])
                step(last)

            def rsqrt_var(ins, std, out_rstd):
                norms[0] += 1
                ins.then_inc(var_ready, 1)
                dve.wait_ge(std_ready, norms[0])
                step(nc.vector.reciprocal(out_rstd, std))

            def layer_norm(src, dst, ready=None):
                row_stats(src)
                rsqrt_var(finish_stats(bst, stat[:, 0:QT], xmean, xvar), xstd, xrstd)
                for t in range(QT):
                    last = nc.vector.tensor_scalar(dst[:, t, :], src[:, t, :], xmean[:, t:t + 1], xrstd[:, t:t + 1],
                                                   ALU.subtract, ALU.mult)
                if ready:
                    last.then_inc(ready, 1)
                else:
                    step(last)

            dve.wait_ge(ld_x, 16)
            layer_norm(xres, xhat, hat_ready)
            dve.wait_ge(ld_w0, 16)
            step(nc.vector.tensor_reduce(wmax, w0f[:, 512:1024], AX.X, ALU.max, apply_absolute_value=True))
            step(nc.vector.tensor_scalar(w0f, w0f, SW, None, ALU.mult))
            step(nc.vector.tensor_copy(w0_hi, w0f))
            nc.vector.tensor_tensor(w0_lo, w0f, w0_hi, ALU.subtract).then_inc(w0_split, 1)
            dve.wait_ge(ld_mask, 32)
            nc.vector.tensor_scalar(mask_rows, mask_i, -MASKED, MASKED, ALU.mult, ALU.add)
            nc.vector.tensor_copy(msel, msel_f).then_inc(w0_split, 1)
            step(nc.vector.memset(bounds, -3.0e38))
            step(nc.vector.tensor_reduce(bounds[0:KC, 0:1], mask_rows, AX.X, ALU.max))
            dve.wait_ge(ld_b0, 32)
            dve.wait_ge(ld_cst, 16)
            nc.vector.tensor_reduce(bounds[:, 2:3], b0s[:, QUADS:2 * QUADS], AX.X, ALU.max, apply_absolute_value=True)
            for i, scale in ((0, SA / math.sqrt(W0)), (1, SA)):
                c = slice(i * QUADS, (i + 1) * QUADS)
                add = cst[:, C_ADD_Q if i == 0 else C_ADD_K:][:, 0:1]
                last = nc.vector.tensor_scalar(qkcol[:, c], b0s[:, c], scale, add, ALU.mult, ALU.add)
            step(nc.vector.tensor_scalar(ln1c, cst[:, C_LN:C_LN + 4], SA, None, ALU.mult))
            dve.wait_ge(hatT_copied, 1)
            nc.vector.scalar_tensor_tensor(out=xT_lo, in0=S[:, 0, :], scalar=SA, in1=xT_hi, op0=ALU.mult,
                                           op1=ALU.subtract).then_inc(hatT_copied, 1)
            dve.wait_ge(ld_ctx, 32)
            with dve.Fori(0, KC) as c:
                for u in range(4):
                    last = nc.vector.bn_stats(cbn[:, 4 * c + u, :], c_raw[:, 4 * c + u, :])
            step(nc.vector.memset(rec, 0.0))
            rsqrt_var(finish_stats(cbn, stat, cmean, cvar), cstd, crstd)

            def normalized(c, b):
                dve.wait_ge(tr_done, c + 1)
                for u in range(4):
                    t = 4 * c + u
                    last = nc.vector.tensor_scalar(xb[:, b, u * P:(u + 1) * P], c_raw[:, t, :], cmean[:, bass.ds(t, 1)],
                                                   crstd[:, bass.ds(t, 1)], ALU.subtract, ALU.mult)
                last.then_inc(xb_ready, 1)

            normalized(0, 0)
            with dve.Fori(0, KC // 2) as i:
                normalized(2 * i + 1, 1)
                normalized(2 * i + 2, 0)
            dve.wait_ge(ld_ctx_t, 16)
            step(nc.vector.tensor_reduce(cmax, cT, AX.X, ALU.max, apply_absolute_value=True))
            step(nc.vector.tensor_tensor(bounds[:, 1:2], wmax, cmax, ALU.mult))
            dve.sem_inc(k0_done, 4)
            dve.sem_inc(v0_done, 4)
            dve.wait_ge(cn_done, KC + 2)
            for g in range(QUADS):
                dve.wait_ge(q0_f, g + 1)
                if g:
                    dve.wait_ge(q0_done, g)
                step(nc.vector.tensor_copy(qtmp, probs[:, g % 2, :]))
                step(nc.vector.scalar_tensor_tensor(out=qtmp, in0=qtmp, scalar=cst[:, C_NLOW_Q:C_NLOW_Q + 1],
                                                    in1=probs[:, g % 2, :], op0=ALU.mult, op1=ALU.add))
                nc.vector.tensor_reduce(qbound[:, g:g + 1], qtmp, AX.X, ALU.max, apply_absolute_value=True)
                for j in range(4):
                    last = nc.vector.tensor_scalar(qz[:, 4 * g + j, :], qtmp, rowsel(j), None, ALU.mult)
                last.then_inc(q0_done, 1)
            dve.wait_ge(q0_done, QUADS)
            step(nc.vector.tensor_reduce(decide[:, 0:1], qbound, AX.X, ALU.max))
            nc.vector.tensor_scalar(bounds[:, 3:4], decide[:, 0:1], cst[:, C_VROW:C_VROW + 1], None, ALU.mult)\
                .then_inc(bounds_ready, 1)
            dve.wait_ge(boundsT_ready, 1)
            for j, (start, end, op) in enumerate(((0, KC - WINDOW, ALU.max), (KC - WINDOW, KC, ALU.max),
                                                  (P, 2 * P, ALU.add), (2 * P, 3 * P, ALU.max),
                                                  (3 * P, 4 * P, ALU.max))):
                last = nc.vector.tensor_reduce(decide[0:1, j:j + 1], S4[0:1, 0, start:end], AX.X, op)
            step(last)
            before, inside, weighted, bias, query, key, x_ok, y_ok = (decide[0:1, j:j + 1] for j in range(8))
            step(nc.vector.tensor_tensor(key, weighted, bias, ALU.add))
            step(nc.vector.tensor_tensor(key, key, query, ALU.mult))
            step(nc.vector.tensor_scalar(key, key, ENTRY_SPREAD / SA, None, ALU.is_lt))
            step(nc.vector.tensor_scalar(x_ok, before, MASKED / 2, None, ALU.is_lt))
            step(nc.vector.tensor_scalar(y_ok, inside, MASKED / 2, None, ALU.is_gt))
            step(nc.vector.tensor_tensor(x_ok, x_ok, y_ok, ALU.mult))
            nc.vector.tensor_tensor(window[0:1, :], key, x_ok, ALU.mult).then_inc(window_ready, 1)

            def attention0(C0, NC):
                dve.wait_ge(cT_hi_ready, 4)
                n = slice(512 * C0, 512 * (C0 + NC))
                nc.vector.scalar_tensor_tensor(out=cT_lo[:, n], in0=cT[:, n], scalar=SA, in1=cT_hi[:, n],
                                               op0=ALU.mult, op1=ALU.subtract).then_inc(cT_hi_ready, 1)
                dve.wait_ge(cT_hi_ready, 5)
                with dve.Fori(0, NC) as c:
                    n = bass.ds(512 * (C0 + c), 512)
                    for g in range(QUADS):
                        dve.wait_ge(k0_f, 4 * c + g + 5)
                        nc.vector.tensor_copy(ks[:, g, n], kf[:, g, :]).then_inc(k0_hi, 1)
                    for g in range(QUADS):
                        dve.wait_ge(k0_hi, 4 * c + g + 1)
                        nc.vector.scalar_tensor_tensor(out=ks[:, g, n], in0=ks[:, g, n], scalar=cst[:, C_NLOW_K:C_NLOW_K + 1],
                                                       in1=kf[:, g, :], op0=ALU.mult, op1=ALU.add).then_inc(k0_done, 1)
                    for u in range(4):
                        v = v0[:, 4 * (C0 + c) + u, :, :]
                        dve.wait_ge(v0_hi, 4 * c + u + 1)
                        nc.vector.scalar_tensor_tensor(out=v[:, :, 0:W0], in0=T4[:, u, 0:D].rearrange("p (h w) -> p h w", w=W0),
                                                       scalar=1.0 / SW, in1=v[:, :, W0:2 * W0], op0=ALU.mult,
                                                       op1=ALU.subtract).then_inc(v0_done, 1)
                dve.wait_ge(k0_done, 4 * NC + 4)
                step(nc.vector.memset(probs[:, :, :], -3.0e38))
                dve.sem_inc(mx_read, 4)
                with dve.Fori(0, H) as h:
                    with dve.Fori(0, NC) as c:
                        for k in range(4):
                            dve.wait_ge(mx_psum, (h * NC + c) * 4 + k + 1)
                            nc.vector.tensor_reduce(mp[:, c, h, 2 * k:2 * k + 2], M4[k], AX.X, ALU.max)\
                                .then_inc(mx_read, 1)
                dve.wait_ge(mx_read, 4 * NC * H + 4)
                step(nc.vector.tensor_reduce(mx, mp.rearrange("p c h q -> p (h q) c"), AX.X, ALU.max))
                step(nc.vector.memset(maxsel, 0.0))
                for n in range(8):
                    g, half = n // 2, n % 2
                    if n >= 2:
                        dve.wait_ge(maxT_ready, n - 1)
                    m = mx[:, 4 * g * QT:4 * (g + 1) * QT].rearrange("p (j q) -> p q j", j=4)[:, 4 * half:4 * half + 4, :]
                    nc.vector.tensor_scalar(maxsel[:, n % 2, :, MAX_ROW::32], m, -1.0 / SCORE, SHIFT0, ALU.mult, ALU.add)\
                        .then_inc(maxsel_ready, 1)
                    dve.wait_ge(maxT_ready, n + 1)
                    for j in range(4):
                        o = qz[:, 4 * g + j, half * 512:half * 512 + 512]
                        last = nc.vector.scalar_tensor_tensor(out=o, in0=S4[:, n % 4, :], scalar=rowsel(j), in1=o,
                                                              op0=ALU.mult, op1=ALU.add)
                    last.then_inc(maxT_read, 1)
                for a in range(2):
                    nc.vector.memset(T4[:, a, 0:QT * VW0], 0.0).then_inc(acc_zero, 1)

                def low0(g, u):
                    dve.wait_ge(exp_done[0], g + 3)
                    dve.wait_ge(pv_done[0], g + 3)
                    nc.vector.tensor_tensor(plow0[u % 2], probs0[u], probs0[u].bitcast(BF16)[:, 1::2], ALU.subtract)\
                        .then_inc(low_ready[0], 1)

                def lows0(h, c):
                    for u in range(4):
                        low0(4 * (h * NC + c) + u, u)

                def output0(h, a):
                    acc = T4[:, a, 0:QT * VW0].rearrange("p (q w) -> p q w", w=VW0)
                    o = h0[:, :, bass.ds(W0 * h, W0)]
                    dve.wait_ge(pv_done[0], (h + 1) * (4 * NC) + 4)
                    dve.wait_ge(acc_read, 5 * h + 1)
                    nc.vector.tensor_scalar(rec, acc[:, :, 2 * W0], SA, None, ALU.mult).then_inc(acc_read, 1)
                    nc.vector.tensor_copy(o, acc[:, :, 0:W0]).then_inc(acc_read, 1)
                    dve.wait_ge(acc_read, 5 * h + 3)
                    nc.vector.reciprocal(rec, rec).then_inc(acc_read, 1)
                    nc.vector.tensor_tensor(o, acc[:, :, W0:2 * W0], o, ALU.add).then_inc(acc_read, 1)
                    dve.wait_ge(acc_read, 5 * h + 5)
                    nc.vector.tensor_tensor(o, o, rec.unsqueeze(2).to_broadcast([P, QT, W0]), ALU.mult).then_inc(acc_read, 1)
                    nc.vector.memset(T4[:, a, 0:QT * VW0], 0.0).then_inc(acc_zero, 1)

                def head0(h, a, last_head=False):
                    with dve.Fori(1, NC) as c:
                        lows0(h, c)
                    if not last_head:
                        lows0(h + 1, 0)
                    output0(h, a)

                dve.sem_inc(acc_read, 1)
                lows0(0, 0)
                with dve.Fori(0, H // 2 - 1) as pair:
                    for a in range(2):
                        head0(2 * pair + a, a)
                head0(H - 2, 0)
                head0(H - 1, 1, last_head=True)

            dve.wait_ge(window_ready, 1)
            counted = steps[0]
            with dve.If(dve.value_load(window[0:1, :], min_val=0, max_val=1) > 0):
                attention0(KC - WINDOW, WINDOW)
            steps[0] = counted
            with dve.Else():
                attention0(0, KC)
            dve.wait_ge(acc_read, 5 * H + 1)
            step(nc.vector.tensor_tensor(xres[:, :, :], xres[:, :, :], h0[:, :, :], ALU.add))
            nc.vector.tensor_tensor(xres[:, :, :], xres[:, :, :], bvs.unsqueeze(1).to_broadcast([P, QT, D]), ALU.add)\
                .then_inc(attn0_done, 1)
            dve.wait_ge(attn0_done, 1)
            layer_norm(xres, xhat)
            row_stats(xhat)
            step(finish_stats(bst, stat[:, 0:QT], xmean, xvar))
            step(nc.vector.tensor_tensor(xmean, xmean, xmean, ALU.mult))
            rsqrt_var(nc.vector.tensor_tensor(xvar, xvar, xmean, ALU.add), xstd, xrstd)
            dve.wait_ge(ld_ffn0, 64)
            for t in range(QT):
                last = nc.vector.scalar_tensor_tensor(out=xn[:, t, :], in0=xhat[:, t, :], scalar=xrstd[:, t:t + 1],
                                                      in1=nscale, op0=ALU.mult, op1=ALU.mult)
            last.then_inc(hat_ready, 1)
            step(nc.vector.tensor_tensor(xres[:, :, :], xres[:, :, :], xhat[:, :, :], ALU.add))

            def ranks(src, n, rk, buf, k):
                gt = buf[:, 0:QT * n * n].rearrange("p (t e f) -> p t e f", e=n, f=n)
                eq = buf[:, QT * n * n:2 * QT * n * n].rearrange("p (t e f) -> p t e f", e=n, f=n)
                tri = cst[:, C_TRI:C_TRI + E0 * E0].rearrange("p (e f) -> p e f", e=E0)[:, 0:n, 0:n]
                for t in range(QT):
                    of = src[:, t, :].unsqueeze(1).to_broadcast([P, n, n])
                    to = src[:, t, :].unsqueeze(2).to_broadcast([P, n, n])
                    nc.vector.tensor_tensor(gt[:, t, :, :], of, to, ALU.is_gt)
                    last = nc.vector.tensor_tensor(eq[:, t, :, :], of, to, ALU.is_equal)
                step(last)
                for t in range(QT):
                    last = nc.vector.tensor_tensor(eq[:, t, :, :], eq[:, t, :, :], tri, ALU.mult)
                step(last)
                step(nc.vector.tensor_tensor(gt, gt, eq, ALU.add))
                step(nc.vector.tensor_reduce(rk, gt, AX.X, ALU.add))
                step(nc.vector.tensor_scalar(rk, rk, k - 0.5, None, ALU.is_lt))

            dve.wait_ge(logits_ready, 1)
            step(nc.vector.tensor_tensor(lg[:, :, :], T4[:, 2, 0:QT * E0].rearrange("p (t e) -> p t e", e=E0),
                                         bg0s.unsqueeze(1).to_broadcast([P, QT, E0]), ALU.add))
            ranks(lg, E0, rank, fab, TOP0)
            step(nc.vector.tensor_reduce(gmax, lg[:, :, :], AX.X, ALU.max))
            nc.vector.tensor_tensor(lg[:, :, :], lg[:, :, :], gmax.unsqueeze(2).to_broadcast([P, QT, E0]),
                                    ALU.subtract).then_inc(gmax_done, 1)
            dve.wait_ge(gexp_done, 1)
            step(nc.vector.tensor_tensor(gate[:, :, :], gate[:, :, :], rank[:, :, :], ALU.mult))
            step(nc.vector.tensor_reduce(gsum, gate[:, :, :], AX.X, ALU.add))
            step(nc.vector.reciprocal(grec, gsum))
            nc.vector.tensor_tensor(gate[:, :, :], gate[:, :, :], grec.unsqueeze(2).to_broadcast([P, QT, E0]),
                                    ALU.mult).then_inc(gates_ready, 1)
            y8 = T4[:, 0:2, :].rearrange("p b (t d) -> p (b t) d", d=D)
            dve.wait_ge(b2_ready, 1)
            step(nc.vector.tensor_tensor(xres[:, :, :], xres[:, :, :], y8, ALU.add))
            dve.sem_inc(h_read, 1)
            dve.sem_inc(y_added, 1)
            dve.sem_inc(s_ready, 2)
            dve.sem_inc(glu_done, 2)

            def expert_clips(e, b):
                dve.wait_ge(a_raw, e + 1)
                nc.vector.tensor_scalar(fa[b], fa[b], LIMIT, None, ALU.min).then_inc(a_ready, 1)
                dve.wait_ge(h_read, e + 2)
                nc.vector.tensor_scalar(fb[b], fb[b], LIMIT, -LIMIT, ALU.min, ALU.max).then_inc(b_ready, 1)

            def expert_s(e, b):
                dve.wait_ge(sig_ready, e + 1)
                nc.vector.tensor_tensor(fsig[b], fsig[b], fa[b], ALU.mult).then_inc(glu_done, 1)
                dve.wait_ge(glu_done, e + 3)
                dve.wait_ge(b_ready, e + 1)
                nc.vector.scalar_tensor_tensor(out=fs, in0=fb[b], scalar=1.0, in1=fsig[b], op0=ALU.add, op1=ALU.mult)\
                    .then_inc(s_ready, 1)

            def expert_add(e):
                dve.wait_ge(y_ready, e + 1)
                for t in range(QT):
                    last = nc.vector.scalar_tensor_tensor(out=xres[:, t, :], in0=y8[:, t, :],
                                                          scalar=gate[:, t, bass.ds(e, 1)], in1=xres[:, t, :],
                                                          op0=ALU.mult, op1=ALU.add)
                last.then_inc(y_added, 1)

            expert_clips(0, 0)
            expert_s(0, 0)
            expert_clips(1, 1)
            expert_add(0)
            expert_s(1, 1)
            with dve.Fori(1, E0 // 2) as i:
                for b in range(2):
                    e = 2 * i + b
                    expert_clips(e, b)
                    expert_add(e - 1)
                    expert_s(e, b)
            expert_add(E0 - 1)
            dve.wait_ge(y_added, E0 + 1)
            layer_norm(xres, xhat)
            layer_norm(xhat, xn, hat_ready)
            dve.wait_ge(hat_ready, 3)
            dve.wait_ge(hatT_ready, 3)
            nc.vector.memset(v1[0][:, KT - 1:KT4, :], 0.0)
            step(nc.vector.memset(v1[1][:, KT - 1:KT4, :], 0.0))
            nc.vector.memset(shift1, SHIFT1)
            for b in range(2):
                nc.vector.memset(v1[b][:, 0:KT - 1, 2 * D1:VW], 1.0)
                last = nc.vector.memset(v1[b][0:LAST, KT - 1, 2 * D1:VW], 1.0)
            last.then_inc(v1_const, 1)
            dve.wait_ge(latf_ready, 1)
            step(nc.vector.tensor_copy(lat_hi, probs[:, 0, :]))
            nc.vector.tensor_tensor(lat_lo, probs[:, 0, :], lat_hi, ALU.subtract).then_inc(hatT_copied, 2)
            dve.sem_inc(proj_read, 1)
            dve.sem_inc(head_done, 1)

            def clip(g, u):
                dve.wait_ge(exp_done[1], g + 3)
                nc.vector.tensor_scalar(probs1[u % 4], probs1[u % 4], EXP_HI, EXP_LO, ALU.min, ALU.max)\
                    .then_inc(clipped, 1)

            def low1(g, u):
                dve.wait_ge(clipped, g + 1)
                dve.wait_ge(pv_done[1], g + 3)
                nc.vector.tensor_tensor(plow1[u % 2], probs1[u], probs1[u].bitcast(BF16)[:, 1::2], ALU.subtract)\
                    .then_inc(low_ready[1], 1)

            def head1(h, first_head=False, last_head=False):
                def chunk(c, last=False):
                    for u in range(4):
                        g = h * KT4 + 4 * c + u
                        if not (last and last_head and u == 3):
                            clip(g + 1, u + 1)
                        low1(g, u)

                chunk(0)
                if not first_head:
                    reciprocals(h - 1)
                with dve.Fori(1, KC - 1) as c:
                    chunk(c)
                chunk(KC - 1, True)

            def reciprocals(h):
                dve.wait_ge(acc_copied, h + 1)
                nc.vector.tensor_scalar(rec, acc_f[:, :, 2 * D1], SA, None, ALU.mult).then_inc(acc_rec, 1)
                dve.wait_ge(acc_rec, 2 * h + 1)
                nc.vector.reciprocal(rec, rec).then_inc(acc_rec, 1)

            clip(0, 0)
            head1(0, first_head=True)
            with dve.Fori(1, H - 1) as h:
                head1(h)
            head1(H - 1, last_head=True)
            reciprocals(H - 1)
            dve.wait_ge(proj_ready, 1)
            dve.wait_ge(ld_end, 64)
            step(nc.vector.tensor_tensor(xres[:, :, :], xres[:, :, :], y8, ALU.add))
            step(nc.vector.tensor_tensor(xres[:, :, :], xres[:, :, :], bo1.unsqueeze(1).to_broadcast([P, QT, D]),
                                         ALU.add))
            layer_norm(xres, xhat, hat_ready)
            dve.wait_ge(logits_ready, 2)
            step(nc.vector.tensor_copy(lg1[:, :, :], T4[:, 2, 0:QT * E1].rearrange("p (t e) -> p t e", e=E1)))
            step(nc.vector.tensor_reduce(gmax, lg1[:, :, :], AX.X, ALU.max))
            nc.vector.tensor_tensor(lg1[:, :, :], lg1[:, :, :], gmax.unsqueeze(2).to_broadcast([P, QT, E1]),
                                    ALU.subtract).then_inc(gmax_done, 1)
            dve.wait_ge(gexp_done, 2)
            for passes in range(2):
                step(nc.vector.tensor_reduce(gsum, gate1[:, :, :], AX.X, ALU.add))
                if passes == 1:
                    step(nc.vector.tensor_scalar(gsum, gsum, 1e-9, None, ALU.add))
                step(nc.vector.reciprocal(grec, gsum))
                step(nc.vector.tensor_tensor(gate1[:, :, :], gate1[:, :, :],
                                             grec.unsqueeze(2).to_broadcast([P, QT, E1]), ALU.mult))
                if passes == 0:
                    ranks(gate1, E1, rank1, probs[:, 0, :], TOP1)
                    step(nc.vector.tensor_tensor(gate1[:, :, :], gate1[:, :, :], rank1[:, :, :], ALU.mult))
            for t in range(QT):
                dve.wait_ge(ex1_ready, t + 1)
                for e in range(E1):
                    last = nc.vector.scalar_tensor_tensor(
                        out=xres[:, t, :], in0=S[:, t % 2, e * P:(e + 1) * P], scalar=gate1[:, t, e:e + 1],
                        in1=xres[:, t, :], op0=ALU.mult, op1=ALU.add)
                    if e < E1 - 1:
                        step(last)
                last.then_inc(ex1_added, 1)
            dve.wait_ge(ex1_added, QT)
            nc.vector.memset(rec, 0.0).then_inc(out_ready, 1)


def kernel(**inputs):
    import numpy as np
    import concourse.bacc as bacc
    from concourse.bass_utils import run_bass_kernel_spmd

    a = {k: np.asarray(v) for k, v in inputs.items()}
    f32 = np.float32

    def rows0(w):
        t = np.zeros((D, H, 4, W0), f32)
        t[:, :, 0:3, :] = w.T.reshape(D, H, 1, W0)
        return t.reshape(D, H * 32)

    def col0(b):
        t = np.zeros((H, 4, W0), f32)
        t[:, 0:3, :] = b.reshape(H, 1, W0)
        return t.reshape(QUADS, P).T

    def twice(w):
        t = np.zeros((D, H, 2, D1), f32)
        t[...] = w.reshape(D, H, 1, D1)
        return t.reshape(D, H * 2 * D1)

    def bcast(v):
        return np.broadcast_to(v, (P, v.shape[-1]))

    row = np.arange(P) % 32
    cst = np.zeros((P, C_N), f32)
    cst[:, C_ID:C_ID + P] = np.eye(P)
    for j in range(4):
        cst[32 * j:32 * j + 32, C_ROWSEL + j] = 1.0
    cst[:, C_NLOW_K] = np.where((row >= 16) & (row < 24), -1.0, 0.0)
    cst[:, C_NLOW_Q] = np.where((row >= 8) & (row < 16), -1.0, 0.0)
    cst[:, C_ADD_K] = np.where(row == MAX_ROW, SCORE, 0.0)
    cst[:, C_ADD_Q] = np.where(row == MASK_ROW, SCORE, 0.0)
    cst[:, C_TRI:C_TRI + E0 * E0] = np.tril(np.ones((E0, E0)), -1).reshape(1, -1)
    for n, name in enumerate(("L1_xattn_ln_l_w", "L1_xattn_ln_l_b", "L1_xattn_ln_c_w", "L1_xattn_ln_c_b")):
        cst[:, C_LN + n] = a[name]
    cst[:, C_VROW] = row < MASK_ROW
    sel = np.zeros((KC, KC, P), f32)
    for c in range(KC):
        sel[c, c, MASK_ROW::32] = SW
    mask = np.full((KC * 512,), 1 + int(NO_KEY - 0) // 10000, np.int32)
    mask[0:SK] = a["mask_BxS2_ik0"].reshape(-1)
    ctx = a["ctx_1024"].reshape(SK, D)
    ctx_t = np.zeros((D, KPAD), f32)
    ctx_t[:, 0:SK] = ctx.T
    w1 = a["L0_ffn_w1"]
    b1 = a["L0_ffn_b1"]
    ew = np.concatenate([w1[:, :, 0::2], w1[:, :, 1::2], a["L0_ffn_w2"], b1[:, 0::2, None], b1[:, 1::2, None]], axis=2)
    arrays = {
        "x": a["x"].reshape(SQ, D),
        "ctx": ctx,
        "ctx_t": ctx_t,
        "mask": mask.reshape(KC, 512),
        "consts": cst,
        "mask_sel": sel.reshape(KC, KC * P),
        "w0": np.concatenate([rows0(a["L0_xattn_Wq"]), rows0(a["L0_xattn_Wk"]), a["L0_xattn_Wv"].T], axis=1),
        "b0": np.concatenate([col0(a["L0_xattn_bq"]), col0(a["L0_xattn_bk"])], axis=1),
        "bv0": bcast(a["L0_xattn_bv"]),
        "norm_scale": bcast(a["L0_ffn_norm_scale"]),
        "wg0": a["L0_ffn_wg"],
        "bg0": bcast(a["L0_ffn_bg"]),
        "ew0": ew,
        "b2": a["L0_ffn_b2"],
        "ln1": cst[:, C_LN:C_LN + 4],
        "w1": np.concatenate([twice(a["L1_xattn_Wkv"][:, 0:H * D1]), twice(a["L1_xattn_Wq"]),
                              a["L1_xattn_Wkv"][:, H * D1:]], axis=1),
        "wo": a["L1_xattn_Wo"].reshape(8, P, D).transpose(1, 0, 2),
        "bo": bcast(a["L1_xattn_bo"]),
        "wg1": a["L1_ffn_Wg"],
        "we1": a["L1_ffn_We"].transpose(1, 0, 2).reshape(D, E1 * D),
    }
    arrays = {k: np.ascontiguousarray(v) for k, v in arrays.items()}
    nc = bacc.Bacc("TRN2", target_bir_lowering=False, num_devices=1)
    args = {k: nc.dram_tensor(f"in_{k}", v.shape, mybir.dt.from_np(v.dtype), kind="ExternalInput").ap()
            for k, v in arrays.items()}
    out = nc.dram_tensor("out_x", (SQ, D), F32, kind="ExternalOutput").ap()
    build(nc, out=out, **args)
    r = run_bass_kernel_spmd(nc, [{f"in_{k}": v for k, v in arrays.items()}], core_ids=[0])
    return r.results[0]["out_x"].reshape(1, SQ, D)
```

```python
import math
from contextlib import ExitStack

import concourse.bass as bass
from concourse import mybir

F32 = mybir.dt.float32
F16 = mybir.dt.float16
BF16 = mybir.dt.bfloat16
I32 = mybir.dt.int32
ALU = mybir.AluOpType
ACT = mybir.ActivationFunctionType
AX = mybir.AxisListType

P = 128
SQ = 1024
QT = SQ // P
SK = 6404
KT = -(-SK // P)
KC = -(-SK // 512)
KT4 = 4 * KC
KPAD = KT4 * P
LAST = SK - (KT - 1) * P
D = 128
H = 16
W0 = 8
QUADS = H // 4
D1 = 64
VW = 2 * D1 + 1
VW0 = 2 * W0 + 1
SHIFT0 = 5.5
SHIFT1 = 5.5
E0 = 16
TOP0 = 4
E1 = 8
TOP1 = 2
EPS = 1e-5
LIMIT = 7.0
ALPHA = 1.702
MASKED = -10000.0
NO_KEY = -30000.0
CLIP = 11.0

SA = 16.0
SW = 256.0
SCORE = SA * SA
MASK_ROW = 24
MAX_ROW = 25

EXP_HI = math.exp(CLIP + SHIFT1)
EXP_LO = math.exp(-CLIP + SHIFT1)

WINDOW = 4
SPREAD = -MASKED - 200.0
ENTRY_SPREAD = 0.98 * SPREAD / 2 * SCORE / W0

C_ID = 0
C_ROWSEL = C_ID + P
C_NLOW_K = C_ROWSEL + 4
C_NLOW_Q = C_NLOW_K + 1
C_ADD_K = C_NLOW_Q + 1
C_ADD_Q = C_ADD_K + 1
C_MASKROW = C_ADD_Q + 1
C_TRI = C_MASKROW
C_LN = C_TRI + E0 * E0
C_VROW = C_LN + 4
C_N = C_VROW + 1
EW = 3 * P + 2
EWBUF = 4
COPIED = 3
ARENA = 39984
W1_AT = 18240
PROJ = 3 * KC + 2

assert KT == KT4 - 1
AHEAD = 3


def build(nc, x, ctx, ctx_t, mask, consts, mask_sel, w0, b0, bv0, norm_scale, wg0, bg0, ew0, b2,
          ln1, w1, wo, bo, wg1, we1, out):
    with ExitStack() as stack:
        def sb(name, shape, dt):
            return stack.enter_context(nc.sbuf_tensor(name, shape, dt))

        def psum(name, shape, dt):
            return stack.enter_context(nc.psum_tensor(name, shape, dt))

        def sem(name):
            return stack.enter_context(nc.semaphore(name))

        cst = sb("cst", [P, C_N], F32)
        cn_hi = sb("cn_hi", [P, KPAD], F16)
        cn_lo = sb("cn_lo", [P, KPAD], F16)
        probs = sb("probs", [P, 2, SQ], F32)
        xres = sb("xres", [P, QT, D], F32)
        xhat = sb("xhat", [P, QT, D], F32)
        small = sb("small", [P, 1792], F32)
        arena = sb("arena", [P, ARENA], F32)

        class Region:

            def __init__(self, of, at=0):
                self.of, self.at = of, at

            def take(self, n, dt=F32):
                words = n if dt in (F32, I32) else -(-n // 2)
                v = self.of[:, self.at:self.at + words]
                self.at += words
                return v if dt == F32 else v.bitcast(dt)

        r = Region(arena)
        cT_hi = r.take(KPAD, F16)
        cT_lo = r.take(KPAD, F16)
        v0_at = r.at
        v0 = r.take(KT4 * H * (VW0 + 1), F16).rearrange("p (t h w) -> p t h w", h=H, w=VW0 + 1)
        w0_hi = r.take(2 * 512 + D, F16)
        w0_lo = r.take(2 * 512 + D, F16)
        xT_hi = r.take(SQ, F16)
        xT_lo = r.take(SQ, F16)
        msel = r.take(KC * P, F16)[0:KC, :]
        mask_rows = r.take(512, F16)[0:KC, :]
        qz_at = r.at
        qz = r.take(H * SQ, F16).rearrange("p (h n) -> p h n", h=H)
        ks_at = r.at
        ks = r.take(QUADS * KPAD, F16).rearrange("p (g n) -> p g n", g=QUADS)
        assert r.at <= ARENA
        r = Region(arena, ks_at)
        c_raw = r.take(KT4 * D).rearrange("p (t d) -> p t d", d=D)
        cT = r.take(KPAD)
        r = Region(arena, qz_at)
        xb = r.take(2 * 512).rearrange("p (b n) -> p b n", b=2)
        yf = r.take(2 * 512).rearrange("p (b n) -> p b n", b=2)
        cbn = r.take(KT4 * 6).rearrange("p (t s) -> p t s", s=6)
        r = Region(arena, v0_at)
        mask_i = r.take(512, I32)[0:KC, :]
        msel_f = r.take(KC * P)[0:KC, :]
        r = Region(arena)
        probs0 = [probs[:, 0, :], probs[:, 1, :], r.take(SQ), r.take(SQ)]
        plow0 = [r.take(SQ, F16), r.take(SQ, F16)]
        sums0 = r.take(H * QT * VW0)
        assert r.at <= v0_at
        w0f = probs[:, :, :].rearrange("p b n -> p (b n)")[:, 0:2 * 512 + D]
        kf = probs[:, :, :].rearrange("p b (c n) -> p (b c) n", n=512)
        qtmp = xhat[:, 0:4, :].rearrange("p t d -> p (t d)").bitcast(F16)
        mp = probs[:, :, :].rearrange("p b n -> p (b n)")[:, 0:KC * H * 2].rearrange(
            "p (c h q) -> p c h q", h=H, q=2)
        r = Region(arena)
        mstage = r.take(COPIED * SQ, F16).rearrange("p (k n) -> p k n", k=COPIED)
        mtop = [r.take(COPIED * SQ, F16).rearrange("p (k n) -> p k n", k=COPIED) for _ in range(2)]
        maxsel = xhat[:, :, :].rearrange("p (b t) d -> p b t d", b=2)
        h0 = xhat
        r = Region(arena)
        fT = r.take(SQ)
        ewb = r.take(EWBUF * EW).rearrange("p (b n) -> p b n", b=EWBUF)
        fab = r.take(7 * SQ)
        fa, fb, fsig = ([fab[:, (2 * i + j) * SQ:(2 * i + j + 1) * SQ] for j in range(2)] for i in range(3))
        fs = fab[:, 6 * SQ:7 * SQ]
        xn = r.take(QT * D).rearrange("p (t d) -> p t d", d=D)
        gT = r.take(SQ)[0:E0, :]
        b2s = r.take(D)[0:E0, :]
        nscale = r.take(D)
        wg0s = r.take(E0)
        bg0s = r.take(E0)
        bos = r.take(D)
        assert r.at <= W1_AT
        r = Region(arena, W1_AT)
        w1_hi = r.take(2 * H * P + H * D1, F16)
        w1_lo = r.take(2 * H * P + H * D1, F16)
        w1f_at = r.at
        w1f = r.take(2 * H * P + H * D1)
        r = Region(arena, w1f_at)
        wos = r.take(8 * D).rearrange("p (c n) -> p c n", c=8)
        we1s = r.take(E1 * D)
        xT1 = r.take(SQ)
        bo1 = r.take(D)
        wg1s = r.take(E1)
        r = Region(arena, w1f_at + 2 * H * P + H * D1)
        lat_hi = r.take(SQ, F16)
        lat_lo = r.take(SQ, F16)
        q1_hi = r.take(2 * SQ, F16).rearrange("p (b n) -> p b n", b=2)
        q1_lo = r.take(2 * SQ, F16).rearrange("p (b n) -> p b n", b=2)
        v1b = r.take(KT4 * (VW + 1), F16).rearrange("p (t w) -> p t w", w=VW + 1)
        probs1 = [probs[:, 0, :], probs[:, 1, :], r.take(SQ), r.take(SQ)]
        proj_f = r.take(4 * 256).rearrange("p (b n) -> p b n", b=4)
        acc_f = r.take(QT * VW).rearrange("p (q w) -> p q w", w=VW)
        acc_s = r.take(QT * D1).rearrange("p (q w) -> p q w", w=D1)
        assert r.at <= ARENA, r.at
        plow1 = [xhat[:, 4 * b:4 * b + 4, :].rearrange("p t d -> p (t d)").bitcast(F16) for b in range(2)]
        r = Region(arena)
        k1 = r.take(2 * KPAD, F16).rearrange("p (b n) -> p b n", b=2)
        v1a = r.take(KT4 * (VW + 1), F16).rearrange("p (t w) -> p t w", w=VW + 1)
        o1 = r.take(QT * H * D1).rearrange("p (t n) -> p t n", t=QT)
        assert r.at <= W1_AT, r.at
        v1 = [v1a, v1b]
        oT = arena[:, 0:8 * SQ].rearrange("p (c n) -> p c n", c=8)
        wk1_hi, wk1_lo = (w[:, 0:H * P].rearrange("p (h n) -> p h n", h=H) for w in (w1_hi, w1_lo))
        wq1_hi, wq1_lo = (w[:, H * P:2 * H * P].rearrange("p (h n) -> p h n", h=H) for w in (w1_hi, w1_lo))
        wv1_hi, wv1_lo = (w[:, 2 * H * P:].rearrange("p (h n) -> p h n", h=H) for w in (w1_hi, w1_lo))

        r = Region(small)
        b0s = r.take(2 * QUADS)
        qkcol = r.take(2 * QUADS)
        bst = r.take(QT * 6).rearrange("p (t s) -> p t s", s=6)
        xmean = r.take(QT)
        xvar = r.take(QT)
        xstd = r.take(QT)
        xrstd = r.take(QT)
        stat = r.take(KT4)
        cmean = r.take(KT4)
        cvar = r.take(KT4)
        cstd = r.take(KT4)
        crstd = r.take(KT4)
        mx = r.take(H * QT)
        rec = r.take(QT)
        shift1 = r.take(1)
        gate = r.take(QT * E0).rearrange("p (t e) -> p t e", e=E0)
        lg = r.take(QT * E0).rearrange("p (t e) -> p t e", e=E0)
        rank = r.take(QT * E0).rearrange("p (t e) -> p t e", e=E0)
        gmax = r.take(QT)
        gsum = r.take(QT)
        grec = r.take(QT)
        bvs = r.take(D)
        ln1s = r.take(4)
        ln1c = r.take(4)
        gate1 = r.take(QT * E1).rearrange("p (t e) -> p t e", e=E1)
        lg1 = r.take(QT * E1).rearrange("p (t e) -> p t e", e=E1)
        rank1 = r.take(QT * E1).rearrange("p (t e) -> p t e", e=E1)
        qbound = r.take(QUADS)
        wmax = r.take(1)
        cmax = r.take(1)
        bounds = r.take(4)
        decide = r.take(8)
        window = r.take(1, I32)
        assert r.at <= 1792, r.at

        ident = cst[:, C_ID:C_ID + P]

        def rowsel(j):
            return cst[:, C_ROWSEL + j:C_ROWSEL + j + 1]

        S = psum("S", [P, 2, SQ], F32)
        A = psum("A", [P, 4, 512], F32)
        S4 = S[:, :, :].rearrange("p b (c n) -> p (b c) n", n=512)
        T4 = A[:, :, :]
        M4 = [S4[:, 0:2, :], S4[:, 2:4, :], T4[:, 0:2, :], T4[:, 2:4, :]]

        ld_cst = sem("ld_cst")
        ld_x = sem("ld_x")
        ld_ctx = sem("ld_ctx")
        ld_ctx_t = sem("ld_ctx_t")
        ld_mask = sem("ld_mask")
        ld_w0 = sem("ld_w0")
        ld_b0 = sem("ld_b0")
        ld_ffn0 = sem("ld_ffn0")
        ld_ew = [sem(f"ld_ew{b}") for b in range(EWBUF)]
        ld_w1 = sem("ld_w1")
        ld_end = sem("ld_end")
        stored = sem("stored")
        raw_zeroed = sem("raw_zeroed")
        dve_step = sem("dve_step")
        pool_step = sem("pool_step")
        w0_split = sem("w0_split")
        var_ready = sem("var_ready")
        std_ready = sem("std_ready")
        hat_ready = sem("hat_ready")
        hatT_ready = sem("hatT_ready")
        hatT_copied = sem("hatT_copied")
        latf_ready = sem("latf_ready")
        cT_hi_ready = sem("cT_hi_ready")
        xb_ready = sem("xb_ready")
        tr_done = sem("tr_done")
        yf_ready = sem("yf_ready")
        cn_done = sem("cn_done")
        k0_psum = sem("k0_psum")
        k0_f = sem("k0_f")
        k0_hi = sem("k0_hi")
        k0_done = sem("k0_done")
        v0_psum = sem("v0_psum")
        v0_done = sem("v0_done")
        v0_hi = sem("v0_hi")
        v0_ones = sem("v0_ones")
        q0_psum = sem("q0_psum")
        q0_f = sem("q0_f")
        q0_done = sem("q0_done")
        bounds_ready = sem("bounds_ready")
        boundsT_ready = sem("boundsT_ready")
        window_ready = sem("window_ready")
        mx_psum = sem("mx_psum")
        mx_read = sem("mx_read")
        mx_copied = sem("mx_copied")
        mx_folded = sem("mx_folded")
        mx_top = sem("mx_top")
        maxsel_ready = sem("maxsel_ready")
        maxT_ready = sem("maxT_ready")
        maxT_read = sem("maxT_read")
        scores_ready = [sem("scores_ready0"), sem("scores_ready1")]
        exp_done = [sem("exp_done0"), sem("exp_done1")]
        clipped = sem("clipped")
        low_ready = [sem("low_ready0"), sem("low_ready1")]
        pv_done = [sem("pv_done0"), sem("pv_done1")]
        acc_zero = sem("acc_zero")
        sums0_copied = sem("sums0_copied")
        acc_copied = sem("acc_copied")
        acc_rec = sem("acc_rec")
        acc_summed = sem("acc_summed")
        head_done = sem("head_done")
        v1_last = sem("v1_last")
        w1_split = sem("w1_split")
        v1_const = sem("v1_const")
        proj_psum = sem("proj_psum")
        proj_hi = sem("proj_hi")
        proj_read = sem("proj_read")
        proj_done = sem("proj_done")
        logits_ready = sem("logits_ready")
        gmax_done = sem("gmax_done")
        gexp_done = sem("gexp_done")
        gates_ready = sem("gates_ready")
        gateT_ready = sem("gateT_ready")
        gateT_copied = sem("gateT_copied")
        b2_ready = sem("b2_ready")
        ffn_base = sem("ffn_base")
        h_ready = sem("h_ready")
        a_raw = sem("a_raw")
        a_ready = sem("a_ready")
        b_ready = sem("b_ready")
        h_read = sem("h_read")
        sig_ready = sem("sig_ready")
        glu_done = sem("glu_done")
        s_ready = sem("s_ready")
        y_ready = sem("y_ready")
        y_added = sem("y_added")
        x2_ready = sem("x2_ready")
        oT_ready = sem("oT_ready")
        oT_copied = sem("oT_copied")
        proj_ready = sem("proj_ready")
        ex1_ready = sem("ex1_ready")
        ex1_added = sem("ex1_added")
        out_ready = sem("out_ready")
        attn0_done = sem("attn0_done")

        PIECE = KPAD // 4
        block = stack.enter_context(nc.Block())

        @block.sync
        def _(sp):
            sp.dma_start(cst[:, :], consts).then_inc(ld_cst, 16)
            sp.dma_start(xres[:, :, :], x.rearrange("(t p) d -> p t d", p=P)).then_inc(ld_x, 16)
            full = (KT - 1) * P
            sp.dma_start(c_raw[:, 0:KT - 1, :], ctx[0:full, :].rearrange("(t p) d -> p t d", p=P)).then_inc(ld_ctx, 16)
            sp.wait_ge(raw_zeroed, 1)
            sp.dma_start(c_raw[0:LAST, KT - 1, :], ctx[full:SK, :]).then_inc(ld_ctx, 16)
            sp.wait_ge(attn0_done, 1)
            for dst, src in ((b2s, b2), (nscale, norm_scale), (wg0s, wg0), (bg0s, bg0)):
                sp.dma_start(dst, src).then_inc(ld_ffn0, 16)
            for b in range(EWBUF):
                sp.dma_start(ewb[:, b, :], ew0[b, :, :]).then_inc(ld_ew[b], 16)
            sp.dma_start(w1f, w1).then_inc(ld_w1, 16)
            sp.dma_start(ln1s, ln1).then_inc(ld_w1, 16)
            with sp.Fori(0, E0 // EWBUF - 1) as i:
                for b in range(EWBUF):
                    sp.wait_ge(y_ready, EWBUF * i + b + 1)
                    sp.dma_start(ewb[:, b, :], ew0[EWBUF * i + EWBUF + b, :, :]).then_inc(ld_ew[b], 16)
            sp.wait_ge(w1_split, 1)
            for dst, src in ((wos, wo), (we1s, we1), (bo1, bo), (wg1s, wg1)):
                sp.dma_start(dst, src).then_inc(ld_end, 16)
            sp.wait_ge(out_ready, 1)
            sp.dma_start(out.rearrange("(t p) d -> p t d", p=P), xres[:, :, :]).then_inc(stored, 16)
            sp.wait_ge(stored, 16)

        @block.gpsimd
        def _(pool):
            steps = [0]

            def step(ins):
                steps[0] += 1
                ins.then_inc(pool_step, 1)
                pool.wait_ge(pool_step, steps[0])

            nc.gpsimd.memset(c_raw[:, KT - 1:KT4, :], 0.0).then_inc(raw_zeroed, 1)
            pool.sem_inc(cn_done, 2)

            def cn_low(c, b):
                n = bass.ds(512 * c, 512)
                pool.wait_ge(yf_ready, c + 3)
                pool.wait_ge(cn_done, c + 2)
                nc.gpsimd.tensor_tensor(cn_lo[:, n], yf[:, b, :], cn_hi[:, n], ALU.subtract).then_inc(cn_done, 1)

            with pool.Fori(0, KC // 2) as i:
                for b in range(2):
                    cn_low(2 * i + b, b)
            cn_low(KC - 1, 0)
            pool.wait_ge(w0_split, 2)
            nc.gpsimd.memset(v0[:, :, :, 2 * W0:VW0], 1.0).then_inc(v0_ones, 1)
            pool.wait_ge(ld_w1, 32)
            step(nc.gpsimd.tensor_scalar(w1f, w1f, SW, None, ALU.mult))
            step(nc.gpsimd.tensor_copy(w1_hi, w1f))
            nc.gpsimd.tensor_tensor(w1_lo, w1f, w1_hi, ALU.subtract).then_inc(w1_split, 1)

            def low(n, o, f, h):
                pool.wait_ge(proj_done, n + 3)
                pool.wait_ge(proj_read, n + 2)
                nc.gpsimd.tensor_tensor(o, f, h, ALU.subtract).then_inc(proj_done, 1)

            def slots1(h, b, c, u, first=None, last=False):
                n = h * PROJ + 3 * c + (2 if first is None else first)
                flat = proj_f.rearrange("p b n -> p (b n)")
                if u < 2:
                    k = k1[D1:P, b, bass.ds(512 * c + 256 * u, 256)]
                    low(n + u, k, proj_f[D1:P, u, :], k)
                elif u == 2 and not last:
                    v = v1[b][:, bass.ds(4 * c, 4), :]
                    low(n + 2, v[:, :, 0:D1], proj_f[:, 2, :].rearrange("p (t w) -> p t w", w=D1), v[:, :, D1:2 * D1])
                elif u == 2:
                    v = v1[b][:, 4 * c:4 * c + 2, :]
                    pool.wait_ge(proj_done, n + 5)
                    pool.wait_ge(proj_read, n + 4)
                    nc.gpsimd.tensor_tensor(v[:, :, 0:D1], proj_f[:, 2, 0:2 * D1].rearrange("p (t w) -> p t w", w=D1),
                                            v[:, :, D1:2 * D1], ALU.subtract).then_inc(v1_last, 1)
                    pool.wait_ge(v1_last, h)
                    v = v1[b][0:LAST, 4 * c + 2, :]
                    nc.gpsimd.tensor_tensor(v[:, 0:D1], proj_f[0:LAST, 2, 2 * D1:3 * D1], v[:, D1:2 * D1],
                                            ALU.subtract).then_inc(proj_done, 1)
                elif first is not None:
                    q = slice(first * 512, first * 512 + 512)
                    low(n + 3, q1_lo[:, b, q], flat[:, 0:512], q1_hi[:, b, q])

            def output1(h):
                if isinstance(h, int) and h >= H - 2:
                    pool.wait_ge(proj_done, H * PROJ + 3)
                    pool.wait_ge(head_done, h + 1)
                else:
                    pool.wait_ge(proj_done, (h + 2) * PROJ + 8 + 3)
                pool.wait_ge(acc_copied, h + 1)
                nc.gpsimd.tensor_tensor(acc_s, acc_f[:, :, 0:D1], acc_f[:, :, D1:2 * D1], ALU.add)\
                    .then_inc(acc_summed, 1)
                pool.wait_ge(acc_summed, h + 1)
                pool.wait_ge(acc_rec, 2 * h + 2)
                nc.gpsimd.tensor_tensor(o1[:, :, bass.ds(D1 * h, D1)], acc_s,
                                        rec.unsqueeze(2).to_broadcast([P, QT, D1]), ALU.mult).then_inc(head_done, 1)

            def projections1(h, b, out_head=None):
                for c in range(2):
                    for u in range(4):
                        slots1(h, b, c, u, c)
                if out_head is not None:
                    output1(out_head)
                with pool.Fori(2, KC - 1) as c:
                    for u in range(3):
                        if u == 0 and out_head is not None:
                            pool.wait_ge(head_done, out_head + 2)
                        slots1(h, b, c, u)
                for u in range(3):
                    slots1(h, b, KC - 1, u, last=True)

            projections1(1, 1)
            projections1(2, 0, 0)
            with pool.Fori(1, H // 2 - 1) as pair:
                projections1(2 * pair + 1, 1, 2 * pair - 1)
                projections1(2 * pair + 2, 0, 2 * pair)
            projections1(H - 1, 1, H - 3)
            output1(H - 2)
            output1(H - 1)

        def act_sqrt(act, n, std, var):
            act.wait_ge(var_ready, n)
            nc.scalar.activation(std, var, ACT.Sqrt).then_inc(std_ready, 1)

        @block.scalar
        def _(act):
            for dst, src, s in ((w0f, w0, ld_w0), (b0s, b0, ld_b0), (bvs, bv0, ld_b0),
                                (mask_i, mask, ld_mask), (msel_f, mask_sel, ld_mask), (cT, ctx_t, ld_ctx_t)):
                act.dma_start(dst, src).then_inc(s, 16)
            act_sqrt(act, 1, xstd, xvar)
            act.wait_ge(hatT_ready, 1)
            nc.scalar.activation(xT_hi, S[:, 0, :], ACT.Copy, scale=SA).then_inc(hatT_copied, 1)
            act.wait_ge(ld_ctx_t, 16)
            for i in range(4):
                nc.scalar.activation(cT_hi[:, i * PIECE:(i + 1) * PIECE], cT[:, i * PIECE:(i + 1) * PIECE],
                                     ACT.Copy, scale=SA).then_inc(cT_hi_ready, 1)
            act_sqrt(act, 2, cstd, cvar)
            act.sem_inc(yf_ready, 2)

            def scaled(c, b):
                act.wait_ge(tr_done, c + 3)
                act.wait_ge(cn_done, c + 1)
                nc.scalar.activation(cn_hi[:, bass.ds(512 * c, 512)], S4[:, b, :], ACT.Identity, bias=ln1c[:, 3:4],
                                     scale=ln1c[:, 2:3])
                nc.scalar.activation(yf[:, b, :], S4[:, b, :], ACT.Identity, bias=ln1c[:, 3:4],
                                     scale=ln1c[:, 2:3]).then_inc(yf_ready, 1)

            with act.Fori(0, KC // 2) as i:
                for b in range(2):
                    scaled(2 * i + b, b)
            scaled(KC - 1, 0)
            for g in range(QUADS):
                act.wait_ge(q0_psum, g + 1)
                if g >= 2:
                    act.wait_ge(q0_done, g - 1)
                nc.scalar.activation(probs[:, g % 2, :], S[:, g % 2, :], ACT.Identity, bias=qkcol[:, g:g + 1],
                                     scale=SA / (SA * SW * math.sqrt(W0))).then_inc(q0_f, 1)
            act.sem_inc(k0_f, 4)
            act.sem_inc(exp_done[0], 2)

            def attention0(C0, NC):
                with act.Fori(0, NC) as c:
                    for g in range(QUADS):
                        act.wait_ge(k0_psum, 4 * c + g + 1)
                        act.wait_ge(k0_done, 4 * c + g + 1)
                        nc.scalar.activation(kf[:, g, :], S4[:, g, :], ACT.Identity, bias=qkcol[:, QUADS + g:QUADS + g + 1],
                                             scale=1.0 / SW).then_inc(k0_f, 1)
                    for u in range(4):
                        act.wait_ge(v0_psum, 4 * c + u + 1)
                        nc.scalar.activation(v0[:, 4 * (C0 + c) + u, :, W0:2 * W0],
                                             T4[:, u, 0:D].rearrange("p (h w) -> p h w", w=W0),
                                             ACT.Copy, scale=1.0 / SW).then_inc(v0_hi, 1)
                nc.scalar.preload_act_table(ACT.Exp)
                act.sem_inc(mx_copied, COPIED)

                def copied(h, c, k, dst):
                    act.wait_ge(mx_psum, (h * NC + c) * 4 + k + 1)
                    nc.scalar.activation(dst[:, k, :], M4[k].rearrange("p m n -> p (m n)"), ACT.Copy,
                                         scale=1.0 / SCORE).then_inc(mx_copied, 1)

                with act.Fori(0, H // 2) as pair:
                    for a in range(2):
                        h = 2 * pair + a
                        act.wait_ge(mx_top, 2 * h + 2)
                        for k in range(COPIED):
                            copied(h, 0, k, mtop[a])
                        with act.Fori(1, NC) as c:
                            for k in range(COPIED):
                                act.wait_ge(mx_folded, (h * (NC - 1) + c - 1) * COPIED + k + 1)
                                copied(h, c, k, mstage)
                act.wait_ge(maxT_read, 8)

                def exps0(h, c, last_chunk=False):
                    for u in range(3 if last_chunk else 4):
                        g = 4 * (h * NC + c) + u
                        act.wait_ge(scores_ready[0], g + 1)
                        act.wait_ge(pv_done[0], g + 1)
                        nc.scalar.activation(probs0[u], S[:, u % 2, :], ACT.Exp, scale=1.0 / SCORE)\
                            .then_inc(exp_done[0], 2 if last_chunk and u == 2 else 1)

                def copy_sums0(h, a):
                    act.wait_ge(pv_done[0], (h + 1) * (4 * NC) + 4)
                    nc.scalar.copy(sums0[:, bass.ds(QT * VW0 * h, QT * VW0)], T4[:, a, 0:QT * VW0])\
                        .then_inc(sums0_copied, 1)

                def head0(h, a, last_head=False):
                    with act.Fori(1, NC - 1) as c:
                        exps0(h, c)
                    exps0(h, NC - 1, last_chunk=True)
                    if not last_head:
                        exps0(h + 1, 0)
                    copy_sums0(h, a)

                exps0(0, 0)
                with act.Fori(0, H // 2 - 1) as pair:
                    for a in range(2):
                        head0(2 * pair + a, a)
                head0(H - 2, 0)
                head0(H - 1, 1, last_head=True)

            act.wait_ge(q0_done, QUADS)
            act.wait_ge(window_ready, 1)
            with act.If(act.value_load(window[0:1, :], min_val=0, max_val=1) > 0):
                attention0(KC - WINDOW, WINDOW)
            with act.Else():
                attention0(0, KC)
            act_sqrt(act, 3, xstd, xvar)
            act_sqrt(act, 4, xstd, xvar)
            act.wait_ge(hatT_ready, 2)
            nc.scalar.copy(fT, S[:, 0, :]).then_inc(hatT_copied, 1)

            def expert_ab(e, b):
                act.wait_ge(h_ready, e + 1)
                act.wait_ge(glu_done, e + 1)
                nc.scalar.activation(fa[b % 2], S[:, 0, :], ACT.Identity, bias=ewb[:, b, 3 * P:3 * P + 1])\
                    .then_inc(a_raw, 1)
                act.wait_ge(s_ready, e + 1)
                nc.scalar.activation(fb[b % 2], S[:, 1, :], ACT.Identity, bias=ewb[:, b, 3 * P + 1:3 * P + 2])\
                    .then_inc(h_read, 1)

            def expert_sig(e, b):
                act.wait_ge(a_ready, e + 1)
                nc.scalar.activation(fsig[b % 2], fa[b % 2], ACT.Sigmoid, scale=ALPHA).then_inc(sig_ready, 1)

            expert_ab(0, 0)
            act.wait_ge(gmax_done, 1)
            nc.scalar.activation(gate[:, :, :], lg[:, :, :], ACT.Exp).then_inc(gexp_done, 1)
            act.wait_ge(gateT_ready, 1)
            nc.scalar.copy(gT, T4[0:E0, 2:4, :].rearrange("p b n -> p (b n)")).then_inc(gateT_copied, 1)
            nc.scalar.preload_act_table(ACT.Sigmoid)
            expert_sig(0, 0)
            for b in range(1, EWBUF):
                expert_ab(b, b)
                expert_sig(b, b)
            with act.Fori(1, E0 // EWBUF) as i:
                for b in range(EWBUF):
                    expert_ab(EWBUF * i + b, b)
                    expert_sig(EWBUF * i + b, b)
            act_sqrt(act, 5, xstd, xvar)
            act_sqrt(act, 6, xstd, xvar)
            act.wait_ge(hatT_ready, 3)
            nc.scalar.activation(probs[:, 0, :], S[:, 0, :], ACT.Identity, bias=ln1c[:, 1:2],
                                 scale=ln1c[:, 0:1]).then_inc(latf_ready, 1)
            nc.scalar.preload_act_table(ACT.Exp)

            def evacuate(n, out_hi, scale, width, at, no_tile=False):
                act.wait_ge(proj_psum, n + 1)
                src = T4[:, 3, 0:width]
                f = proj_f.rearrange("p b n -> p (b n)")[:, at:at + width]
                high = nc.scalar.activation(out_hi, src if len(out_hi.shape) == 2 else src.rearrange(
                    "p (t w) -> p t w", w=D1), ACT.Copy, scale=scale)
                if no_tile:
                    high.then_inc(exp_done[1], 1)
                nc.scalar.activation(f, src, ACT.Copy, scale=scale).then_inc(proj_read, 1)

            def k1_slot(n, c, half, b, no_tile):
                act.wait_ge(proj_done, n + 3 - half)
                evacuate(n, k1[:, b, bass.ds(512 * c + 256 * half, 256)], 1.0 / SW, 256, 256 * half,
                         no_tile)

            def v1_slot(n, c, b, last):
                act.wait_ge(proj_done, n + 1)
                if not last:
                    evacuate(n, v1[b][:, bass.ds(4 * c, 4), D1:2 * D1], 1.0 / SW, 4 * D1, 512)
                    return
                act.wait_ge(proj_psum, n + 1)
                o = v1[b]
                nc.scalar.activation(o[:, 4 * c:4 * c + 2, D1:2 * D1], T4[:, 3, 0:2 * D1].rearrange(
                    "p (t w) -> p t w", w=D1), ACT.Copy, scale=1.0 / SW)
                nc.scalar.activation(o[0:LAST, 4 * c + 2, D1:2 * D1], T4[0:LAST, 3, 2 * D1:3 * D1], ACT.Copy,
                                     scale=1.0 / SW).then_inc(proj_hi, 1)
                nc.scalar.activation(proj_f[:, 2, 0:3 * D1], T4[:, 3, 0:3 * D1], ACT.Copy,
                                     scale=1.0 / SW).then_inc(proj_read, 1)

            def q1_slot(n, half, b):
                act.wait_ge(proj_done, n + 3)
                evacuate(n, q1_hi[:, b, half * 512:half * 512 + 512], 1.0 / SW, 512, 0)

            def slots1(h, b, c, u, first=None, last=False):
                n = h * PROJ + 3 * c + (2 if first is None else first)
                if u < 2:
                    k1_slot(n + u, c, u, b, last and u == 0)
                elif u == 2:
                    v1_slot(n + 2, c, b, last)
                elif first is not None:
                    q1_slot(n + 3, first, b)

            def exp1(g, u):
                act.wait_ge(scores_ready[1], g + 1)
                act.wait_ge(pv_done[1], g + 1)
                nc.scalar.activation(probs1[u % 4], S[:, u % 2, :], ACT.Exp, bias=shift1,
                                     scale=1.0 / (SCORE * math.sqrt(D1))).then_inc(exp_done[1], 1)

            def copy_sums(h):
                act.wait_ge(pv_done[1], (h + 1) * KT4 + 4)
                act.wait_ge(head_done, h + 1)
                for k in range(3):
                    q = slice(3 * k, min(3 * k + 3, QT))
                    w = (q.stop - q.start) * VW
                    last = nc.scalar.copy(acc_f[:, q, :], T4[:, k, 0:w].rearrange("p (q w) -> p q w", w=VW))
                last.then_inc(acc_copied, 1)

            def head1(h, hb, last_head=False):
                def chunk(c, first=None, last=False):
                    for u in range(4):
                        if not last_head:
                            slots1(h + 1, 1 - hb, c, u, first, last)
                        if last and u == 3:
                            copy_sums(h)
                        if not last or (u >= 4 - AHEAD and not last_head):
                            exp1(h * KT4 + 4 * c + u + AHEAD, u + AHEAD)

                chunk(0, 0)
                chunk(1, 1)
                with act.Fori(2, KC - 1) as c:
                    chunk(c)
                chunk(KC - 1, last=True)

            act.sem_inc(exp_done[1], 2)
            act.wait_ge(v1_const, 1)
            def early1(c, u, first=None, last=False):
                n = 3 * c + (2 if first is None else first) + u
                src = T4[:, 3 - u, :]
                k = k1[:, 0, bass.ds(512 * c + 256 * (u % 2), 256)]
                tiles = slice(4 * c, 4 * c + 2) if last else bass.ds(4 * c, 4)
                v = v1[0][:, tiles, :]
                act.wait_ge(proj_psum, n + 1)
                if u < 2:
                    end = nc.scalar.activation(k, src[:, 0:256], ACT.Copy, scale=1.0 / SW)
                elif u == 2:
                    w = (2 if last else 4) * D1
                    end = nc.scalar.activation(v[:, :, D1:2 * D1], src[:, 0:w].rearrange("p (t w) -> p t w", w=D1), ACT.Copy,
                                               scale=1.0 / SW)
                    if last:
                        v = v1[0][0:LAST, 4 * c + 2, :]
                        end = nc.scalar.activation(v[:, D1:2 * D1], src[0:LAST, w:w + D1], ACT.Copy, scale=1.0 / SW)
                else:
                    q = slice(first * 512, first * 512 + 512)
                    end = nc.scalar.activation(q1_hi[:, 0, q], src, ACT.Copy, scale=1.0 / SW)
                end.then_inc(proj_hi, 1)

            for c in range(2):
                for u in range(4):
                    early1(c, u, c)
            with act.Fori(2, KC - 1) as c:
                for u in range(3):
                    early1(c, u)
            for u in range(3):
                early1(KC - 1, u, last=True)
            for u in range(AHEAD):
                exp1(u, u)
            head1(0, 0)
            head1(1, 1)
            with act.Fori(1, H // 2 - 1) as pair:
                for a in range(2):
                    head1(2 * pair + a, a)
            head1(H - 2, 0)
            head1(H - 1, 1, last_head=True)
            for c in range(8):
                act.wait_ge(oT_ready, c + 1)
                nc.scalar.copy(oT[:, c, :], S[:, c % 2, :]).then_inc(oT_copied, 1)
            act_sqrt(act, 7, xstd, xvar)
            act.wait_ge(hatT_ready, 4)
            nc.scalar.copy(xT1, S[:, 0, :]).then_inc(hatT_copied, 1)
            act.wait_ge(gmax_done, 2)
            nc.scalar.activation(gate1[:, :, :], lg1[:, :, :], ACT.Exp).then_inc(gexp_done, 1)

        @block.tensor
        def _(pe):
            def transposes(n, src, dst):
                pe.wait_ge(hat_ready, n)
                for t in range(QT):
                    last = nc.tensor.transpose(dst[:, t * P:(t + 1) * P], src[:, t, :], ident)
                last.then_inc(hatT_ready, 1)

            def split_product(o, l_hi, l_lo, r_hi, r_lo, **kw):
                nc.tensor.matmul(o, l_hi, r_hi, start=True, stop=False, **kw)
                nc.tensor.matmul(o, l_lo, r_hi, start=False, stop=False, **kw)
                return nc.tensor.matmul(o, l_hi, r_lo, start=False, stop=True, **kw)

            pe.wait_ge(ld_cst, 16)
            transposes(1, xhat, S[:, 0, :])
            pe.wait_ge(hatT_copied, 2)
            pe.sem_inc(tr_done, 2)

            def ctx_transposes(c, b):
                pe.wait_ge(xb_ready, c + 1)
                pe.wait_ge(yf_ready, c + 1)
                for u in range(4):
                    last = nc.tensor.transpose(S4[:, b, u * P:(u + 1) * P], xb[:, b, u * P:(u + 1) * P], ident)
                last.then_inc(tr_done, 1)

            with pe.Fori(0, KC // 2) as i:
                for b in range(2):
                    ctx_transposes(2 * i + b, b)
            ctx_transposes(KC - 1, 0)

            pe.wait_ge(w0_split, 2)
            pe.wait_ge(yf_ready, KC + 2)
            for g in range(QUADS):
                if g >= 2:
                    pe.wait_ge(q0_f, g - 1)
                w = slice(g * P, (g + 1) * P)
                for half in range(2):
                    n = slice(half * 512, half * 512 + 512)
                    last = split_product(S[:, g % 2, n], w0_hi[:, w], w0_lo[:, w], xT_hi[:, n], xT_lo[:, n])
                last.then_inc(q0_psum, 1)
            pe.wait_ge(q0_f, QUADS)
            pe.wait_ge(q0_done, QUADS)
            def hi(p, q):
                return p[:, q * P:(q + 1) * P].bitcast(BF16)[:, 1::2]

            pe.wait_ge(bounds_ready, 1)
            for j in range(4):
                last = nc.tensor.transpose(S4[0:1, 0, j * P:(j + 1) * P], bounds[:, j:j + 1], ident)
            last.then_inc(boundsT_ready, 1)

            def attention0(C0, NC):
                pe.wait_ge(cT_hi_ready, 5)
                with pe.Fori(0, NC) as c:
                    for g in range(QUADS):
                        pe.wait_ge(k0_f, 4 * c + g + 1)
                        chunk = bass.ds(512 * (C0 + c), 512)
                        w = slice(512 + g * P, 512 + (g + 1) * P)
                        nc.tensor.matmul(S4[:, g, :], w0_hi[:, w], cT_hi[:, chunk], start=True, stop=False)
                        nc.tensor.matmul(S4[:, g, :], w0_lo[:, w], cT_hi[:, chunk], start=False, stop=False)
                        nc.tensor.matmul(S4[:, g, :], w0_hi[:, w], cT_lo[:, chunk], start=False, stop=False)
                        nc.tensor.matmul(S4[:, g, :], msel[:, bass.ds(P * (C0 + c), P)], mask_rows, start=False,
                                         stop=True).then_inc(k0_psum, 1)
                    for u in range(4):
                        pe.wait_ge(v0_done, 4 * c + u + 1)
                        tile = bass.ds(512 * (C0 + c) + u * P, P)
                        nc.tensor.matmul(T4[:, u, 0:D], cT_hi[:, tile], w0_hi[:, 1024:1024 + D], start=True, stop=False)
                        nc.tensor.matmul(T4[:, u, 0:D], cT_hi[:, tile], w0_lo[:, 1024:1024 + D], start=False, stop=False)
                        nc.tensor.matmul(T4[:, u, 0:D], cT_lo[:, tile], w0_hi[:, 1024:1024 + D], start=False,
                                         stop=True).then_inc(v0_psum, 1)
                pe.wait_ge(k0_done, 4 * NC + 4)
                pe.wait_ge(v0_done, 4 * NC + 4)
                with pe.Fori(0, H) as h:
                    with pe.Fori(0, NC) as c:
                        for k in range(4):
                            if k < COPIED:
                                pe.wait_ge(mx_copied, (h * NC + c) * COPIED + k + 1)
                            else:
                                pe.wait_ge(mx_read, h * NC + c + 1)
                            for m in range(2):
                                last = nc.tensor.matmul(M4[k][:, m, :], qz[:, h, (2 * k + m) * P:(2 * k + m + 1) * P],
                                                        ks[:, h // 4, bass.ds(512 * (C0 + c), 512)], start=True, stop=True)
                            last.then_inc(mx_psum, 1)
                for n in range(8):
                    pe.wait_ge(maxsel_ready, n + 1)
                    if n >= 4:
                        pe.wait_ge(maxT_read, n - 3)
                    for u in range(4):
                        last = nc.tensor.transpose(S4[:, n % 4, u * P:(u + 1) * P], maxsel[:, n % 2, u, :], ident)
                    last.then_inc(maxT_ready, 1)

                def scores0(g, u, quad, h, t):
                    pe.wait_ge(exp_done[0], g + 1)
                    for half in range(2):
                        last = nc.tensor.matmul(S[:, u % 2, half * 512:half * 512 + 512], ks[:, quad, bass.ds(P * t, P)],
                                                qz[:, h, half * 512:half * 512 + 512], start=True, stop=True)
                    last.then_inc(scores_ready[0], 1)

                def pv0(g, u, h, t, a, last_chunk):
                    pe.wait_ge(low_ready[0], g + 1)
                    for q in range(QT):
                        o = T4[:, a, q * VW0:(q + 1) * VW0]
                        first = nc.tensor.matmul(o, hi(probs0[u], q), v0[:, t, h, 0:VW0], start=False, stop=False,
                                                 skip_group_check=True)
                        if last_chunk and u == 0 and q == 0:
                            first.then_inc(scores_ready[0], 1)
                        last = nc.tensor.matmul(o[:, W0:VW0], plow0[u % 2][:, q * P:(q + 1) * P], v0[:, t, h, W0:VW0],
                                                start=False, stop=False, skip_group_check=True)
                    last.then_inc(pv_done[0], 2 if last_chunk and u == 2 else 1)

                pe.sem_inc(pv_done[0], 4)
                pe.wait_ge(maxT_read, 8)
                pe.wait_ge(v0_ones, 1)
                for u in range(AHEAD):
                    scores0(u, u, 0, 0, 4 * C0 + u)

                def quad0(quad, last_quad):
                    for j in range(4):
                        h = quad * 4 + j

                        def chunk(c, last):
                            for u in range(4):
                                g = 4 * (h * NC + c) + u
                                t = 4 * (C0 + c) + u
                                if not last:
                                    scores0(g + AHEAD, u + AHEAD, quad, h, t + AHEAD)
                                elif u >= 4 - AHEAD and (j < 3 or not last_quad):
                                    scores0(g + AHEAD, u + AHEAD, quad + (j == 3), h + 1, 4 * C0 + u + AHEAD - 4)
                                if not last and u == 0:
                                    pe.wait_ge(acc_zero, h + 1)
                                if not last or u < 3:
                                    pv0(g, u, h, t, j % 2, last)

                        with pe.Fori(0, NC - 1) as c:
                            chunk(c, False)
                        chunk(NC - 1, True)

                with pe.Fori(0, QUADS - 1) as quad:
                    quad0(quad, False)
                quad0(QUADS - 1, True)

            pe.wait_ge(window_ready, 1)
            with pe.If(pe.value_load(window[0:1, :], min_val=0, max_val=1) > 0):
                attention0(KC - WINDOW, WINDOW)
            with pe.Else():
                attention0(0, KC)
            transposes(2, xn, S[:, 0, :])
            pe.wait_ge(ld_ffn0, 64)
            pe.wait_ge(hatT_copied, 3)
            for t in range(QT):
                last = nc.tensor.matmul(T4[:, 2, t * E0:(t + 1) * E0], fT[:, t * P:(t + 1) * P], wg0s,
                                        start=True, stop=True)
            last.then_inc(logits_ready, 1)

            def expert_h(e, b, i):
                pe.wait_ge(ld_ew[b], 16 * i + 16)
                pe.wait_ge(h_read, e + 1)
                for ab in range(2):
                    for half in range(2):
                        n = slice(half * 512, half * 512 + 512)
                        last = nc.tensor.matmul(S[:, ab, n], ewb[:, b, ab * P:(ab + 1) * P], fT[:, n],
                                                start=True, stop=True)
                last.then_inc(h_ready, 1)

            def expert_y(e, b):
                pe.wait_ge(s_ready, e + 3)
                pe.wait_ge(y_added, e + 1)
                for t in range(QT):
                    last = nc.tensor.matmul(T4[:, t // 4, (t % 4) * P:(t % 4 + 1) * P], fs[:, t * P:(t + 1) * P],
                                            ewb[:, b, 2 * P:3 * P], start=True, stop=True)
                last.then_inc(y_ready, 1)

            expert_h(0, 0, 0)
            pe.wait_ge(gates_ready, 1)
            for t in range(QT):
                last = nc.tensor.transpose(T4[0:E0, 2 + t // 4, (t % 4) * P:(t % 4 + 1) * P], gate[:, t, :], ident)
            last.then_inc(gateT_ready, 1)
            pe.wait_ge(gateT_copied, 1)
            for t in range(QT):
                last = nc.tensor.matmul(T4[:, t // 4, (t % 4) * P:(t % 4 + 1) * P], gT[:, t * P:(t + 1) * P], b2s,
                                        start=True, stop=True)
            last.then_inc(b2_ready, 1)
            with pe.Fori(0, E0 // EWBUF - 1) as i:
                for b in range(EWBUF):
                    e = EWBUF * i + b
                    expert_h(e + 1, (b + 1) % EWBUF, i + (b + 1) // EWBUF)
                    expert_y(e, b)
            for b in range(EWBUF):
                e = E0 - EWBUF + b
                if b < EWBUF - 1:
                    expert_h(e + 1, b + 1, E0 // EWBUF - 1)
                expert_y(e, b)
            transposes(3, xn, S[:, 0, :])
            pe.wait_ge(w1_split, 1)
            pe.wait_ge(hatT_copied, 5)
            pe.wait_ge(v1_const, 1)

            def free_bank(n, u, early):
                if not early:
                    pe.wait_ge(proj_read, n + 1)
                elif isinstance(n, int) and n < 3:
                    pe.wait_ge(proj_read, 1)
                else:
                    pe.wait_ge(proj_done, n + 1)
                return T4[:, 3 - u if early else 3, :]

            def k1_slot(h, n, c, half, early):
                bank = free_bank(n, half, early)
                k = bass.ds(512 * c + 256 * half, 256)
                split_product(bank[:, 0:256], wk1_hi[:, h, :], wk1_lo[:, h, :], cn_hi[:, k], cn_lo[:, k])\
                    .then_inc(proj_psum, 1)

            def v1_slot(h, n, c, last, early):
                bank = free_bank(n, 2, early)
                for u in range(3 if last else 4):
                    t = bass.ds(512 * c + P * u, P)
                    o = bank[:, u * D1:(u + 1) * D1]
                    nc.tensor.matmul(o, cn_hi[:, t], wv1_hi[:, h, :], start=(u == 0), stop=False, skip_group_check=True)
                    nc.tensor.matmul(o, cn_hi[:, t], wv1_lo[:, h, :], start=False, stop=False, skip_group_check=True)
                    end = nc.tensor.matmul(o, cn_lo[:, t], wv1_hi[:, h, :], start=False, stop=True,
                                           skip_group_check=True)
                end.then_inc(proj_psum, 1)

            def q1_slot(h, n, half, early):
                bank = free_bank(n, 3, early)
                k = slice(half * 512, half * 512 + 512)
                split_product(bank, wq1_hi[:, h, :], wq1_lo[:, h, :], lat_hi[:, k], lat_lo[:, k])\
                    .then_inc(proj_psum, 1)

            def slots1(h, c, u, first=None, last=False, early=False):
                n = h * PROJ + 3 * c + (2 if first is None else first)
                if u < 2:
                    k1_slot(h, n + u, c, u, early)
                elif u == 2:
                    v1_slot(h, n + 2, c, last, early)
                elif first is not None:
                    q1_slot(h, n + 3, first, early)

            def scores1(g, u, hb, t):
                pe.wait_ge(exp_done[1], g + 1)
                for half in range(2):
                    n = slice(half * 512, half * 512 + 512)
                    k = k1[:, hb, bass.ds(P * t, P)]
                    nc.tensor.matmul(S[:, u % 2, n], k, q1_hi[:, hb, n], start=True, stop=False)
                    last = nc.tensor.matmul(S[:, u % 2, n], k, q1_lo[:, hb, n], start=False, stop=True)
                last.then_inc(scores_ready[1], 1)

            def pv1(g, u, hb, t, first, last_chunk):
                pe.wait_ge(low_ready[1], g + 1)
                for q in range(QT):
                    at = (q % 3) * VW
                    o = T4[:, q // 3, at:at + VW]
                    high = nc.tensor.matmul(o, hi(probs1[u], q), v1[hb][:, t, 0:VW], start=(first and q % 3 == 0),
                                            stop=False, skip_group_check=True)
                    if last_chunk and u == 0 and q == 0:
                        high.then_inc(scores_ready[1], 1)
                    last = nc.tensor.matmul(o[:, D1:VW], plow1[u % 2][:, q * P:(q + 1) * P], v1[hb][:, t, D1:VW],
                                            start=False, stop=False, skip_group_check=True)
                last.then_inc(pv_done[1], 2 if last_chunk and u == 2 else 1)

            def head1(h, hb, first_head=False, last_head=False):
                def chunk(c, first=None, last=False):
                    for u in range(4):
                        t = 4 * c + u
                        if not last_head:
                            slots1(h + 1, c, u, first, last)
                        if not last:
                            scores1(h * KT4 + t + AHEAD, u + AHEAD, hb, t + AHEAD)
                        elif not last_head and u >= 4 - AHEAD:
                            pe.wait_ge(proj_done, (h + 1) * PROJ + 8 + 3)
                            scores1(h * KT4 + t + AHEAD, u + AHEAD, 1 - hb, u + AHEAD - 4)
                        if first == 0 and u == 0:
                            pe.wait_ge(proj_done, (h + 1) * PROJ + 3)
                            if not first_head:
                                pe.wait_ge(acc_copied, h)
                        if not last or u < 3:
                            pv1(h * KT4 + t, u, hb, t, first == 0 and u == 0, last)

                chunk(0, 0)
                chunk(1, 1)
                with pe.Fori(2, KC - 1) as c:
                    chunk(c)
                chunk(KC - 1, last=True)

            pe.sem_inc(pv_done[1], 4)
            for c in range(2):
                for u in range(4):
                    slots1(0, c, u, c, early=True)
            with pe.Fori(2, KC - 1) as c:
                for u in range(3):
                    slots1(0, c, u, early=True)
            for u in range(3):
                slots1(0, KC - 1, u, last=True, early=True)
            pe.wait_ge(proj_done, 8 + 3)
            for u in range(AHEAD):
                scores1(u, u, 0, u)
            head1(0, 0, first_head=True)
            head1(1, 1)
            with pe.Fori(1, H // 2 - 1) as pair:
                for a in range(2):
                    head1(2 * pair + a, a)
            head1(H - 2, 0)
            head1(H - 1, 1, last_head=True)
            pe.wait_ge(head_done, H + 1)
            for c in range(8):
                if c >= 2:
                    pe.wait_ge(oT_copied, c - 1)
                for t in range(QT):
                    last = nc.tensor.transpose(S[:, c % 2, t * P:(t + 1) * P], o1[:, t, c * P:(c + 1) * P], ident)
                last.then_inc(oT_ready, 1)
            pe.wait_ge(ld_end, 64)
            pe.wait_ge(oT_copied, 8)
            for t in range(QT):
                for c in range(8):
                    last = nc.tensor.matmul(T4[:, t // 4, (t % 4) * P:(t % 4 + 1) * P], oT[:, c, t * P:(t + 1) * P],
                                            wos[:, c, :], start=(c == 0), stop=(c == 7))
            last.then_inc(proj_ready, 1)
            transposes(4, xhat, S[:, 0, :])
            pe.wait_ge(hatT_copied, 6)
            for t in range(QT):
                last = nc.tensor.matmul(T4[:, 2, t * E1:(t + 1) * E1], xT1[:, t * P:(t + 1) * P], wg1s,
                                        start=True, stop=True)
            last.then_inc(logits_ready, 1)
            for t in range(QT):
                if t >= 4:
                    pe.wait_ge(ex1_added, t - 3)
                elif t == 3:
                    pe.wait_ge(gmax_done, 2)
                for half in range(2):
                    last = nc.tensor.matmul(M4[t % 4][:, half, :], xT1[:, t * P:(t + 1) * P],
                                            we1s[:, half * 512:half * 512 + 512], start=True, stop=True)
                last.then_inc(ex1_ready, 1)

        @block.vector
        def _(dve):
            steps = [0]
            norms = [0]

            def step(ins):
                steps[0] += 1
                ins.then_inc(dve_step, 1)
                dve.wait_ge(dve_step, steps[0])

            def finish_stats(st, tmp, mean, var):
                step(nc.vector.tensor_tensor(mean, st[:, :, 1], st[:, :, 4], ALU.add))
                step(nc.vector.tensor_tensor(tmp, st[:, :, 1], st[:, :, 4], ALU.subtract))
                step(nc.vector.tensor_scalar(mean, mean, 0.5, None, ALU.mult))
                step(nc.vector.tensor_scalar(tmp, tmp, 0.5, None, ALU.mult))
                step(nc.vector.tensor_tensor(tmp, tmp, tmp, ALU.mult))
                step(nc.vector.tensor_tensor(var, st[:, :, 2], st[:, :, 5], ALU.add))
                step(nc.vector.tensor_scalar(var, var, 1.0 / D, EPS, ALU.mult, ALU.add))
                return nc.vector.tensor_tensor(var, var, tmp, ALU.add)

            def row_stats(src):
                for t in range(QT):
                    last = nc.vector.bn_stats(bst[:, t, :], src[:, t, :])
                step(last)

            def rsqrt_var(ins, std, out_rstd):
                norms[0] += 1
                ins.then_inc(var_ready, 1)
                dve.wait_ge(std_ready, norms[0])
                step(nc.vector.reciprocal(out_rstd, std))

            def layer_norm(src, dst, ready=None):
                row_stats(src)
                rsqrt_var(finish_stats(bst, stat[:, 0:QT], xmean, xvar), xstd, xrstd)
                for t in range(QT):
                    last = nc.vector.tensor_scalar(dst[:, t, :], src[:, t, :], xmean[:, t:t + 1], xrstd[:, t:t + 1],
                                                   ALU.subtract, ALU.mult)
                if ready:
                    last.then_inc(ready, 1)
                else:
                    step(last)

            dve.wait_ge(ld_x, 16)
            layer_norm(xres, xhat, hat_ready)
            dve.wait_ge(ld_w0, 16)
            step(nc.vector.tensor_reduce(wmax, w0f[:, 512:1024], AX.X, ALU.max, apply_absolute_value=True))
            step(nc.vector.tensor_scalar(w0f, w0f, SW, None, ALU.mult))
            step(nc.vector.tensor_copy(w0_hi, w0f))
            nc.vector.tensor_tensor(w0_lo, w0f, w0_hi, ALU.subtract).then_inc(w0_split, 1)
            dve.wait_ge(ld_mask, 32)
            nc.vector.tensor_scalar(mask_rows, mask_i, -MASKED, MASKED, ALU.mult, ALU.add)
            nc.vector.tensor_copy(msel, msel_f).then_inc(w0_split, 1)
            step(nc.vector.memset(bounds, -3.0e38))
            step(nc.vector.tensor_reduce(bounds[0:KC, 0:1], mask_rows, AX.X, ALU.max))
            dve.wait_ge(ld_b0, 32)
            dve.wait_ge(ld_cst, 16)
            nc.vector.tensor_reduce(bounds[:, 2:3], b0s[:, QUADS:2 * QUADS], AX.X, ALU.max, apply_absolute_value=True)
            for i, scale in ((0, SA / math.sqrt(W0)), (1, SA)):
                c = slice(i * QUADS, (i + 1) * QUADS)
                add = cst[:, C_ADD_Q if i == 0 else C_ADD_K:][:, 0:1]
                last = nc.vector.tensor_scalar(qkcol[:, c], b0s[:, c], scale, add, ALU.mult, ALU.add)
            step(nc.vector.tensor_scalar(ln1c, cst[:, C_LN:C_LN + 4], SA, None, ALU.mult))
            dve.wait_ge(hatT_copied, 1)
            nc.vector.scalar_tensor_tensor(out=xT_lo, in0=S[:, 0, :], scalar=SA, in1=xT_hi, op0=ALU.mult,
                                           op1=ALU.subtract).then_inc(hatT_copied, 1)
            dve.wait_ge(ld_ctx, 32)
            with dve.Fori(0, KC) as c:
                for u in range(4):
                    last = nc.vector.bn_stats(cbn[:, 4 * c + u, :], c_raw[:, 4 * c + u, :])
            step(nc.vector.memset(rec, 0.0))
            rsqrt_var(finish_stats(cbn, stat, cmean, cvar), cstd, crstd)

            def normalized(c, b):
                dve.wait_ge(tr_done, c + 1)
                for u in range(4):
                    t = 4 * c + u
                    last = nc.vector.tensor_scalar(xb[:, b, u * P:(u + 1) * P], c_raw[:, t, :], cmean[:, bass.ds(t, 1)],
                                                   crstd[:, bass.ds(t, 1)], ALU.subtract, ALU.mult)
                last.then_inc(xb_ready, 1)

            normalized(0, 0)
            with dve.Fori(0, KC // 2) as i:
                normalized(2 * i + 1, 1)
                normalized(2 * i + 2, 0)
            dve.wait_ge(ld_ctx_t, 16)
            step(nc.vector.tensor_reduce(cmax, cT, AX.X, ALU.max, apply_absolute_value=True))
            step(nc.vector.tensor_tensor(bounds[:, 1:2], wmax, cmax, ALU.mult))
            dve.sem_inc(k0_done, 4)
            dve.sem_inc(v0_done, 4)
            dve.wait_ge(cn_done, KC + 2)
            for g in range(QUADS):
                dve.wait_ge(q0_f, g + 1)
                if g:
                    dve.wait_ge(q0_done, g)
                step(nc.vector.tensor_copy(qtmp, probs[:, g % 2, :]))
                step(nc.vector.scalar_tensor_tensor(out=qtmp, in0=qtmp, scalar=cst[:, C_NLOW_Q:C_NLOW_Q + 1],
                                                    in1=probs[:, g % 2, :], op0=ALU.mult, op1=ALU.add))
                nc.vector.tensor_reduce(qbound[:, g:g + 1], qtmp, AX.X, ALU.max, apply_absolute_value=True)
                for j in range(4):
                    last = nc.vector.tensor_scalar(qz[:, 4 * g + j, :], qtmp, rowsel(j), None, ALU.mult)
                last.then_inc(q0_done, 1)
            dve.wait_ge(q0_done, QUADS)
            step(nc.vector.tensor_reduce(decide[:, 0:1], qbound, AX.X, ALU.max))
            nc.vector.tensor_scalar(bounds[:, 3:4], decide[:, 0:1], cst[:, C_VROW:C_VROW + 1], None, ALU.mult)\
                .then_inc(bounds_ready, 1)
            dve.wait_ge(boundsT_ready, 1)
            for j, (start, end, op) in enumerate(((0, KC - WINDOW, ALU.max), (KC - WINDOW, KC, ALU.max),
                                                  (P, 2 * P, ALU.add), (2 * P, 3 * P, ALU.max),
                                                  (3 * P, 4 * P, ALU.max))):
                last = nc.vector.tensor_reduce(decide[0:1, j:j + 1], S4[0:1, 0, start:end], AX.X, op)
            step(last)
            before, inside, weighted, bias, query, key, x_ok, y_ok = (decide[0:1, j:j + 1] for j in range(8))
            step(nc.vector.tensor_tensor(key, weighted, bias, ALU.add))
            step(nc.vector.tensor_tensor(key, key, query, ALU.mult))
            step(nc.vector.tensor_scalar(key, key, ENTRY_SPREAD / SA, None, ALU.is_lt))
            step(nc.vector.tensor_scalar(x_ok, before, MASKED / 2, None, ALU.is_lt))
            step(nc.vector.tensor_scalar(y_ok, inside, MASKED / 2, None, ALU.is_gt))
            step(nc.vector.tensor_tensor(x_ok, x_ok, y_ok, ALU.mult))
            nc.vector.tensor_tensor(window[0:1, :], key, x_ok, ALU.mult).then_inc(window_ready, 1)

            def attention0(C0, NC):
                dve.wait_ge(cT_hi_ready, 4)
                n = slice(512 * C0, 512 * (C0 + NC))
                nc.vector.scalar_tensor_tensor(out=cT_lo[:, n], in0=cT[:, n], scalar=SA, in1=cT_hi[:, n],
                                               op0=ALU.mult, op1=ALU.subtract).then_inc(cT_hi_ready, 1)
                dve.wait_ge(cT_hi_ready, 5)
                with dve.Fori(0, NC) as c:
                    n = bass.ds(512 * (C0 + c), 512)
                    for g in range(QUADS):
                        dve.wait_ge(k0_f, 4 * c + g + 5)
                        nc.vector.tensor_copy(ks[:, g, n], kf[:, g, :]).then_inc(k0_hi, 1)
                    for g in range(QUADS):
                        dve.wait_ge(k0_hi, 4 * c + g + 1)
                        nc.vector.scalar_tensor_tensor(out=ks[:, g, n], in0=ks[:, g, n], scalar=cst[:, C_NLOW_K:C_NLOW_K + 1],
                                                       in1=kf[:, g, :], op0=ALU.mult, op1=ALU.add).then_inc(k0_done, 1)
                    for u in range(4):
                        v = v0[:, 4 * (C0 + c) + u, :, :]
                        dve.wait_ge(v0_hi, 4 * c + u + 1)
                        nc.vector.scalar_tensor_tensor(out=v[:, :, 0:W0], in0=T4[:, u, 0:D].rearrange("p (h w) -> p h w", w=W0),
                                                       scalar=1.0 / SW, in1=v[:, :, W0:2 * W0], op0=ALU.mult,
                                                       op1=ALU.subtract).then_inc(v0_done, 1)
                dve.wait_ge(k0_done, 4 * NC + 4)
                step(nc.vector.memset(probs[:, :, :], -3.0e38))
                dve.sem_inc(mx_read, 1)
                dve.sem_inc(mx_folded, COPIED)
                dve.sem_inc(mx_top, 4)
                mxh = mx.rearrange("p (h q) -> p h q", q=QT)

                def direct(h, c):
                    dve.wait_ge(mx_psum, (h * NC + c) * 4 + COPIED + 1)
                    nc.vector.tensor_reduce(mp[:, c, h, :], M4[COPIED], AX.X, ALU.max).then_inc(mx_read, 1)

                with dve.Fori(0, H // 2) as pair:
                    for a in range(2):
                        h = 2 * pair + a
                        direct(h, 0)
                        with dve.Fori(1, NC) as c:
                            for k in range(COPIED):
                                n = (h * (NC - 1) + c - 1) * COPIED + k
                                dve.wait_ge(mx_copied, (h * NC + c) * COPIED + k + COPIED + 1)
                                dve.wait_ge(mx_folded, n + 1)
                                nc.vector.tensor_tensor(mtop[a][:, k, :], mtop[a][:, k, :], mstage[:, k, :], ALU.max)\
                                    .then_inc(mx_folded, 1)
                            direct(h, c)
                        dve.wait_ge(mx_folded, (h + 1) * (NC - 1) * COPIED + COPIED)
                        top = mtop[a].rearrange("p k (m n) -> p (k m) n", n=512)
                        nc.vector.tensor_tensor(top[:, :, 0:256], top[:, :, 0:256], top[:, :, 256:512], ALU.max)\
                            .then_inc(mx_top, 1)
                        dve.wait_ge(mx_top, 2 * h + 5)
                        nc.vector.tensor_reduce(mxh[:, h, 0:2 * COPIED], top[:, :, 0:256], AX.X, ALU.max)\
                            .then_inc(mx_top, 1)
                dve.wait_ge(mx_read, NC * H + 1)
                dve.wait_ge(mx_top, 2 * H + 4)
                nc.vector.tensor_scalar(mxh[:, :, 0:2 * COPIED], mxh[:, :, 0:2 * COPIED], SCORE, None, ALU.mult)
                step(nc.vector.tensor_reduce(mxh[:, :, 2 * COPIED:], mp.rearrange("p c h q -> p h q c"), AX.X, ALU.max))
                step(nc.vector.memset(maxsel, 0.0))

                def make_maxsel(n):
                    if n >= 2:
                        dve.wait_ge(maxT_ready, n - 1)
                    g, half = n // 2, n % 2
                    m = mx[:, 4 * g * QT:4 * (g + 1) * QT].rearrange("p (j q) -> p q j", j=4)
                    nc.vector.tensor_scalar(maxsel[:, n % 2, :, MAX_ROW::32], m[:, 4 * half:4 * half + 4, :],
                                            -1.0 / SCORE, SHIFT0, ALU.mult, ALU.add).then_inc(maxsel_ready, 1)

                make_maxsel(0)
                for n in range(8):
                    if n < 7:
                        make_maxsel(n + 1)
                    g, half = n // 2, n % 2
                    dve.wait_ge(maxT_ready, n + 1)
                    for j in range(4):
                        o = qz[:, 4 * g + j, half * 512:half * 512 + 512]
                        last = nc.vector.scalar_tensor_tensor(out=o, in0=S4[:, n % 4, :], scalar=rowsel(j), in1=o,
                                                              op0=ALU.mult, op1=ALU.add)
                    last.then_inc(maxT_read, 1)
                for a in range(2):
                    nc.vector.memset(T4[:, a, 0:QT * VW0], 0.0).then_inc(acc_zero, 1)

                def low0(g, u, count):
                    dve.wait_ge(exp_done[0], g + 3)
                    dve.wait_ge(pv_done[0], g + 3)
                    nc.vector.tensor_tensor(plow0[u % 2], probs0[u], probs0[u].bitcast(BF16)[:, 1::2], ALU.subtract)\
                        .then_inc(low_ready[0], count)

                def lows0(h, c, last_chunk=False):
                    for u in range(3 if last_chunk else 4):
                        low0(4 * (h * NC + c) + u, u, 2 if last_chunk and u == 2 else 1)

                def head0(h, a, first_head=False, last_head=False):
                    lows0(h, 1)
                    if not first_head:
                        dve.wait_ge(sums0_copied, h)
                        nc.vector.memset(T4[:, 1 - a, 0:QT * VW0], 0.0).then_inc(acc_zero, 1)
                    with dve.Fori(2, NC - 1) as c:
                        lows0(h, c)
                    lows0(h, NC - 1, last_chunk=True)
                    if not last_head:
                        lows0(h + 1, 0)

                lows0(0, 0)
                head0(0, 0, first_head=True)
                head0(1, 1)
                with dve.Fori(1, H // 2 - 1) as pair:
                    for a in range(2):
                        head0(2 * pair + a, a)
                head0(H - 2, 0)
                head0(H - 1, 1, last_head=True)

            dve.wait_ge(window_ready, 1)
            counted = steps[0]
            with dve.If(dve.value_load(window[0:1, :], min_val=0, max_val=1) > 0):
                attention0(KC - WINDOW, WINDOW)
            steps[0] = counted
            with dve.Else():
                attention0(0, KC)
            dve.wait_ge(sums0_copied, H)
            sums = sums0.rearrange("p (h q w) -> p h q w", q=QT, w=VW0)
            rec0 = mx.rearrange("p (h q) -> p h q", q=QT)
            o0 = h0.rearrange("p q (h w) -> p h q w", w=W0)
            nc.vector.tensor_tensor(o0, sums[:, :, :, 0:W0], sums[:, :, :, W0:2 * W0], ALU.add)
            step(nc.vector.tensor_scalar(rec0, sums[:, :, :, 2 * W0], SA, None, ALU.mult))
            step(nc.vector.reciprocal(mx, mx))
            step(nc.vector.tensor_tensor(o0, o0, rec0.unsqueeze(3).to_broadcast([P, H, QT, W0]), ALU.mult))
            step(nc.vector.tensor_tensor(xres[:, :, :], xres[:, :, :], h0[:, :, :], ALU.add))
            nc.vector.tensor_tensor(xres[:, :, :], xres[:, :, :], bvs.unsqueeze(1).to_broadcast([P, QT, D]), ALU.add)\
                .then_inc(attn0_done, 1)
            dve.wait_ge(attn0_done, 1)
            layer_norm(xres, xhat)
            row_stats(xhat)
            step(finish_stats(bst, stat[:, 0:QT], xmean, xvar))
            step(nc.vector.tensor_tensor(xmean, xmean, xmean, ALU.mult))
            rsqrt_var(nc.vector.tensor_tensor(xvar, xvar, xmean, ALU.add), xstd, xrstd)
            dve.wait_ge(ld_ffn0, 64)
            for t in range(QT):
                last = nc.vector.scalar_tensor_tensor(out=xn[:, t, :], in0=xhat[:, t, :], scalar=xrstd[:, t:t + 1],
                                                      in1=nscale, op0=ALU.mult, op1=ALU.mult)
            last.then_inc(hat_ready, 1)
            step(nc.vector.tensor_tensor(xres[:, :, :], xres[:, :, :], xhat[:, :, :], ALU.add))

            def ranks(src, n, rk, buf, k):
                gt = buf[:, 0:QT * n * n].rearrange("p (t e f) -> p t e f", e=n, f=n)
                eq = buf[:, QT * n * n:2 * QT * n * n].rearrange("p (t e f) -> p t e f", e=n, f=n)
                tri = cst[:, C_TRI:C_TRI + E0 * E0].rearrange("p (e f) -> p e f", e=E0)[:, 0:n, 0:n]
                for t in range(QT):
                    of = src[:, t, :].unsqueeze(1).to_broadcast([P, n, n])
                    to = src[:, t, :].unsqueeze(2).to_broadcast([P, n, n])
                    nc.vector.tensor_tensor(gt[:, t, :, :], of, to, ALU.is_gt)
                    last = nc.vector.tensor_tensor(eq[:, t, :, :], of, to, ALU.is_equal)
                step(last)
                for t in range(QT):
                    last = nc.vector.tensor_tensor(eq[:, t, :, :], eq[:, t, :, :], tri, ALU.mult)
                step(last)
                step(nc.vector.tensor_tensor(gt, gt, eq, ALU.add))
                step(nc.vector.tensor_reduce(rk, gt, AX.X, ALU.add))
                step(nc.vector.tensor_scalar(rk, rk, k - 0.5, None, ALU.is_lt))

            dve.sem_inc(h_read, 1)
            dve.sem_inc(s_ready, 2)
            dve.sem_inc(glu_done, 2)
            dve.wait_ge(logits_ready, 1)
            step(nc.vector.tensor_tensor(lg[:, :, :], T4[:, 2, 0:QT * E0].rearrange("p (t e) -> p t e", e=E0),
                                         bg0s.unsqueeze(1).to_broadcast([P, QT, E0]), ALU.add))
            ranks(lg, E0, rank, fab[:, 3 * SQ:7 * SQ], TOP0)
            step(nc.vector.tensor_reduce(gmax, lg[:, :, :], AX.X, ALU.max))
            nc.vector.tensor_tensor(lg[:, :, :], lg[:, :, :], gmax.unsqueeze(2).to_broadcast([P, QT, E0]),
                                    ALU.subtract).then_inc(gmax_done, 1)
            dve.wait_ge(gexp_done, 1)
            step(nc.vector.tensor_tensor(gate[:, :, :], gate[:, :, :], rank[:, :, :], ALU.mult))
            step(nc.vector.tensor_reduce(gsum, gate[:, :, :], AX.X, ALU.add))
            step(nc.vector.reciprocal(grec, gsum))
            nc.vector.tensor_tensor(gate[:, :, :], gate[:, :, :], grec.unsqueeze(2).to_broadcast([P, QT, E0]),
                                    ALU.mult).then_inc(gates_ready, 1)
            y8 = T4[:, 0:2, :].rearrange("p b (t d) -> p (b t) d", d=D)

            def expert_clips(e, b):
                dve.wait_ge(a_raw, e + 1)
                nc.vector.tensor_scalar(fa[b], fa[b], LIMIT, None, ALU.min).then_inc(a_ready, 1)
                dve.wait_ge(h_read, e + 2)
                nc.vector.tensor_scalar(fb[b], fb[b], LIMIT, -LIMIT, ALU.min, ALU.max).then_inc(b_ready, 1)

            def expert_s(e, b):
                dve.wait_ge(sig_ready, e + 1)
                nc.vector.tensor_tensor(fsig[b], fsig[b], fa[b], ALU.mult).then_inc(glu_done, 1)
                dve.wait_ge(glu_done, e + 3)
                dve.wait_ge(b_ready, e + 1)
                nc.vector.scalar_tensor_tensor(out=fs, in0=fb[b], scalar=1.0, in1=fsig[b], op0=ALU.add, op1=ALU.mult)\
                    .then_inc(s_ready, 1)

            def expert_add(e):
                dve.wait_ge(y_ready, e + 1)
                for t in range(QT):
                    last = nc.vector.scalar_tensor_tensor(out=xres[:, t, :], in0=y8[:, t, :],
                                                          scalar=gate[:, t, bass.ds(e, 1)], in1=xres[:, t, :],
                                                          op0=ALU.mult, op1=ALU.add)
                last.then_inc(y_added, 1)

            expert_clips(0, 0)
            dve.wait_ge(b2_ready, 1)
            step(nc.vector.tensor_tensor(xres[:, :, :], xres[:, :, :], y8, ALU.add))
            dve.sem_inc(y_added, 1)
            expert_s(0, 0)
            expert_clips(1, 1)
            expert_add(0)
            expert_s(1, 1)
            with dve.Fori(1, E0 // 2) as i:
                for b in range(2):
                    e = 2 * i + b
                    expert_clips(e, b)
                    expert_add(e - 1)
                    expert_s(e, b)
            expert_add(E0 - 1)
            dve.wait_ge(y_added, E0 + 1)
            layer_norm(xres, xhat)
            layer_norm(xhat, xn, hat_ready)
            dve.wait_ge(hat_ready, 3)
            dve.wait_ge(hatT_ready, 3)
            nc.vector.memset(v1[0][:, KT - 1:KT4, :], 0.0)
            step(nc.vector.memset(v1[1][:, KT - 1:KT4, :], 0.0))
            nc.vector.memset(shift1, SHIFT1)
            for b in range(2):
                nc.vector.memset(v1[b][:, 0:KT - 1, 2 * D1:VW], 1.0)
                last = nc.vector.memset(v1[b][0:LAST, KT - 1, 2 * D1:VW], 1.0)
            last.then_inc(v1_const, 1)
            dve.wait_ge(latf_ready, 1)
            step(nc.vector.tensor_copy(lat_hi, probs[:, 0, :]))
            nc.vector.tensor_tensor(lat_lo, probs[:, 0, :], lat_hi, ALU.subtract).then_inc(hatT_copied, 2)
            dve.sem_inc(proj_read, 1)
            dve.sem_inc(proj_done, 3)
            dve.sem_inc(head_done, 1)

            def clip(g, u, count=1):
                dve.wait_ge(exp_done[1], g + 3)
                nc.vector.tensor_scalar(probs1[u % 4], probs1[u % 4], EXP_HI, EXP_LO, ALU.min, ALU.max)\
                    .then_inc(clipped, count)

            def low1(g, u, count=1):
                dve.wait_ge(clipped, g + 1)
                dve.wait_ge(pv_done[1], g + 3)
                nc.vector.tensor_tensor(plow1[u % 2], probs1[u], probs1[u].bitcast(BF16)[:, 1::2], ALU.subtract)\
                    .then_inc(low_ready[1], count)

            def head1(h, first_head=False, last_head=False):
                def chunk(c, last=False):
                    for u in range(4):
                        g = h * KT4 + 4 * c + u
                        if not last or u < 2:
                            clip(g + 1, u + 1, 2 if last and u == 1 else 1)
                        elif u == 3 and not last_head:
                            clip(g + 1, u + 1)
                        if not last or u < 3:
                            low1(g, u, 2 if last and u == 2 else 1)

                chunk(0)
                if not first_head:
                    reciprocals(h - 1)
                with dve.Fori(1, KC - 1) as c:
                    chunk(c)
                chunk(KC - 1, True)

            def reciprocals(h):
                dve.wait_ge(acc_copied, h + 1)
                nc.vector.tensor_scalar(rec, acc_f[:, :, 2 * D1], SA, None, ALU.mult).then_inc(acc_rec, 1)
                dve.wait_ge(acc_rec, 2 * h + 1)
                nc.vector.reciprocal(rec, rec).then_inc(acc_rec, 1)

            def early1(c, u, first=None, last=False):
                n = 3 * c + (2 if first is None else first) + u
                src = T4[:, 3 - u, :]
                k = k1[D1:P, 0, bass.ds(512 * c + 256 * (u % 2), 256)]
                tiles = slice(4 * c, 4 * c + 2) if last else bass.ds(4 * c, 4)
                v = v1[0][:, tiles, :]
                dve.wait_ge(proj_hi, n + 1)
                if u < 2:
                    end = nc.vector.scalar_tensor_tensor(out=k, in0=src[D1:P, 0:256], scalar=1.0 / SW, in1=k,
                                                         op0=ALU.mult, op1=ALU.subtract)
                elif u == 2:
                    w = (2 if last else 4) * D1
                    end = nc.vector.scalar_tensor_tensor(out=v[:, :, 0:D1], in0=src[:, 0:w].rearrange("p (t w) -> p t w", w=D1), scalar=1.0 / SW, in1=v[:, :, D1:2 * D1],
                                                         op0=ALU.mult, op1=ALU.subtract)
                    if last:
                        v = v1[0][0:LAST, 4 * c + 2, :]
                        end = nc.vector.scalar_tensor_tensor(out=v[:, 0:D1], in0=src[0:LAST, w:w + D1], scalar=1.0 / SW, in1=v[:, D1:2 * D1],
                                                         op0=ALU.mult, op1=ALU.subtract)
                else:
                    q = slice(first * 512, first * 512 + 512)
                    end = nc.vector.scalar_tensor_tensor(out=q1_lo[:, 0, q], in0=src, scalar=1.0 / SW, in1=q1_hi[:, 0, q],
                                                         op0=ALU.mult, op1=ALU.subtract)
                end.then_inc(proj_done, 1)

            for c in range(2):
                for u in range(4):
                    early1(c, u, c)
            with dve.Fori(2, KC - 1) as c:
                for u in range(3):
                    early1(c, u)
            for u in range(3):
                early1(KC - 1, u, last=True)
            dve.wait_ge(proj_done, PROJ + 3)
            dve.sem_inc(proj_read, PROJ)

            clip(0, 0)
            head1(0, first_head=True)
            with dve.Fori(1, H - 1) as h:
                head1(h)
            head1(H - 1, last_head=True)
            reciprocals(H - 1)
            dve.wait_ge(proj_ready, 1)
            dve.wait_ge(ld_end, 64)
            step(nc.vector.tensor_tensor(xres[:, :, :], xres[:, :, :], y8, ALU.add))
            step(nc.vector.tensor_tensor(xres[:, :, :], xres[:, :, :], bo1.unsqueeze(1).to_broadcast([P, QT, D]),
                                         ALU.add))
            layer_norm(xres, xhat, hat_ready)
            dve.wait_ge(logits_ready, 2)
            step(nc.vector.tensor_copy(lg1[:, :, :], T4[:, 2, 0:QT * E1].rearrange("p (t e) -> p t e", e=E1)))
            step(nc.vector.tensor_reduce(gmax, lg1[:, :, :], AX.X, ALU.max))
            nc.vector.tensor_tensor(lg1[:, :, :], lg1[:, :, :], gmax.unsqueeze(2).to_broadcast([P, QT, E1]),
                                    ALU.subtract).then_inc(gmax_done, 1)
            dve.wait_ge(gexp_done, 2)
            for passes in range(2):
                step(nc.vector.tensor_reduce(gsum, gate1[:, :, :], AX.X, ALU.add))
                if passes == 1:
                    step(nc.vector.tensor_scalar(gsum, gsum, 1e-9, None, ALU.add))
                step(nc.vector.reciprocal(grec, gsum))
                step(nc.vector.tensor_tensor(gate1[:, :, :], gate1[:, :, :],
                                             grec.unsqueeze(2).to_broadcast([P, QT, E1]), ALU.mult))
                if passes == 0:
                    ranks(gate1, E1, rank1, probs[:, 0, :], TOP1)
                    step(nc.vector.tensor_tensor(gate1[:, :, :], gate1[:, :, :], rank1[:, :, :], ALU.mult))
            for t2 in range(0, QT, 2):
                dve.wait_ge(ex1_ready, t2 + 2)
                added = {}
                for e in range(E1):
                    for t in (t2, t2 + 1):
                        if e:
                            dve.wait_ge(dve_step, added[t])
                        last = nc.vector.scalar_tensor_tensor(
                            out=xres[:, t, :], in0=M4[t % 4][:, e // 4, (e % 4) * P:(e % 4 + 1) * P],
                            scalar=gate1[:, t, e:e + 1], in1=xres[:, t, :], op0=ALU.mult, op1=ALU.add)
                        if e < E1 - 1:
                            last.then_inc(dve_step, 1)
                            steps[0] += 1
                            added[t] = steps[0]
                        else:
                            last.then_inc(ex1_added, 1)
            dve.wait_ge(ex1_added, QT)
            nc.vector.memset(rec, 0.0).then_inc(out_ready, 1)


def kernel(**inputs):
    import numpy as np
    import concourse.bacc as bacc
    from concourse.bass_utils import run_bass_kernel_spmd

    a = {k: np.asarray(v) for k, v in inputs.items()}
    f32 = np.float32

    def rows0(w):
        t = np.zeros((D, H, 4, W0), f32)
        t[:, :, 0:3, :] = w.T.reshape(D, H, 1, W0)
        return t.reshape(D, H * 32)

    def col0(b):
        t = np.zeros((H, 4, W0), f32)
        t[:, 0:3, :] = b.reshape(H, 1, W0)
        return t.reshape(QUADS, P).T

    def twice(w):
        t = np.zeros((D, H, 2, D1), f32)
        t[...] = w.reshape(D, H, 1, D1)
        return t.reshape(D, H * 2 * D1)

    def bcast(v):
        return np.broadcast_to(v, (P, v.shape[-1]))

    row = np.arange(P) % 32
    cst = np.zeros((P, C_N), f32)
    cst[:, C_ID:C_ID + P] = np.eye(P)
    for j in range(4):
        cst[32 * j:32 * j + 32, C_ROWSEL + j] = 1.0
    cst[:, C_NLOW_K] = np.where((row >= 16) & (row < 24), -1.0, 0.0)
    cst[:, C_NLOW_Q] = np.where((row >= 8) & (row < 16), -1.0, 0.0)
    cst[:, C_ADD_K] = np.where(row == MAX_ROW, SCORE, 0.0)
    cst[:, C_ADD_Q] = np.where(row == MASK_ROW, SCORE, 0.0)
    cst[:, C_TRI:C_TRI + E0 * E0] = np.tril(np.ones((E0, E0)), -1).reshape(1, -1)
    for n, name in enumerate(("L1_xattn_ln_l_w", "L1_xattn_ln_l_b", "L1_xattn_ln_c_w", "L1_xattn_ln_c_b")):
        cst[:, C_LN + n] = a[name]
    cst[:, C_VROW] = row < MASK_ROW
    sel = np.zeros((KC, KC, P), f32)
    for c in range(KC):
        sel[c, c, MASK_ROW::32] = SW
    mask = np.full((KC * 512,), 1 + int(NO_KEY - 0) // 10000, np.int32)
    mask[0:SK] = a["mask_BxS2_ik0"].reshape(-1)
    ctx = a["ctx_1024"].reshape(SK, D)
    ctx_t = np.zeros((D, KPAD), f32)
    ctx_t[:, 0:SK] = ctx.T
    w1 = a["L0_ffn_w1"]
    b1 = a["L0_ffn_b1"]
    ew = np.concatenate([w1[:, :, 0::2], w1[:, :, 1::2], a["L0_ffn_w2"], b1[:, 0::2, None], b1[:, 1::2, None]], axis=2)
    arrays = {
        "x": a["x"].reshape(SQ, D),
        "ctx": ctx,
        "ctx_t": ctx_t,
        "mask": mask.reshape(KC, 512),
        "consts": cst,
        "mask_sel": sel.reshape(KC, KC * P),
        "w0": np.concatenate([rows0(a["L0_xattn_Wq"]), rows0(a["L0_xattn_Wk"]), a["L0_xattn_Wv"].T], axis=1),
        "b0": np.concatenate([col0(a["L0_xattn_bq"]), col0(a["L0_xattn_bk"])], axis=1),
        "bv0": bcast(a["L0_xattn_bv"]),
        "norm_scale": bcast(a["L0_ffn_norm_scale"]),
        "wg0": a["L0_ffn_wg"],
        "bg0": bcast(a["L0_ffn_bg"]),
        "ew0": ew,
        "b2": a["L0_ffn_b2"],
        "ln1": cst[:, C_LN:C_LN + 4],
        "w1": np.concatenate([twice(a["L1_xattn_Wkv"][:, 0:H * D1]), twice(a["L1_xattn_Wq"]),
                              a["L1_xattn_Wkv"][:, H * D1:]], axis=1),
        "wo": a["L1_xattn_Wo"].reshape(8, P, D).transpose(1, 0, 2),
        "bo": bcast(a["L1_xattn_bo"]),
        "wg1": a["L1_ffn_Wg"],
        "we1": a["L1_ffn_We"].transpose(1, 0, 2).reshape(D, E1 * D),
    }
    arrays = {k: np.ascontiguousarray(v) for k, v in arrays.items()}
    nc = bacc.Bacc("TRN2", target_bir_lowering=False, num_devices=1)
    args = {k: nc.dram_tensor(f"in_{k}", v.shape, mybir.dt.from_np(v.dtype), kind="ExternalInput").ap()
            for k, v in arrays.items()}
    out = nc.dram_tensor("out_x", (SQ, D), F32, kind="ExternalOutput").ap()
    build(nc, out=out, **args)
    r = run_bass_kernel_spmd(nc, [{f"in_{k}": v for k, v in arrays.items()}], core_ids=[0])
    return r.results[0]["out_x"].reshape(1, SQ, D)
```
